# Optimizing a Trainium2 kernel written in Bass

```python
import numpy as np
import jax
import jax.numpy as jnp

def _softmax(x, axis=-1):
    return jax.nn.softmax(x, axis=axis)

def _gelu(x):
    return jax.nn.gelu(x, approximate=True)

def _silu(x):
    return jax.nn.silu(x)

def _sigmoid(x):
    return jax.nn.sigmoid(x)

def _layernorm(x, axis=-1, eps=1e-05):
    m = jnp.mean(x, axis=axis, keepdims=True)
    v = jnp.var(x, axis=axis, keepdims=True)
    return (x - m) / jnp.sqrt(v + eps)

def _scatter_add(tgt, idx, src, axis=0):
    return tgt.at[idx].add(src)

def _segment_sum(src, seg, n):
    return jax.ops.segment_sum(src, seg, n)
kernel_name = 'mk_adj_preln_d4_adj_r2_13f805'

def setup_inputs(seed: int=0):
    np.random.seed(seed)
    _w = jnp.asarray

    def _rec_inputs():
        import jax
        import jax.numpy as jnp
        _gk = jax.random.key(seed)
        x = -0.000125 + 0.9999 * jax.random.normal(jax.random.fold_in(_gk, 1), (64, 128, 256), jnp.float32)
        _a = jax.random.bernoulli(jax.random.fold_in(_gk, 2), 0.125, (128, 128))
        _af = _a.astype(jnp.float32)
        adj = _af
        return (x, adj)
    x, adj = _rec_inputs()

    def _L0_gnn_setup():
        import jax, jax.numpy as jnp
        import numpy as np
        ALPHA = 0.2
        key = jax.random.key(seed)
        k0, k1, k2, k3 = jax.random.split(key, 4)
        B, N, C, F = (64, 512, 256, 256)
        x = jax.random.normal(k0, (B, N, C), dtype=jnp.float32)
        W = jax.random.normal(k1, (C, F), dtype=jnp.float32) * (1.414 / np.sqrt(C + F))
        a = jax.random.normal(k2, (2 * F, 1), dtype=jnp.float32) * (1.414 / np.sqrt(2 * F + 1))
        beta = jnp.ones((1,), dtype=jnp.float32)
        mask = (jax.random.uniform(k3, (N, N)) < 0.3).astype(jnp.float32)
        return {'x': x, 'W': W, 'a': a, 'beta': beta, 'mask': mask}
    _L0_gnn_all = _L0_gnn_setup()
    _L0_gnn_in = {k: v for k, v in _L0_gnn_all.items() if k in ('W', 'a', 'beta')}
    del _L0_gnn_all

    def _L1_gnn_setup():
        import jax, jax.numpy as jnp
        import numpy as np
        B, N, D, H = (4, 1024, 256, 8)
        HD = D // H
        key = jax.random.key(seed)
        ks = jax.random.split(key, 10)
        x = jax.random.normal(ks[0], (B, N, D), dtype=jnp.float32)
        adj = (jax.random.uniform(ks[1], (N, N)) < 0.1).astype(jnp.float32)
        s = 1.0 / np.sqrt(D)
        Wq = jax.random.normal(ks[2], (D, D), dtype=jnp.float32) * s
        Wk = jax.random.normal(ks[3], (D, D), dtype=jnp.float32) * s
        Wv = jax.random.normal(ks[4], (D, D), dtype=jnp.float32) * s
        Wo = jax.random.normal(ks[5], (D, D), dtype=jnp.float32) * s
        bq = jnp.zeros((D,), jnp.float32)
        bk = jnp.zeros((D,), jnp.float32)
        bv = jnp.zeros((D,), jnp.float32)
        bo = jnp.zeros((D,), jnp.float32)
        return {'x': x, 'adj': adj, 'Wq': Wq, 'bq': bq, 'Wk': Wk, 'bk': bk, 'Wv': Wv, 'bv': bv, 'Wo': Wo, 'bo': bo}
    _L1_gnn_all = _L1_gnn_setup()
    _L1_gnn_in = {k: v for k, v in _L1_gnn_all.items() if k in ('Wq', 'bq', 'Wk', 'bk', 'Wv', 'bv', 'Wo', 'bo')}
    del _L1_gnn_all

    def _L2_gnn_setup():
        import jax, jax.numpy as jnp
        import numpy as np
        B, N, D, T = (64, 128, 256, 3)

        def _lin(v, W, b):
            return jnp.einsum('...i,oi->...o', v, W) + b
        key = jax.random.key(seed)
        ks = jax.random.split(key, 12)
        s2 = 1.0 / np.sqrt(2 * D)
        s1 = 1.0 / np.sqrt(D)
        return {'x': jax.random.normal(ks[0], (B, N, D), jnp.float32), 'in_mat': jax.random.uniform(ks[1], (N, N), jnp.float32) / N, 'out_mat': jax.random.uniform(ks[2], (N, N), jnp.float32) / N, 'w3_w': jax.random.normal(ks[3], (D, 2 * D), jnp.float32) * s2, 'w3_b': jnp.zeros((D,), jnp.float32), 'u3_w': jax.random.normal(ks[4], (D, D), jnp.float32) * s1, 'u3_b': jnp.zeros((D,), jnp.float32), 'w4_w': jax.random.normal(ks[5], (D, 2 * D), jnp.float32) * s2, 'w4_b': jnp.zeros((D,), jnp.float32), 'w5_w': jax.random.normal(ks[6], (D, 2 * D), jnp.float32) * s2, 'w5_b': jnp.zeros((D,), jnp.float32), 'u5_w': jax.random.normal(ks[7], (D, D), jnp.float32) * s1, 'u5_b': jnp.zeros((D,), jnp.float32)}
    _L2_gnn_all = _L2_gnn_setup()
    _L2_gnn_in = {k: v for k, v in _L2_gnn_all.items() if k in ('w3_w', 'w3_b', 'u3_w', 'u3_b', 'w4_w', 'w4_b', 'w5_w', 'w5_b', 'u5_w', 'u5_b')}
    del _L2_gnn_all

    def _L3_gnn_setup():
        import jax, jax.numpy as jnp
        import numpy as np
        B, N, D, O = (8, 2048, 256, 256)
        key = jax.random.key(seed)
        k1, k2, k3, k4 = jax.random.split(key, 4)
        x = jax.random.normal(k1, (B, N, D), dtype=jnp.float32)
        adj = jax.random.uniform(k2, (N, N), dtype=jnp.float32)
        weight = jax.random.normal(k3, (D, O), dtype=jnp.float32) * 0.02
        bias = jax.random.normal(k4, (O,), dtype=jnp.float32) * 0.02
        return {'x': x, 'adj': adj, 'weight': weight, 'bias': bias}
    _L3_gnn_all = _L3_gnn_setup()
    _L3_gnn_in = {k: v for k, v in _L3_gnn_all.items() if k in ('weight', 'bias')}
    del _L3_gnn_all
    return {'x': x, 'adj': adj, 'L0_gnn_W': _L0_gnn_in['W'], 'L0_gnn_a': _L0_gnn_in['a'], 'L0_gnn_beta': _L0_gnn_in['beta'], 'L1_gnn_Wq': _L1_gnn_in['Wq'], 'L1_gnn_bq': _L1_gnn_in['bq'], 'L1_gnn_Wk': _L1_gnn_in['Wk'], 'L1_gnn_bk': _L1_gnn_in['bk'], 'L1_gnn_Wv': _L1_gnn_in['Wv'], 'L1_gnn_bv': _L1_gnn_in['bv'], 'L1_gnn_Wo': _L1_gnn_in['Wo'], 'L1_gnn_bo': _L1_gnn_in['bo'], 'L2_gnn_w3_w': _L2_gnn_in['w3_w'], 'L2_gnn_w3_b': _L2_gnn_in['w3_b'], 'L2_gnn_u3_w': _L2_gnn_in['u3_w'], 'L2_gnn_u3_b': _L2_gnn_in['u3_b'], 'L2_gnn_w4_w': _L2_gnn_in['w4_w'], 'L2_gnn_w4_b': _L2_gnn_in['w4_b'], 'L2_gnn_w5_w': _L2_gnn_in['w5_w'], 'L2_gnn_w5_b': _L2_gnn_in['w5_b'], 'L2_gnn_u5_w': _L2_gnn_in['u5_w'], 'L2_gnn_u5_b': _L2_gnn_in['u5_b'], 'L3_gnn_weight': _L3_gnn_in['weight'], 'L3_gnn_bias': _L3_gnn_in['bias']}

def reference(x, adj, L0_gnn_W, L0_gnn_a, L0_gnn_beta, L1_gnn_Wq, L1_gnn_bq, L1_gnn_Wk, L1_gnn_bk, L1_gnn_Wv, L1_gnn_bv, L1_gnn_Wo, L1_gnn_bo, L2_gnn_w3_w, L2_gnn_w3_b, L2_gnn_u3_w, L2_gnn_u3_b, L2_gnn_w4_w, L2_gnn_w4_b, L2_gnn_w5_w, L2_gnn_w5_b, L2_gnn_u5_w, L2_gnn_u5_b, L3_gnn_weight, L3_gnn_bias):
    import jax
    import jax.numpy as jnp

    def _L0_gnn_ref(x, W, a, beta, mask):
        import jax, jax.numpy as jnp
        import numpy as np
        ALPHA = 0.2
        F_ = W.shape[1]
        h = jnp.einsum('bnc,cf->bnf', x, W)
        a1, a2 = (a[:F_, 0], a[F_:, 0])
        s1 = jnp.einsum('bnf,f->bn', h, a1)
        s2 = jnp.einsum('bnf,f->bn', h, a2)
        e = jax.nn.leaky_relu(s1[:, :, None] + s2[:, None, :], negative_slope=ALPHA)
        e = e * mask[None, :, :]
        att = jax.nn.softmax(e, axis=2)
        h_prime = jnp.einsum('bij,bjf->bif', att, h)
        return jax.nn.elu(h_prime + beta * h)

    def _L1_gnn_ref(x, adj, Wq, bq, Wk, bk, Wv, bv, Wo, bo):
        import jax, jax.numpy as jnp
        import numpy as np
        B, N, D, H = (4, 1024, 256, 8)
        HD = D // H
        b, n, d = x.shape
        q = (x @ Wq + bq).reshape(b, n, H, HD)
        k = (x @ Wk + bk).reshape(b, n, H, HD)
        v = (x @ Wv + bv).reshape(b, n, H, HD)
        scores = jnp.einsum('bqhd,bkhd->bhqk', q, k) / jnp.sqrt(jnp.float32(HD))
        scores = scores + (1.0 - adj)[None, None, :, :] * -1000000000.0
        attn = jax.nn.softmax(scores, axis=-1)
        out = jnp.einsum('bhqk,bkhd->bqhd', attn, v).reshape(b, n, d)
        return out @ Wo + bo

    def _L2_gnn_ref(x, in_mat, out_mat, w3_w, w3_b, u3_w, u3_b, w4_w, w4_b, w5_w, w5_b, u5_w, u5_b):
        import jax, jax.numpy as jnp
        import numpy as np
        B, N, D, T = (64, 128, 256, 3)

        def _lin(v, W, b):
            return jnp.einsum('...i,oi->...o', v, W) + b
        h = x
        for _ in range(T):
            a_in = jnp.einsum('nm,bmd->bnd', in_mat, h)
            a_out = jnp.einsum('nm,bmd->bnd', out_mat, h)
            av = jnp.concatenate([a_in, a_out], axis=-1)
            z = jax.nn.sigmoid(_lin(av, w3_w, w3_b) + _lin(h, u3_w, u3_b))
            r = jax.nn.sigmoid(_lin(av, w4_w, w4_b) + _lin(h, u3_w, u3_b))
            hv = jnp.tanh(_lin(av, w5_w, w5_b) + _lin(r * h, u5_w, u5_b))
            h = (1.0 - z) * h + z * hv
        return h

    def _L3_gnn_ref(x, adj, weight, bias):
        import jax, jax.numpy as jnp
        import numpy as np
        B, N, D, O = (8, 2048, 256, 256)
        y = jnp.einsum('nm,bmd->bnd', adj, x)
        out = jnp.einsum('bnd,do->bno', y, weight) + bias
        return out
    h = jnp.maximum(_layernorm(x, axis=-1), 0.0)
    x = x + _L0_gnn_ref(h, L0_gnn_W, L0_gnn_a, L0_gnn_beta, adj)
    h = jnp.maximum(_layernorm(x, axis=-1), 0.0)
    x = x + _L1_gnn_ref(h, adj, L1_gnn_Wq, L1_gnn_bq, L1_gnn_Wk, L1_gnn_bk, L1_gnn_Wv, L1_gnn_bv, L1_gnn_Wo, L1_gnn_bo)
    h = jnp.maximum(_layernorm(x, axis=-1), 0.0)
    x = x + _L2_gnn_ref(h, adj, adj, L2_gnn_w3_w, L2_gnn_w3_b, L2_gnn_u3_w, L2_gnn_u3_b, L2_gnn_w4_w, L2_gnn_w4_b, L2_gnn_w5_w, L2_gnn_w5_b, L2_gnn_u5_w, L2_gnn_u5_b)
    h = jnp.maximum(_layernorm(x, axis=-1), 0.0)
    x = x + _L3_gnn_ref(h, adj, L3_gnn_weight, L3_gnn_bias)
    return x

_drawn_inputs = setup_inputs


def setup_inputs(seed=0):
    import zlib

    import numpy as np

    out = dict(_drawn_inputs(seed))
    spreads = {'L1_gnn_bq': (0.0, 0.8),
     'L1_gnn_bk': (0.0, 0.8),
     'L1_gnn_bv': (0.0, 0.1),
     'L1_gnn_bo': (0.0, 0.1),
     'L2_gnn_w3_b': (0.0, 0.373),
     'L2_gnn_u3_b': (0.0, 0.349),
     'L2_gnn_w4_b': (0.0, 0.8),
     'L2_gnn_w5_b': (0.0, 0.423),
     'L2_gnn_u5_b': (0.0, 0.268)}
    factors = {'L3_gnn_bias': 8.0}
    for name, (base, spread) in spreads.items():
        noise = np.random.default_rng([zlib.crc32(name.encode()), seed]).standard_normal(out[name].shape)
        drawn = base * np.exp(spread * noise) if base else spread * noise
        out[name] = jnp.asarray(drawn.astype(out[name].dtype))
    for name, factor in factors.items():
        out[name] = (out[name] * factor).astype(out[name].dtype)
    return out
```

```python
from contextlib import ExitStack

import concourse.bass as bass
from concourse import mybir

F32 = mybir.dt.float32
F16 = mybir.dt.float16
ALU = mybir.AluOpType
ACT = mybir.ActivationFunctionType
AX = mybir.AxisListType.X

GRAPHS, NODES, FEATURES = 64, 128, 256
P = 128
CHUNKS = FEATURES // P
GROUP = 4
GROUPS = GRAPHS // GROUP
TOKENS = GROUP * NODES
HEADS = 8
HEAD = FEATURES // HEADS
LN_EPS = 1e-5
MASKED = -1e9
LEAK = 0.2
STEPS = 3

RAW = {"gat": 0, "q": 2, "k": 4, "v": 6, "o": 8, "w3": 10, "w4": 14, "w5": 18, "u3": 22, "u5": 24, "conv": 26}
RAW_SLOTS = 28
SPLIT = {"gat": 0, "q": 2, "k": 4, "v": 6, "o": 8, "conv": 10, "u3": 12, "u5": 14, "w4": 16, "w5": 18, "w3": 20}
SPLIT_SLOTS = 22
COLS = {"a1": 0, "a2": 2, "bq": 4, "bk": 6, "bv": 8, "w3b": 10, "u3b": 12, "w4b": 14, "w5b": 16, "u5b": 18}
COL_SLOTS = 20
ROWS = {"a1": 0, "a2": 1, "bo": 2, "conv_bias": 3}

HI, LO = 0, 1
PARTS = ((HI, HI), (HI, LO), (LO, HI))


def product(pe, out, stationary, moving, chunks=CHUNKS, start=True, stop=True, loose=False):
    last = None
    for c in range(chunks):
        for n, (a, b) in enumerate(PARTS):
            last = pe.matmul(out, stationary(a, c), moving(b, c),
                             start=start and c == 0 and n == 0,
                             stop=stop and c == chunks - 1 and n == len(PARTS) - 1,
                             skip_group_check=loose)
    return last


def graph(g, b):
    return bass.ds(g * GROUP + b, 1)


def group(g):
    return bass.ds(g * GROUP, GROUP)


def load_constants(nc, sem, dram, k):
    with ExitStack() as ctx:
        def sb(name, shape, dt=F32):
            return ctx.enter_context(nc.sbuf_tensor(name, shape, dt))

        raw = sb("raw_weights", [P, RAW_SLOTS, FEATURES])
        cols = sb("cols", [P, COL_SLOTS])
        rows = sb("rows", [P, 4, FEATURES])
        adj = sb("adj_raw", [P, 2, NODES])
        summed = sb("summed", [P, 3, CHUNKS, FEATURES])
        attn_vec = sb("attn_vec", [P, 2, CHUNKS])
        scratch = sb("scratch", [P, 2, CHUNKS, FEATURES])
        spread = sb("spread", [P, 3, CHUNKS, P])
        bv_split = sb("bv_split", [P, 2, CHUNKS, P], F16)
        crow = ctx.enter_context(nc.psum_tensor("crow", [P, FEATURES], F32))

        small_in = sem("small_in")
        gat_in = sem("gat_in")
        weights_in = sem("weights_in")
        done = sem("setup_done")
        split = sem("bv_split_ready")
        crow_ready = sem("crow_ready")
        block = ctx.enter_context(nc.Block())

        @block.sync
        def _(sp):
            view = dram["weights"].rearrange("(k p) f -> p k f", p=P)
            sp.dma_start(raw[:, 0:2, :], view[:, 0:2, :]).then_inc(gat_in, 16)
            sp.dma_start(cols[:], dram["cols"]).then_inc(small_in, 16)
            sp.dma_start(rows[:], dram["rows"]).then_inc(small_in, 16)
            sp.dma_start(adj[:], dram["adj"]).then_inc(small_in, 16)
            sp.dma_start(k.identity[:], dram["identity"]).then_inc(small_in, 16)
            sp.dma_start(k.beta[:], dram["beta"]).then_inc(small_in, 16)
            sp.dma_start(raw[:, 2:RAW_SLOTS, :], view[:, 2:RAW_SLOTS, :]).then_inc(weights_in, 16)

        @block.vector
        def _(dve):
            n = [0]

            def step(ins):
                n[0] += 1
                ins.then_inc(done, 1)
                dve.wait_ge(done, n[0])

            def split_of(hi, lo, full):
                step(dve.tensor_copy(hi, full))
                step(dve.tensor_tensor(lo, full, hi, ALU.subtract))

            step(dve.memset(k.eps[:], LN_EPS))
            step(dve.memset(k.minus_half[:], -0.5))
            dve.wait_ge(small_in, 16 * 5)
            step(dve.tensor_copy(k.identity16[:], k.identity[:]))
            step(dve.tensor_copy(k.mask[:, 0, :], adj[:, 0, :]))
            split_of(k.adjT[:, HI, :], k.adjT[:, LO, :], adj[:, 1, :])
            step(dve.tensor_scalar(k.mask_bias[:, 0, :], adj[:, 0, :], -1.0, 1.0, ALU.mult, ALU.add))
            step(dve.tensor_scalar(k.mask_bias[:, 0, :], k.mask_bias[:, 0, :], MASKED, None, ALU.mult))
            dve.wait_ge(gat_in, 16)
            for v in range(2):
                for c in range(CHUNKS):
                    step(dve.tensor_tensor(scratch[:, v, c, :], raw[:, c, :], rows[:, ROWS["a1"] + v, :], ALU.mult))
                    step(dve.reduce_sum(attn_vec[:, v, c:c + 1], scratch[:, v, c, :], AX))
                    step(dve.tensor_copy(spread[:, v, c, :], attn_vec[:, v, c:c + 1].broadcast_to([P, P])))
                    split_of(k.attn_vecs[:, HI, v, c, :], k.attn_vecs[:, LO, v, c, :], spread[:, v, c, :])
            split_of(k.w[:, HI, 0:2, :], k.w[:, LO, 0:2, :], raw[:, 0:2, :])
            dve.wait_ge(weights_in, 16)
            for name in ("q", "k", "v", "o", "u3", "u5", "conv"):
                a, b = RAW[name], SPLIT[name]
                split_of(k.w[:, HI, b:b + 2, :], k.w[:, LO, b:b + 2, :], raw[:, a:a + 2, :])
            for c in range(CHUNKS):
                step(dve.tensor_copy(spread[:, 2, c, :], cols[:, COLS["bv"] + c:COLS["bv"] + c + 1].broadcast_to([P, P])))
            step(dve.tensor_copy(bv_split[:, HI], spread[:, 2]))
            step(dve.tensor_tensor(bv_split[:, LO], spread[:, 2], bv_split[:, HI], ALU.subtract))
            dve.engine_nop().then_inc(split, 1)
            for j, name in enumerate(("w3", "w4", "w5")):
                a = RAW[name]
                step(dve.tensor_tensor(summed[:, j], raw[:, a:a + 2, :], raw[:, a + 2:a + 4, :], ALU.add))
            step(dve.tensor_tensor(summed[:, 0], summed[:, 0], summed[:, 1], ALU.subtract))
            for j, name in enumerate(("w3", "w4", "w5")):
                b = SPLIT[name]
                split_of(k.w[:, HI, b:b + 2, :], k.w[:, LO, b:b + 2, :], summed[:, j])
            step(dve.tensor_copy(k.bias_q[:], cols[:, COLS["bq"]:COLS["bq"] + 2]))
            step(dve.tensor_copy(k.bias_k[:], cols[:, COLS["bk"]:COLS["bk"] + 2]))
            for out, first, second in ((k.bias_z, "w3b", "u3b"), (k.bias_r, "w4b", "u3b"), (k.bias_h, "w5b", "u5b")):
                step(dve.tensor_tensor(out[:], cols[:, COLS[first]:COLS[first] + 2],
                                       cols[:, COLS[second]:COLS[second] + 2], ALU.add))
            step(dve.tensor_copy(k.conv_bias[:, 0, :], rows[:, ROWS["conv_bias"], :]))
            dve.wait_ge(crow_ready, 1)
            step(dve.tensor_tensor(k.attn_bias[:, 0, :], crow[:], rows[:, ROWS["bo"], :], ALU.add))

        @block.tensor
        def _(pe):
            pe.wait_ge(split, 1)
            product(pe, crow[:], lambda a, c: bv_split[:, a, c, :],
                    lambda b, c: k.w[:, b, SPLIT["o"] + c, :]).then_inc(crow_ready, 1)


def settle(eng, s):
    eng.sem_inc(s.settled, 1)


def layer_norm_stats(dve, k, g, ready, s):
    for b in range(GROUP):
        dve.bn_stats(s.stats[:, b, :], k.x[:, graph(g, b), :].rearrange("p a f -> p (a f)")).then_inc(ready, 1)
    dve.wait_ge(ready, (g * 2 + 1) * GROUP)
    settle(dve, s)
    for b in range(GROUP):
        dve.bn_aggr(s.moments[:, b, :], s.stats[:, b, :]).then_inc(ready, 1)


def layer_norm_rstd(pool, k, g, moments_ready, pool_step, s):
    pool.wait_ge(moments_ready, (g + 1) * 2 * GROUP)
    pool.tensor_tensor(s.var_eps[:], s.moments[:, :, 1], k.eps[:], ALU.add).then_inc(pool_step, 1)
    pool.wait_ge(pool_step, g * 2 + 1)
    pool.tensor_tensor(s.rstd[:], s.var_eps[:], k.minus_half[:], ALU.pow).then_inc(pool_step, 1)


def gat_layer(nc, sem, dram, k):
    with ExitStack() as ctx:
        def sb(name, shape, dt=F32):
            return ctx.enter_context(nc.sbuf_tensor("gat_" + name, shape, dt))

        def ps(name, shape):
            return ctx.enter_context(nc.psum_tensor("gat_" + name, shape, F32))

        class s:
            settled = sem("gat_settled")
            stats = sb("stats", [P, GROUP, 6])
            moments = sb("moments", [P, GROUP, 2])
            var_eps = sb("var_eps", [P, GROUP])
            rstd = sb("rstd", [P, GROUP])
        normed = sb("normed", [P, GROUP, FEATURES])
        hT = sb("hT", [P, 2, CHUNKS, TOKENS], F16)
        wh = sb("wh", [P, 2, GROUP, FEATURES], F16)
        beta_wh = sb("beta_wh", [P, GROUP, FEATURES])
        e_raw = sb("e_raw", [P, GROUP, NODES])
        e_leaky = sb("e_leaky", [P, GROUP, NODES])
        row_max = sb("row_max", [P, GROUP, 1])
        prob = sb("prob", [P, GROUP, NODES])
        row_sum = sb("row_sum", [P, GROUP])
        inv_sum = sb("inv_sum", [P, GROUP])
        probT = sb("probT", [P, 2, GROUP, NODES], F16)
        y = sb("y", [P, GROUP, FEATURES])
        y_neg = sb("y_neg", [P, GROUP, FEATURES])
        y_exp = sb("y_exp", [P, GROUP, FEATURES])

        hT_ps = ps("hT_ps", [P, CHUNKS, TOKENS])
        e_ps = ps("e_ps", [P, GROUP, NODES])
        wh_ps = ps("wh_ps", [P, GROUP, FEATURES])
        probT_ps = ps("probT_ps", [P, GROUP, NODES])
        att_ps = ps("att_ps", [P, GROUP, FEATURES])

        x_in = sem("x_in")
        moments_ready = sem("gat_moments_ready")
        rstd_step = sem("gat_rstd_step")
        normed_ready = sem("gat_normed_ready")
        hT_turned = sem("gat_hT_turned")
        hT_hi = sem("gat_hT_hi")
        hT_lo = sem("gat_hT_lo")
        e_ready = sem("gat_e_ready")
        e_copied = sem("gat_e_copied")
        leaky_ready = sem("gat_leaky_ready")
        masked_ready = sem("gat_masked_ready")
        max_ready = sem("gat_max_ready")
        shifted_ready = sem("gat_shifted_ready")
        prob_ready = sem("gat_prob_ready")
        sum_step = sem("gat_sum_step")
        wh_ready = sem("gat_wh_ready")
        wh_hi = sem("gat_wh_hi")
        beta_wh_ready = sem("gat_beta_wh_ready")
        wh_lo = sem("gat_wh_lo")
        probT_turned = sem("gat_probT_turned")
        probT_hi = sem("gat_probT_hi")
        probT_lo = sem("gat_probT_lo")
        att_ready = sem("gat_att_ready")
        y_ready = sem("gat_y_ready")
        y_neg_ready = sem("gat_y_neg_ready")
        y_exp_ready = sem("gat_y_exp_ready")
        y_pos_ready = sem("gat_y_pos_ready")
        x_step = sem("gat_x_step")
        block = ctx.enter_context(nc.Block())

        def pipeline(eng, body):
            body(0, None, None)
            body(1, 0, None)
            body(2, 1, 0)
            with eng.Fori(3, GROUPS) as i:
                body(i, i - 1, i - 2)
            body(None, GROUPS - 1, GROUPS - 2)
            body(None, None, GROUPS - 1)

        @block.sync
        def _(sp):
            x_view = dram["x"].rearrange("b n d -> n b d")
            sp.dma_start(k.x[:, group(0), :], x_view[:, group(0), :]).then_inc(x_in, 16)
            with sp.Fori(1, GROUPS) as g:
                sp.wait_ge(x_in, g * 16)
                sp.dma_start(k.x[:, group(g), :], x_view[:, group(g), :]).then_inc(x_in, 16)
            sp.wait_ge(x_in, GROUPS * 16)

        @block.vector
        def _(dve):
            def body(front, mid, back):
                if back is not None:
                    dve.wait_ge(probT_hi, back + 1)
                    if not isinstance(back, int) or back > 0:
                        dve.wait_ge(att_ready, back * 2)
                    dve.tensor_tensor(probT[:, LO], probT_ps[:], probT[:, HI], ALU.subtract).then_inc(probT_lo, 1)
                if mid is not None:
                    dve.wait_ge(e_copied, mid + 1)
                    dve.wait_ge(shifted_ready, mid)
                    dve.wait_ge(prob_ready, mid)
                    dve.scalar_tensor_tensor(e_leaky[:], e_raw[:], LEAK, e_raw[:], ALU.mult,
                                             ALU.max).then_inc(leaky_ready, 1)
                if back is not None:
                    dve.wait_ge(y_exp_ready, back)
                    dve.wait_ge(y_pos_ready, back)
                    dve.wait_ge(x_step, back * 2)
                    dve.wait_ge(beta_wh_ready, (back + 1) * 2)
                    dve.wait_ge(sum_step, (back + 1) * 2)
                    for b in range(GROUP):
                        if b % 2 == 0:
                            dve.wait_ge(att_ready, back * 2 + b // 2 + 1)
                        dve.scalar_tensor_tensor(y[:, b, :], att_ps[:, b, :], inv_sum[:, b:b + 1], beta_wh[:, b, :],
                                                 ALU.mult, ALU.add).then_inc(y_ready, 1)
                if mid is not None:
                    for j in range(2):
                        dve.wait_ge(wh_hi, mid * 2 + j + 1)
                        h = slice(2 * j, 2 * j + 2)
                        dve.tensor_tensor(wh[:, LO, h, :], wh_ps[:, h, :], wh[:, HI, h, :],
                                          ALU.subtract).then_inc(wh_lo, 1)
                if front is not None:
                    dve.wait_ge(x_in, (front + 1) * 16)
                    dve.wait_ge(rstd_step, front * 2)
                    layer_norm_stats(dve, k, front, moments_ready, s)
                if mid is not None:
                    dve.wait_ge(masked_ready, mid + 1)
                    dve.reduce_max(row_max[:, :, 0], e_leaky[:], AX).then_inc(max_ready, 1)
                if back is not None:
                    dve.wait_ge(y_neg_ready, back + 1)
                    dve.tensor_scalar(y[:], y[:], 0.0, -1.0, ALU.max, ALU.add).then_inc(y_pos_ready, 1)
                if front is not None:
                    dve.wait_ge(rstd_step, (front + 1) * 2)
                    dve.wait_ge(hT_turned, front * CHUNKS)
                    for b in range(GROUP):
                        dve.tensor_scalar(normed[:, b, :], k.x[:, graph(front, b), :].rearrange("p a f -> p (a f)"),
                                          s.moments[:, b, 0:1], s.rstd[:, b:b + 1], ALU.subtract,
                                          ALU.mult).then_inc(normed_ready, 1)
                if mid is not None:
                    dve.wait_ge(prob_ready, mid + 1)
                    dve.reduce_sum(row_sum[:], prob[:], AX).then_inc(sum_step, 1)
                    dve.wait_ge(sum_step, mid * 2 + 1)
                    if back is not None:
                        dve.wait_ge(y_ready, (back + 1) * GROUP)
                    dve.reciprocal(inv_sum[:], row_sum[:]).then_inc(sum_step, 1)
                if front is not None:
                    for c in range(CHUNKS):
                        dve.wait_ge(hT_hi, front * CHUNKS + c + 1)
                        dve.scalar_tensor_tensor(hT[:, LO, c, :], hT_ps[:, c, :], 0.0, hT[:, HI, c, :], ALU.max,
                                                 ALU.subtract).then_inc(hT_lo, 1)

            pipeline(dve, body)

        @block.gpsimd
        def _(pool):
            def body(front, mid, back):
                if mid is not None:
                    pool.wait_ge(leaky_ready, mid + 1)
                    pool.tensor_tensor(e_leaky[:], e_leaky[:], k.mask[:].broadcast_to([P, GROUP, NODES]),
                                       ALU.mult).then_inc(masked_ready, 1)
                if front is not None:
                    layer_norm_rstd(pool, k, front, moments_ready, rstd_step, s)
                if mid is not None:
                    pool.wait_ge(max_ready, mid + 1)
                    pool.tensor_tensor(e_leaky[:], e_leaky[:], row_max[:].broadcast_to([P, GROUP, NODES]),
                                       ALU.subtract).then_inc(shifted_ready, 1)
                if back is not None:
                    pool.wait_ge(y_pos_ready, back + 1)
                    settle(pool, s)
                    pool.tensor_tensor(k.x[:, group(back), :], k.x[:, group(back), :], y[:], ALU.add).then_inc(x_step, 1)
                    pool.wait_ge(x_step, back * 2 + 1)
                    pool.wait_ge(y_exp_ready, back + 1)
                    settle(pool, s)
                    pool.tensor_tensor(k.x[:, group(back), :], k.x[:, group(back), :], y_exp[:],
                                       ALU.add).then_inc(x_step, 1)

            pipeline(pool, body)

        @block.scalar
        def _(act):
            def body(front, mid, back):
                if back is not None:
                    act.wait_ge(probT_turned, back + 1)
                    act.wait_ge(att_ready, back * 2)
                    act.copy(probT[:, HI], probT_ps[:]).then_inc(probT_hi, 1)
                if mid is not None:
                    act.wait_ge(e_ready, mid + 1)
                    act.wait_ge(leaky_ready, mid)
                    act.copy(e_raw[:], e_ps[:]).then_inc(e_copied, 1)
                    for j in range(2):
                        h = slice(2 * j, 2 * j + 2)
                        act.wait_ge(wh_ready, mid * 2 + j + 1)
                        if back is not None:
                            act.wait_ge(y_ready, (back + 1) * GROUP)
                            act.wait_ge(att_ready, (back + 1) * 2)
                        act.activation(beta_wh[:, h, :], wh_ps[:, h, :], ACT.Identity,
                                       scale=k.beta[:, 0:1]).then_inc(beta_wh_ready, 1)
                        act.copy(wh[:, HI, h, :], wh_ps[:, h, :]).then_inc(wh_hi, 1)
                if back is not None:
                    act.wait_ge(y_ready, (back + 1) * GROUP)
                    act.wait_ge(y_exp_ready, back)
                    act.activation(y_neg[:], y[:], ACT.Relu, scale=-1.0).then_inc(y_neg_ready, 1)
                    act.wait_ge(y_neg_ready, back + 1)
                    act.wait_ge(x_step, back * 2)
                    act.activation(y_exp[:], y_neg[:], ACT.Exp, scale=-1.0).then_inc(y_exp_ready, 1)
                if mid is not None:
                    act.wait_ge(shifted_ready, mid + 1)
                    act.wait_ge(probT_turned, mid)
                    act.wait_ge(sum_step, mid * 2)
                    act.activation(prob[:], e_leaky[:], ACT.Exp).then_inc(prob_ready, 1)
                if front is not None:
                    for c in range(CHUNKS):
                        act.wait_ge(hT_turned, front * CHUNKS + c + 1)
                        act.wait_ge(wh_ready, front * 2)
                        act.activation(hT[:, HI, c, :], hT_ps[:, c, :], ACT.Relu).then_inc(hT_hi, 1)

            pipeline(act, body)

        @block.tensor
        def _(pe):
            def nodes(b):
                return slice(b * NODES, (b + 1) * NODES)

            def body(front, mid, back):
                if back is not None:
                    pe.wait_ge(prob_ready, back + 1)
                    pe.wait_ge(probT_lo, back)
                    for b in range(GROUP):
                        last = pe.transpose(probT_ps[:, b, :], prob[:, b, :], k.identity[:])
                    last.then_inc(probT_turned, 1)
                if mid is not None:
                    pe.wait_ge(hT_lo, (mid + 1) * CHUNKS)
                    pe.wait_ge(e_copied, mid)
                    product(pe, e_ps[:].rearrange("p b n -> p (b n)"), lambda a, c: k.attn_vecs[:, a, 1, c, :],
                            lambda b, c: hT[:, b, c, :], stop=False, loose=True)
                    for b in range(GROUP):
                        last = product(pe, e_ps[:, b, :], lambda a, c: hT[:, a, c, nodes(b)],
                                       lambda m, c: k.attn_vecs[:, m, 0, c, :], start=False, loose=True)
                    last.then_inc(e_ready, 1)
                if back is not None:
                    pe.wait_ge(probT_lo, back + 1)
                    pe.wait_ge(wh_lo, (back + 1) * 2)
                    pe.wait_ge(y_ready, back * GROUP)
                    for b in range(GROUP):
                        last = product(pe, att_ps[:, b, :], lambda a, c: probT[:, a, b, :],
                                       lambda m, c: wh[:, m, b, :], chunks=1)
                        if b % 2:
                            last.then_inc(att_ready, 1)
                if mid is not None:
                    pe.wait_ge(wh_lo, mid * 2)
                    for b in range(GROUP):
                        last = product(pe, wh_ps[:, b, :], lambda a, c: hT[:, a, c, nodes(b)],
                                       lambda m, c: k.w[:, m, SPLIT["gat"] + c, :])
                        if b % 2:
                            last.then_inc(wh_ready, 1)
                if front is not None:
                    pe.wait_ge(normed_ready, (front + 1) * GROUP)
                    pe.wait_ge(hT_lo, front * CHUNKS)
                    for c in range(CHUNKS):
                        for b in range(GROUP):
                            last = pe.transpose(hT_ps[:, c, nodes(b)], normed[:, b, c * P:(c + 1) * P], k.identity[:])
                        last.then_inc(hT_turned, 1)

            pipeline(pe, body)


class Group:
    def __init__(self, pairs, j):
        self.pairs, self.j, self.index = pairs, j, pairs * 2 + j

    def parts(self):
        return self.index, self.pairs + (self.j // 2 + 1), self.j % 2


class Group:
    def __init__(self, pairs, j):
        self.pairs, self.j = pairs, j
        self.index, self.parity = pairs * 2 + j, j % 2
        self.same = pairs + (j // 2 + 1)

    def before(self):
        return Group(self.pairs, self.j - 1)

    def exists(self, back):
        return not isinstance(self.index, int) or self.index >= back


def attention_layer(nc, sem, dram, k):
    with ExitStack() as ctx:
        def sb(name, shape, dt=F32):
            return ctx.enter_context(nc.sbuf_tensor("att_" + name, shape, dt))

        def ps(name, shape):
            return ctx.enter_context(nc.psum_tensor("att_" + name, shape, F32))

        class s:
            settled = sem("att_settled")
            stats = sb("stats", [P, GROUP, 6])
            moments = sb("moments", [P, GROUP, 2])
            var_eps = sb("var_eps", [P, GROUP])
            rstd = sb("rstd", [P, GROUP])
        normed = sb("normed", [P, GROUP, FEATURES])
        hT = sb("hT", [P, 2, CHUNKS, TOKENS], F16)
        qT = sb("qT", [P, 2, CHUNKS, TOKENS], F16)
        kT = sb("kT", [P, 2, CHUNKS, TOKENS], F16)
        stack_q = [sb(f"stack_q{j}", [3 * HEAD, HEADS, TOKENS], F16) for j in range(2)]
        stack_k = [sb(f"stack_k{j}", [3 * HEAD, HEADS, TOKENS], F16) for j in range(2)]
        v = [sb(f"v{j}", [P, 2, GROUP, HEADS, HEAD + 1], F16) for j in range(2)]
        score = [sb(f"score{j}", [P, HEADS, NODES]) for j in range(2)]
        prob = [sb(f"prob{j}", [P, HEADS, NODES]) for j in range(2)]
        row_max = sb("row_max", [P, HEADS, 1])
        probT = sb("probT", [P, 2, HEADS, NODES], F16)
        inv_sum = sb("inv_sum", [P, HEADS, 1])
        mixed = [sb(f"mixed{j}", [P, HEADS, HEAD]) for j in range(2)]
        mixedT = sb("mixedT", [P, 2, CHUNKS, NODES], F16)

        score_ps = ps("score_ps", [P, HEADS, NODES])
        probT_ps = ps("probT_ps", [P, HEADS, NODES])
        mix_ps = ps("mix_ps", [P, HEADS, HEAD + 1])
        out_ps = ps("out_ps", [P, FEATURES])
        front_ps = ps("front_ps", [P, CHUNKS, TOKENS])

        moments_ready = sem("att_moments_ready")
        rstd_step = sem("att_rstd_step")
        normed_ready = sem("att_normed_ready")
        turned = sem("att_turned")
        hT_hi = sem("att_hT_hi")
        hT_lo = sem("att_hT_lo")
        q_ready = sem("att_q_ready")
        q_hi = sem("att_q_hi")
        q_lo = sem("att_q_lo")
        k_ready = sem("att_k_ready")
        k_hi = sem("att_k_hi")
        k_lo = sem("att_k_lo")
        v_ready = sem("att_v_ready")
        v_hi = sem("att_v_hi")
        v_lo = sem("att_v_lo")
        ones_ready = sem("att_ones_ready")
        q_stacked = [sem(f"att_q_stacked{j}") for j in range(2)]
        k_stacked = [sem(f"att_k_stacked{j}") for j in range(2)]
        scores_ready = sem("att_scores_ready")
        masked = sem("att_masked")
        max_ready = sem("att_max_ready")
        shifted = sem("att_shifted")
        prob_ready = sem("att_prob_ready")
        prob_turned = sem("att_prob_turned")
        probT_hi = sem("att_probT_hi")
        probT_lo = sem("att_probT_lo")
        mix_ready = sem("att_mix_ready")
        inv_ready = sem("att_inv_ready")
        mixed_ready = sem("att_mixed_ready")
        mixed_turned = sem("att_mixed_turned")
        mixedT_hi = sem("att_mixedT_hi")
        mixedT_lo = sem("att_mixedT_lo")
        out_ready = sem("att_out_ready")
        x_ready = sem("att_x_ready")
        x_biased = sem("att_x_biased")
        block = ctx.enter_context(nc.Block())
        scale = 1.0 / float(HEAD) ** 0.5
        STACK_DMAS = 3 * (P // HEAD) * 16

        def half(j):
            return slice(4 * j, 4 * j + 4)

        def nodes(b):
            return slice(b * NODES, (b + 1) * NODES)

        def pipeline(eng, body):
            def pair(pairs, last=False):
                for j in range(2):
                    for b in range(GROUP):
                        ahead = 1 if b < 3 else 2
                        body(None if last and j + ahead > 1 else (Group(pairs, j + ahead), b), Group(pairs, j), b)
            body((Group(0, 0), 3), None, None)
            for part in (0, 1, 2):
                body((Group(0, 0), part), None, None)
            body((Group(0, 1), 3), None, None)
            pair(0)
            with eng.Fori(1, GROUPS // 2 - 1) as pairs:
                pair(pairs)
            pair(GROUPS // 2 - 1, last=True)
            for b in range(GROUP):
                body(None, Group(GROUPS // 2, 0), b)

        def newest(now, b, back):
            if now is None:
                return None
            n = now.index * GROUP + (b - back)
            if isinstance(n, int) and not 0 <= n < GRAPHS:
                return None
            return n

        def there_is(n):
            return n is not None and (not isinstance(n, int) or n >= 0)

        @block.sync
        def _(sp):
            def stack(dst, sources, ready):
                for i, (src, part) in enumerate(sources):
                    heads = dst[i * HEAD:(i + 1) * HEAD, :, :].rearrange("p (c q) t -> p q c t", c=CHUNKS)
                    for q in range(P // HEAD):
                        sp.dma_start(heads[:, q], src[q * HEAD:(q + 1) * HEAD, part, :, :]).then_inc(ready, 16)

            def body(front, now, b):
                if front is None:
                    return
                f, part = front
                if part == 0:
                    sp.wait_ge(q_lo, (f.index + 1) * CHUNKS)
                    if f.exists(2):
                        sp.wait_ge(scores_ready, (f.index - 1) * GROUP * 2)
                    stack(stack_q[f.parity], ((qT, HI), (qT, HI), (qT, LO)), q_stacked[f.parity])
                if part == 1:
                    sp.wait_ge(k_lo, (f.index + 1) * CHUNKS)
                    stack(stack_k[f.parity], ((kT, HI), (kT, LO), (kT, HI)), k_stacked[f.parity])

            pipeline(sp, body)

        @block.vector
        def _(dve):
            for j in range(2):
                dve.memset(v[j][:, HI, :, :, HEAD:], 1.0).then_inc(ones_ready, 1)
                dve.memset(v[j][:, LO, :, :, HEAD:], 0.0).then_inc(ones_ready, 1)

            def body(front, now, b):
                n = newest(now, b, 2)
                if n is not None:
                    dve.wait_ge(mix_ready, n + 1)
                    dve.wait_ge(mixed_ready, n)
                    dve.reciprocal(inv_sum[:], mix_ps[:, :, HEAD:]).then_inc(inv_ready, 1)
                    dve.wait_ge(inv_ready, n + 1)
                    if there_is(newest(now, b, 4)):
                        dve.wait_ge(mixed_turned, n - 1)
                    dve.tensor_tensor(mixed[b % 2][:], mix_ps[:, :, 0:HEAD], inv_sum[:].broadcast_to([P, HEADS, HEAD]),
                                      ALU.mult).then_inc(mixed_ready, 1)
                n = newest(now, b, 0)
                if n is not None:
                    if there_is(newest(now, b, 2)):
                        dve.wait_ge(prob_ready, n - 1)
                    for h in range(2):
                        dve.wait_ge(scores_ready, n * 2 + h + 1)
                        dve.scalar_tensor_tensor(score[b % 2][:, half(h), :], score_ps[:, half(h), :], scale,
                                                 k.mask_bias[:].broadcast_to([P, 4, NODES]), ALU.mult,
                                                 ALU.add).then_inc(masked, 1)
                    dve.wait_ge(masked, n * 2 + 2)
                    dve.wait_ge(shifted, n)
                    dve.reduce_max(row_max[:, :, 0], score[b % 2][:], AX).then_inc(max_ready, 1)
                if front is not None:
                    f, part = front
                    g = f.index
                    if part in (0, 1):
                        hi, lo, dst, bias = ((q_hi, q_lo, qT, k.bias_q), (k_hi, k_lo, kT, k.bias_k))[part]
                        for c in range(CHUNKS):
                            dve.wait_ge(hi, g * CHUNKS + c + 1)
                            dve.scalar_tensor_tensor(dst[:, LO, c, :], front_ps[:, c, :], bias[:, c:c + 1],
                                                     dst[:, HI, c, :], ALU.add, ALU.subtract).then_inc(lo, 1)
                    if part == 2:
                        for h in range(2):
                            dve.wait_ge(v_hi, g * 2 + h + 1)
                            dst = v[f.parity][:, :, 2 * h:2 * h + 2, :, 0:HEAD]
                            src = front_ps[:, h, :].rearrange("p (b h e) -> p b h e", b=2, h=HEADS)
                            for i in range(2):
                                dve.tensor_tensor(dst[:, LO, i], src[:, i], dst[:, HI, i], ALU.subtract).then_inc(v_lo, 1)
                    if part == 3:
                        dve.wait_ge(rstd_step, g * 2)
                        layer_norm_stats(dve, k, g, moments_ready, s)
                n = newest(now, b, 1)
                if n is not None:
                    for h in range(2):
                        dve.wait_ge(probT_hi, n * 2 + h + 1)
                        dve.tensor_tensor(probT[:, LO, half(h), :], probT_ps[:, half(h), :], probT[:, HI, half(h), :],
                                          ALU.subtract).then_inc(probT_lo, 1)
                if front is not None and part == 3:
                    dve.wait_ge(rstd_step, (g + 1) * 2)
                    dve.wait_ge(turned, g * CHUNKS)
                    for b_ in range(GROUP):
                        dve.tensor_scalar(normed[:, b_, :], k.x[:, graph(g, b_), :].rearrange("p a f -> p (a f)"),
                                          s.moments[:, b_, 0:1], s.rstd[:, b_:b_ + 1], ALU.subtract,
                                          ALU.mult).then_inc(normed_ready, 1)
                n = newest(now, b, 4)
                if n is not None:
                    dve.wait_ge(x_biased, now.index)
                    dve.wait_ge(out_ready, n + 1)
                    xn = k.x[:, bass.ds(n, 1), :].rearrange("p a f -> p (a f)")
                    dve.tensor_tensor(xn, xn, out_ps[:], ALU.add).then_inc(x_ready, 1)
                n = newest(now, b, 3)
                if n is not None:
                    dve.wait_ge(mixedT_hi, n + 1)
                    dve.tensor_tensor(mixedT[:, LO], out_ps[:].rearrange("p (c t) -> p c t", c=CHUNKS), mixedT[:, HI],
                                      ALU.subtract).then_inc(mixedT_lo, 1)
                if front is not None and part == 3:
                    for c in range(CHUNKS):
                        dve.wait_ge(hT_hi, g * CHUNKS + c + 1)
                        dve.scalar_tensor_tensor(hT[:, LO, c, :], front_ps[:, c, :], 0.0, hT[:, HI, c, :], ALU.max,
                                                 ALU.subtract).then_inc(hT_lo, 1)

            pipeline(dve, body)

        @block.gpsimd
        def _(pool):
            def body(front, now, b):
                n = newest(now, b, 0)
                if n is not None:
                    pool.wait_ge(max_ready, n + 1)
                    pool.tensor_tensor(score[b % 2][:], score[b % 2][:], row_max[:].broadcast_to([P, HEADS, NODES]),
                                       ALU.subtract).then_inc(shifted, 1)
                if front is not None and front[1] == 3:
                    g = front[0].index
                    layer_norm_rstd(pool, k, g, moments_ready, rstd_step, s)
                    pool.wait_ge(normed_ready, (g + 1) * GROUP)
                    settle(pool, s)
                    pool.tensor_tensor(k.x[:, group(g), :], k.x[:, group(g), :],
                                       k.attn_bias[:].broadcast_to([P, GROUP, FEATURES]), ALU.add).then_inc(x_biased, 1)

            pipeline(pool, body)

        @block.scalar
        def _(act):
            def body(front, now, b):
                if front is not None:
                    f, part = front
                    g = f.index
                    if part in (0, 1):
                        ready, hi, dst, bias, stacked = ((q_ready, q_hi, qT, k.bias_q, q_stacked),
                                                         (k_ready, k_hi, kT, k.bias_k, k_stacked))[part]
                        if f.exists(1):
                            act.wait_ge(stacked[f.before().parity], f.before().same * STACK_DMAS)
                        for c in range(CHUNKS):
                            act.wait_ge(ready, g * CHUNKS + c + 1)
                            act.activation(dst[:, HI, c, :], front_ps[:, c, :], ACT.Identity,
                                           bias=bias[:, c:c + 1]).then_inc(hi, 1)
                    if part == 2:
                        act.wait_ge(ones_ready, 4)
                        if f.exists(2):
                            act.wait_ge(mix_ready, (g - 1) * GROUP)
                        for h in range(2):
                            act.wait_ge(v_ready, g * 2 + h + 1)
                            dst = v[f.parity][:, HI, 2 * h:2 * h + 2, :, 0:HEAD]
                            act.copy(dst, front_ps[:, h, :].rearrange("p (b h e) -> p b h e", b=2, h=HEADS)).then_inc(v_hi, 1)
                n = newest(now, b, 1)
                if n is not None:
                    act.wait_ge(mix_ready, n)
                    for h in range(2):
                        act.wait_ge(prob_turned, n * 2 + h + 1)
                        act.copy(probT[:, HI, half(h), :], probT_ps[:, half(h), :]).then_inc(probT_hi, 1)
                n = newest(now, b, 3)
                if n is not None:
                    act.wait_ge(mixed_turned, n + 1)
                    act.wait_ge(out_ready, n)
                    act.copy(mixedT[:, HI], out_ps[:].rearrange("p (c t) -> p c t", c=CHUNKS)).then_inc(mixedT_hi, 1)
                n = newest(now, b, 0)
                if n is not None:
                    act.wait_ge(shifted, n + 1)
                    if there_is(newest(now, b, 2)):
                        act.wait_ge(prob_turned, (n - 1) * 2)
                    act.activation(prob[b % 2][:], score[b % 2][:], ACT.Exp).then_inc(prob_ready, 1)
                if front is not None and part == 3:
                    act.wait_ge(v_ready, g * 2)
                    for c in range(CHUNKS):
                        act.wait_ge(turned, g * CHUNKS + c + 1)
                        act.activation(hT[:, HI, c, :], front_ps[:, c, :], ACT.Relu).then_inc(hT_hi, 1)

            pipeline(act, body)

        @block.tensor
        def _(pe):
            def project(f, part):
                g = f.index
                if part in (0, 1):
                    before, ready, slot = ((hT_lo, q_ready, SPLIT["q"]), (q_lo, k_ready, SPLIT["k"]))[part]
                    for c in range(CHUNKS):
                        pe.wait_ge(before, (g + 1) * CHUNKS)
                        product(pe, front_ps[:, c, :], lambda a, i: k.w[:, a, slot + i, c * P:(c + 1) * P],
                                lambda m, i: hT[:, m, i, :]).then_inc(ready, 1)
                if part == 2:
                    pe.wait_ge(k_lo, (g + 1) * CHUNKS)
                    for b in range(GROUP):
                        last = product(pe, front_ps[:, b // 2, (b % 2) * FEATURES:(b % 2 + 1) * FEATURES],
                                       lambda a, c: hT[:, a, c, nodes(b)], lambda m, c: k.w[:, m, SPLIT["v"] + c, :])
                        if b % 2:
                            last.then_inc(v_ready, 1)

            def body(front, now, b):
                n = newest(now, b, 2)
                if n is not None:
                    pe.wait_ge(mixed_ready, n)
                    pe.wait_ge(probT_lo, (n + 1) * 2)
                    source = now if b >= 2 else now.before()
                    pe.wait_ge(v_lo, (source.index + 1) * 4)
                    for h in range(HEADS):
                        last = product(pe, mix_ps[:, h, :], lambda a, c: probT[:, a, h, :],
                                       lambda m, c: v[source.parity][:, m, (b - 2) % GROUP, h, :], chunks=1)
                    last.then_inc(mix_ready, 1)
                n = newest(now, b, 0)
                if n is not None:
                    if b == 0:
                        pe.wait_ge(q_stacked[now.parity], now.same * STACK_DMAS)
                        pe.wait_ge(k_stacked[now.parity], now.same * STACK_DMAS)
                    for h in range(HEADS):
                        if h % 4 == 0 and there_is(newest(now, b, 1)):
                            pe.wait_ge(masked, (n - 1) * 2 + h // 4 + 1)
                        last = pe.matmul(score_ps[:, h, :], stack_q[now.parity][:, h, nodes(b)],
                                         stack_k[now.parity][:, h, nodes(b)], start=True, stop=True)
                        if h % 4 == 3:
                            last.then_inc(scores_ready, 1)
                if front is not None and front[1] < 3:
                    project(*front)
                n = newest(now, b, 1)
                if n is not None:
                    pe.wait_ge(prob_ready, n + 1)
                    for h in range(HEADS):
                        if h % 4 == 0 and there_is(newest(now, b, 2)):
                            pe.wait_ge(probT_lo, (n - 1) * 2 + h // 4 + 1)
                        last = pe.transpose(probT_ps[:, h, :], prob[(b - 1) % 2][:, h, :], k.identity[:])
                        if h % 4 == 3:
                            last.then_inc(prob_turned, 1)
                n = newest(now, b, 4)
                if n is not None:
                    pe.wait_ge(mixedT_lo, n + 1)
                    product(pe, out_ps[:], lambda a, c: mixedT[:, a, c, :],
                            lambda m, c: k.w[:, m, SPLIT["o"] + c, :]).then_inc(out_ready, 1)
                n = newest(now, b, 3)
                if n is not None:
                    pe.wait_ge(mixed_ready, n + 1)
                    pe.wait_ge(x_ready, n)
                    for c in range(CHUNKS):
                        last = pe.transpose(out_ps[:, c * P:(c + 1) * P],
                                            mixed[(b - 3) % 2][:, 4 * c:4 * c + 4, :].rearrange("p h e -> p (h e)"), k.identity[:])
                    last.then_inc(mixed_turned, 1)
                if front is not None and front[1] == 3:
                    g = front[0].index
                    pe.wait_ge(normed_ready, (g + 1) * GROUP)
                    pe.wait_ge(v_lo, g * 4)
                    for c in range(CHUNKS):
                        for b_ in range(GROUP):
                            last = pe.transpose(front_ps[:, c, nodes(b_)], normed[:, b_, c * P:(c + 1) * P], k.identity[:])
                        last.then_inc(turned, 1)

            pipeline(pe, body)


def gated_layer(nc, sem, dram, k):
    with ExitStack() as ctx:
        def sb(name, shape, dt=F32):
            return ctx.enter_context(nc.sbuf_tensor("gru_" + name, shape, dt))

        class Stream:
            def __init__(self, j):
                def sb_(name, shape, dt=F32):
                    return sb(f"{name}{j}", shape, dt)

                def sem_(name):
                    return sem(f"gru_{name}{j}")

                self.settled = sem_("settled")
                self.stats = sb_("stats", [P, GROUP, 6])
                self.moments = sb_("moments", [P, GROUP, 2])
                self.var_eps = sb_("var_eps", [P, GROUP])
                self.rstd = sb_("rstd", [P, GROUP])
                self.normed = sb_("normed", [P, GROUP, FEATURES])
                self.h = sb_("h", [P, CHUNKS, TOKENS])
                self.hT = sb_("hT", [P, 2, CHUNKS, TOKENS], F16)
                self.h_rows = sb_("h_rows", [P, 2, GROUP, FEATURES], F16)
                self.aT = sb_("aT", [P, 2, CHUNKS, TOKENS], F16)
                self.r = sb_("r", [P, CHUNKS, TOKENS])
                self.rh = sb_("rh", [P, 2, CHUNKS, TOKENS], F16)
                self.z = sb_("z", [P, CHUNKS, TOKENS])
                self.new = sb_("new", [P, CHUNKS, TOKENS])
                self.mix_ps = ctx.enter_context(nc.psum_tensor(f"gru_mix_ps{j}", [P, CHUNKS, TOKENS], F32))
                self.gate_ps = ctx.enter_context(nc.psum_tensor(f"gru_gate_ps{j}", [P, CHUNKS, TOKENS], F32))
                self.moments_ready = sem_("moments_ready")
                self.rstd_step = sem_("rstd_step")
                self.normed_ready = sem_("normed_ready")
                self.normed_turned = sem_("normed_turned")
                self.first_copied = sem_("first_copied")
                self.h_hi = sem_("h_hi")
                self.h_lo = sem_("h_lo")
                self.h_turned = sem_("h_turned")
                self.rows_ready = sem_("rows_ready")
                self.a_ready = sem_("a_ready")
                self.a_hi = sem_("a_hi")
                self.a_lo = sem_("a_lo")
                self.r_sum = sem_("r_sum")
                self.r_ready = sem_("r_ready")
                self.rh_full = sem_("rh_full")
                self.rh_hi = sem_("rh_hi")
                self.rh_lo = sem_("rh_lo")
                self.z_sum = sem_("z_sum")
                self.z_ready = sem_("z_ready")
                self.new_sum = sem_("new_sum")
                self.new_ready = sem_("new_ready")
                self.update = sem_("update")
                self.out_turned = sem_("out_turned")
                self.x_ready = sem_("x_ready")

        streams = [Stream(j) for j in range(2)]
        block = ctx.enter_context(nc.Block())

        def nodes(b):
            return slice(b * NODES, (b + 1) * NODES)

        def half(c):
            return slice(c * P, (c + 1) * P)

        def pipeline(eng, body):
            body(0, True, False)
            with eng.Fori(1, GROUPS // 2 - 1) as pairs:
                body(pairs, False, False)
            body(GROUPS // 2 - 1, False, True)

        def turned_before(pairs, t):
            return (pairs * (STEPS - 1) + (t - 1)) * 2

        def turned_view(st, part):
            return st.mix_ps[:, part, :].bitcast(F16).rearrange("p (b f) -> p b f", b=GROUP)

        @block.vector
        def _(dve):
            def norm(st, j, pairs):
                g = pairs * 2 + j
                dve.wait_ge(st.rstd_step, pairs * 2)
                for b in range(GROUP):
                    dve.bn_stats(st.stats[:, b, :], k.x[:, graph(g, b), :].rearrange("p a f -> p (a f)")).then_inc(st.moments_ready, 1)
                dve.wait_ge(st.moments_ready, (pairs * 2 + 1) * GROUP)
                settle(dve, st)
                for b in range(GROUP):
                    dve.bn_aggr(st.moments[:, b, :], st.stats[:, b, :]).then_inc(st.moments_ready, 1)

            def norm_apply(st, j, pairs):
                g = pairs * 2 + j
                dve.wait_ge(st.rstd_step, (pairs + 1) * 2)
                dve.wait_ge(st.normed_turned, pairs * CHUNKS)
                dve.wait_ge(st.rows_ready, pairs * 2 * STEPS)
                for b in range(GROUP):
                    dve.tensor_scalar(st.normed[:, b, :], k.x[:, graph(g, b), :].rearrange("p a f -> p (a f)"),
                                      st.moments[:, b, 0:1], st.rstd[:, b:b + 1], ALU.subtract,
                                      ALU.mult).then_inc(st.normed_ready, 1)

            def finish(st, j, pairs):
                g = pairs * 2 + j
                for c in range(CHUNKS):
                    dve.wait_ge(st.out_turned, pairs * CHUNKS + c + 1)
                    xg = k.x[:, bass.ds(g * GROUP + 2 * c, 2), :]
                    dve.tensor_tensor(xg, xg, st.mix_ps[:, c, :].rearrange("p (b f) -> p b f", b=2),
                                      ALU.add).then_inc(st.x_ready, 1)

            def start(st, pairs):
                q = pairs * STEPS
                dve.wait_ge(st.normed_ready, (pairs + 1) * GROUP)
                dve.wait_ge(st.a_ready, q * 2)
                dve.tensor_scalar(st.h_rows[:, HI], st.normed[:], 0.0, None, ALU.max).then_inc(st.rows_ready, 1)
                dve.wait_ge(st.rows_ready, q * 2 + 1)
                dve.scalar_tensor_tensor(st.h_rows[:, LO], st.normed[:], 0.0, st.h_rows[:, HI], ALU.max,
                                         ALU.subtract).then_inc(st.rows_ready, 1)
                for c in range(CHUNKS):
                    dve.wait_ge(st.h_hi, q * 2 + c + 1)
                    dve.scalar_tensor_tensor(st.hT[:, LO, c, :], st.gate_ps[:, c, :], 0.0, st.hT[:, HI, c, :],
                                             ALU.max, ALU.subtract).then_inc(st.h_lo, 1)

            def rows(st, pairs, t):
                q = pairs * STEPS + t
                dve.wait_ge(st.a_ready, q * 2)
                for part in (HI, LO):
                    dve.wait_ge(st.h_turned, turned_before(pairs, t) + part + 1)
                    dve.tensor_copy(st.h_rows[:, part], turned_view(st, part)).then_inc(st.rows_ready, 1)

            def a_low(st, q):
                for c in range(CHUNKS):
                    dve.wait_ge(st.a_hi, q * 2 + c + 1)
                    dve.tensor_tensor(st.aT[:, LO, c, :], st.mix_ps[:, c, :], st.aT[:, HI, c, :],
                                      ALU.subtract).then_inc(st.a_lo, 1)

            def reset(st, q):
                for c in range(CHUNKS):
                    dve.wait_ge(st.r_ready, q * 2 + c + 1)
                    dve.tensor_tensor(st.r[:, c, :], st.r[:, c, :], st.h[:, c, :], ALU.mult).then_inc(st.rh_full, 1)
                for c in range(CHUNKS):
                    dve.wait_ge(st.rh_hi, q * 2 + c + 1)
                    dve.tensor_tensor(st.rh[:, LO, c, :], st.r[:, c, :], st.rh[:, HI, c, :],
                                      ALU.subtract).then_inc(st.rh_lo, 1)

            def update(st, q, last_step):
                for c in range(CHUNKS):
                    n = q * 6 + 3 * c
                    dve.wait_ge(st.new_ready, q * 2 + c + 1)
                    dve.tensor_tensor(st.new[:, c, :], st.new[:, c, :], st.h[:, c, :], ALU.subtract).then_inc(st.update, 1)
                    dve.wait_ge(st.z_ready, q * 2 + c + 1)
                    dve.wait_ge(st.update, n + 1)
                    dve.tensor_tensor(st.new[:, c, :], st.new[:, c, :], st.z[:, c, :], ALU.mult).then_inc(st.update, 1)
                    dve.wait_ge(st.update, n + 2)
                    dve.tensor_tensor(st.h[:, c, :], st.h[:, c, :], st.new[:, c, :], ALU.add).then_inc(st.update, 1)
                if not last_step:
                    for c in range(CHUNKS):
                        dve.wait_ge(st.h_hi, q * 2 + 2 + c + 1)
                        dve.tensor_tensor(st.hT[:, LO, c, :], st.h[:, c, :], st.hT[:, HI, c, :],
                                          ALU.subtract).then_inc(st.h_lo, 1)

            for j, st in enumerate(streams):
                norm(st, j, 0)
                norm_apply(st, j, 0)

            def body(pairs, first, last):
                for t in range(STEPS):
                    q = pairs * STEPS + t
                    for j, st in enumerate(streams):
                        if t == 0:
                            if not first:
                                finish(st, j, pairs - 1)
                            start(st, pairs)
                        else:
                            rows(st, pairs, t)
                        a_low(st, q)
                    for j, st in enumerate(streams):
                        reset(st, q)
                        if t == 1 and not last:
                            norm(st, j, pairs + 1)
                        if t == 2 and not last:
                            norm_apply(st, j, pairs + 1)
                        update(st, q, t == STEPS - 1)

            pipeline(dve, body)
            for j, st in enumerate(streams):
                finish(st, j, GROUPS // 2 - 1)

        @block.gpsimd
        def _(pool):
            def rstd(st, pairs):
                layer_norm_rstd(pool, k, pairs, st.moments_ready, st.rstd_step, st)

            for st in streams:
                rstd(st, 0)

            def body(pairs, first, last):
                if not last:
                    for st in streams:
                        rstd(st, pairs + 1)

            pipeline(pool, body)

        @block.scalar
        def _(act):
            def start(st, pairs):
                q = pairs * STEPS
                for c in range(CHUNKS):
                    act.wait_ge(st.normed_turned, pairs * CHUNKS + c + 1)
                    act.wait_ge(st.out_turned, pairs * CHUNKS)
                    act.wait_ge(st.r_sum, q * 2)
                    act.activation(st.h[:, c, :], st.gate_ps[:, c, :], ACT.Relu).then_inc(st.first_copied, 1)
                    act.activation(st.hT[:, HI, c, :], st.gate_ps[:, c, :], ACT.Relu).then_inc(st.h_hi, 1)

            def a_high(st, q):
                for c in range(CHUNKS):
                    act.wait_ge(st.a_ready, q * 2 + c + 1)
                    act.wait_ge(st.z_sum, q * 2)
                    act.copy(st.aT[:, HI, c, :], st.mix_ps[:, c, :]).then_inc(st.a_hi, 1)

            def gates(st, q):
                for c in range(CHUNKS):
                    act.wait_ge(st.r_sum, q * 2 + c + 1)
                    act.wait_ge(st.rh_lo, q * 2)
                    act.activation(st.r[:, c, :], st.gate_ps[:, c, :], ACT.Sigmoid,
                                   bias=k.bias_r[:, c:c + 1]).then_inc(st.r_ready, 1)
                for c in range(CHUNKS):
                    act.wait_ge(st.rh_full, q * 2 + c + 1)
                    act.wait_ge(st.new_sum, q * 2)
                    act.copy(st.rh[:, HI, c, :], st.r[:, c, :]).then_inc(st.rh_hi, 1)
                for c in range(CHUNKS):
                    act.wait_ge(st.z_sum, q * 2 + c + 1)
                    act.wait_ge(st.update, q * 6)
                    act.activation(st.z[:, c, :], st.gate_ps[:, c, :], ACT.Sigmoid,
                                   bias=k.bias_z[:, c:c + 1]).then_inc(st.z_ready, 1)

            def candidate(st, q, last_step):
                for c in range(CHUNKS):
                    act.wait_ge(st.new_sum, q * 2 + c + 1)
                    act.activation(st.new[:, c, :], st.mix_ps[:, c, :], ACT.Tanh,
                                   bias=k.bias_h[:, c:c + 1]).then_inc(st.new_ready, 1)
                if not last_step:
                    for c in range(CHUNKS):
                        act.wait_ge(st.update, q * 6 + 3 * c + 3)
                        act.copy(st.hT[:, HI, c, :], st.h[:, c, :]).then_inc(st.h_hi, 1)

            def body(pairs, first, last):
                for t in range(STEPS):
                    q = pairs * STEPS + t
                    for st in streams:
                        if t == 0:
                            start(st, pairs)
                        a_high(st, q)
                    for st in streams:
                        gates(st, q)
                        candidate(st, q, t == STEPS - 1)

            pipeline(act, body)

        @block.tensor
        def _(pe):
            def weight(name, a, i, c):
                return k.w[:, a, SPLIT[name] + i, half(c)]

            def finish(st, pairs):
                pe.wait_ge(st.update, (pairs + 1) * STEPS * 6)
                for c in range(CHUNKS):
                    for b in (2 * c, 2 * c + 1):
                        for i in range(CHUNKS):
                            at = (b % 2) * FEATURES + i * P
                            last = pe.transpose(st.mix_ps[:, c, at:at + P], st.h[:, i, nodes(b)], k.identity[:])
                    last.then_inc(st.out_turned, 1)

            def start(st, pairs):
                pe.wait_ge(st.normed_ready, (pairs + 1) * GROUP)
                pe.wait_ge(st.z_ready, pairs * STEPS * 2)
                for c in range(CHUNKS):
                    for b in range(GROUP):
                        last = pe.transpose(st.gate_ps[:, c, nodes(b)], st.normed[:, b, half(c)], k.identity[:])
                    last.then_inc(st.normed_turned, 1)

            def turn(st, pairs, t):
                q = pairs * STEPS + t
                pe.wait_ge(st.new_ready, q * 2)
                for part, ready in ((HI, st.h_hi), (LO, st.h_lo)):
                    pe.wait_ge(ready, q * 2 + 2)
                    for b in range(GROUP):
                        for c in range(CHUNKS):
                            last = pe.transpose(turned_view(st, part)[:, b, half(c)], st.hT[:, part, c, nodes(b)],
                                                k.identity16[:])
                    last.then_inc(st.h_turned, 1)

            def gate_from_h(st, pairs, q):
                pe.wait_ge(st.h_lo, q * 2 + 2)
                pe.wait_ge(st.first_copied, (pairs + 1) * CHUNKS)
                pe.wait_ge(st.z_ready, q * 2)
                for c in range(CHUNKS):
                    product(pe, st.gate_ps[:, c, :], lambda a, i: weight("u3", a, i, c),
                            lambda m, i: st.hT[:, m, i, :], stop=False, loose=True)

            def neighbours(st, pairs, t):
                q = pairs * STEPS + t
                pe.wait_ge(st.rows_ready, q * 2 + 2)
                if t == 0:
                    pe.wait_ge(st.x_ready, pairs * CHUNKS)
                for c in range(CHUNKS):
                    for b in range(GROUP):
                        last = product(pe, st.mix_ps[:, c, nodes(b)], lambda a, i: st.h_rows[:, a, b, half(c)],
                                       lambda m, i: k.adjT[:, m, :], chunks=1)
                    last.then_inc(st.a_ready, 1)

            def gates_from_a(st, q):
                pe.wait_ge(st.a_lo, q * 2 + 2)
                for c in range(CHUNKS):
                    product(pe, st.gate_ps[:, c, :], lambda a, i: weight("w4", a, i, c),
                            lambda m, i: st.aT[:, m, i, :], start=False, loose=True).then_inc(st.r_sum, 1)
                for c in range(CHUNKS):
                    product(pe, st.mix_ps[:, c, :], lambda a, i: weight("w5", a, i, c),
                            lambda m, i: st.aT[:, m, i, :], stop=False, loose=True)
                for c in range(CHUNKS):
                    pe.wait_ge(st.r_ready, q * 2 + c + 1)
                    product(pe, st.gate_ps[:, c, :], lambda a, i: weight("w3", a, i, c),
                            lambda m, i: st.aT[:, m, i, :], start=False, loose=True).then_inc(st.z_sum, 1)

            def candidate(st, q):
                pe.wait_ge(st.rh_lo, q * 2 + 2)
                for c in range(CHUNKS):
                    product(pe, st.mix_ps[:, c, :], lambda a, i: weight("u5", a, i, c),
                            lambda m, i: st.rh[:, m, i, :], start=False, loose=True).then_inc(st.new_sum, 1)

            def body(pairs, first, last):
                for t in range(STEPS):
                    q = pairs * STEPS + t
                    for st in streams:
                        if t == 0:
                            if not first:
                                finish(st, pairs - 1)
                            start(st, pairs)
                        else:
                            turn(st, pairs, t)
                        gate_from_h(st, pairs, q)
                        neighbours(st, pairs, t)
                    for st in streams:
                        gates_from_a(st, q)
                        candidate(st, q)

            pipeline(pe, body)
            for st in streams:
                finish(st, GROUPS // 2 - 1)


def conv_layer(nc, sem, dram, k):
    with ExitStack() as ctx:
        def sb(name, shape, dt=F32):
            return ctx.enter_context(nc.sbuf_tensor("conv_" + name, shape, dt))

        def ps(name, shape):
            return ctx.enter_context(nc.psum_tensor("conv_" + name, shape, F32))

        class s:
            settled = sem("conv_settled")
            stats = sb("stats", [P, GROUP, 6])
            moments = sb("moments", [P, GROUP, 2])
            var_eps = sb("var_eps", [P, GROUP])
            rstd = sb("rstd", [P, GROUP])
        normed = sb("normed", [P, GROUP, FEATURES])
        h_rows = sb("h_rows", [P, 2, GROUP, FEATURES], F16)
        aT = sb("aT", [P, 2, CHUNKS, TOKENS], F16)
        a_ps = ps("a_ps", [P, CHUNKS, TOKENS])
        y_ps = ps("y_ps", [P, GROUP, FEATURES])

        moments_ready = sem("conv_moments_ready")
        rstd_step = sem("conv_rstd_step")
        normed_ready = sem("conv_normed_ready")
        rows_hi = sem("conv_rows_hi")
        rows_lo = sem("conv_rows_lo")
        x_biased = sem("conv_x_biased")
        a_ready = sem("conv_a_ready")
        a_hi = sem("conv_a_hi")
        a_lo = sem("conv_a_lo")
        y_ready = sem("conv_y_ready")
        x_ready = sem("conv_x_ready")
        stored = sem("conv_stored")
        block = ctx.enter_context(nc.Block())

        def pipeline(eng, body):
            body(0, None, None)
            body(1, 0, None)
            body(2, 1, 0)
            with eng.Fori(3, GROUPS) as i:
                body(i, i - 1, i - 2)
            body(None, GROUPS - 1, GROUPS - 2)
            body(None, None, GROUPS - 1)

        def nodes(b):
            return slice(b * NODES, (b + 1) * NODES)

        @block.sync
        def _(sp):
            view = dram["out"].rearrange("b n d -> n b d")

            def body(front, mid, back):
                if back is not None:
                    sp.wait_ge(x_ready, (back + 1) * 2)
                    if not isinstance(back, int) or back > 0:
                        sp.wait_ge(stored, back * 16)
                    sp.dma_start(view[:, group(back), :], k.x[:, group(back), :]).then_inc(stored, 16)

            pipeline(sp, body)
            sp.wait_ge(stored, GROUPS * 16)

        @block.vector
        def _(dve):
            def body(front, mid, back):
                if front is not None:
                    dve.wait_ge(rstd_step, front * 2)
                    layer_norm_stats(dve, k, front, moments_ready, s)
                if mid is not None:
                    for c in range(CHUNKS):
                        dve.wait_ge(a_hi, mid * CHUNKS + c + 1)
                        dve.tensor_tensor(aT[:, LO, c, :], a_ps[:, c, :], aT[:, HI, c, :], ALU.subtract).then_inc(a_lo, 1)
                if front is not None:
                    dve.wait_ge(rstd_step, (front + 1) * 2)
                    dve.wait_ge(rows_lo, front)
                    for b in range(GROUP):
                        dve.tensor_scalar(normed[:, b, :], k.x[:, graph(front, b), :].rearrange("p a f -> p (a f)"),
                                          s.moments[:, b, 0:1], s.rstd[:, b:b + 1], ALU.subtract,
                                          ALU.mult).then_inc(normed_ready, 1)
                if back is not None:
                    dve.wait_ge(x_biased, back + 1)
                    for j in range(2):
                        dve.wait_ge(y_ready, back * 2 + j + 1)
                        xh = k.x[:, bass.ds(back * GROUP + 2 * j, 2), :]
                        dve.tensor_tensor(xh, xh, y_ps[:, 2 * j:2 * j + 2, :], ALU.add).then_inc(x_ready, 1)
                if front is not None:
                    dve.wait_ge(rows_hi, front + 1)
                    dve.scalar_tensor_tensor(h_rows[:, LO], normed[:], 0.0, h_rows[:, HI], ALU.max,
                                             ALU.subtract).then_inc(rows_lo, 1)

            pipeline(dve, body)

        @block.gpsimd
        def _(pool):
            def body(front, mid, back):
                if front is not None:
                    layer_norm_rstd(pool, k, front, moments_ready, rstd_step, s)
                    pool.wait_ge(normed_ready, (front + 1) * GROUP)
                    settle(pool, s)
                    pool.tensor_tensor(k.x[:, group(front), :], k.x[:, group(front), :],
                                       k.conv_bias[:].broadcast_to([P, GROUP, FEATURES]), ALU.add).then_inc(x_biased, 1)

            pipeline(pool, body)

        @block.scalar
        def _(act):
            def body(front, mid, back):
                if mid is not None:
                    act.wait_ge(y_ready, mid * 2)
                    for c in range(CHUNKS):
                        act.wait_ge(a_ready, mid * CHUNKS + c + 1)
                        act.copy(aT[:, HI, c, :], a_ps[:, c, :]).then_inc(a_hi, 1)
                if front is not None:
                    act.wait_ge(normed_ready, (front + 1) * GROUP)
                    act.wait_ge(a_ready, front * CHUNKS)
                    act.activation(h_rows[:, HI], normed[:], ACT.Relu).then_inc(rows_hi, 1)

            pipeline(act, body)

        @block.tensor
        def _(pe):
            def body(front, mid, back):
                if back is not None:
                    pe.wait_ge(a_lo, (back + 1) * CHUNKS)
                    pe.wait_ge(x_ready, back * 2)
                    for b in range(GROUP):
                        last = product(pe, y_ps[:, b, :], lambda a, c: aT[:, a, c, nodes(b)],
                                       lambda m, c: k.w[:, m, SPLIT["conv"] + c, :])
                        if b % 2:
                            last.then_inc(y_ready, 1)
                if mid is not None:
                    pe.wait_ge(rows_lo, mid + 1)
                    pe.wait_ge(a_lo, mid * CHUNKS)
                    for c in range(CHUNKS):
                        for b in range(GROUP):
                            last = product(pe, a_ps[:, c, nodes(b)], lambda a, i: h_rows[:, a, b, c * P:(c + 1) * P],
                                           lambda m, i: k.adjT[:, m, :], chunks=1)
                        last.then_inc(a_ready, 1)

            pipeline(pe, body)


def build(nc, dram, out):
    dram = dict(dram, out=out)
    with ExitStack() as ctx:
        def sb(name, shape, dt=F32):
            return ctx.enter_context(nc.sbuf_tensor(name, shape, dt))

        def sem(name):
            return ctx.enter_context(nc.semaphore(name))

        class k:
            x = sb("x_res", [P, GRAPHS, FEATURES])
            w = sb("w_split", [P, 2, SPLIT_SLOTS, FEATURES], F16)
            identity = sb("identity", [P, P])
            identity16 = sb("identity16", [P, P], F16)
            adjT = sb("adjT", [P, 2, NODES], F16)
            mask = sb("mask", [P, 1, NODES])
            mask_bias = sb("mask_bias", [P, 1, NODES])
            attn_vecs = sb("attn_vecs", [P, 2, 2, CHUNKS, P], F16)
            bias_q = sb("bias_q", [P, CHUNKS])
            bias_k = sb("bias_k", [P, CHUNKS])
            bias_z = sb("bias_z", [P, CHUNKS])
            bias_r = sb("bias_r", [P, CHUNKS])
            bias_h = sb("bias_h", [P, CHUNKS])
            attn_bias = sb("attn_bias", [P, 1, FEATURES])
            conv_bias = sb("conv_bias", [P, 1, FEATURES])
            beta = sb("beta", [P, 1])
            eps = sb("eps", [P, GROUP])
            minus_half = sb("minus_half", [P, GROUP])

        load_constants(nc, sem, dram, k)
        for layer in (gat_layer, attention_layer, gated_layer, conv_layer):
            layer(nc, sem, dram, k)


def kernel(**inputs):
    import numpy as np
    import concourse.bacc as bacc
    from concourse.bass_utils import run_bass_kernel_spmd

    f32 = {name: np.asarray(a, dtype=np.float32) for name, a in inputs.items()}

    def tile_rows(v):
        return np.broadcast_to(v.reshape(1, -1), (P, v.size))

    def column(v):
        return v.reshape(CHUNKS, P).T

    a = f32["L0_gnn_a"].reshape(2, FEATURES)
    arrays = {
        "x": f32["x"],
        "weights": np.concatenate([
            f32["L0_gnn_W"], f32["L1_gnn_Wq"], f32["L1_gnn_Wk"], f32["L1_gnn_Wv"], f32["L1_gnn_Wo"],
            f32["L2_gnn_w3_w"].T, f32["L2_gnn_w4_w"].T, f32["L2_gnn_w5_w"].T, f32["L2_gnn_u3_w"].T,
            f32["L2_gnn_u5_w"].T, f32["L3_gnn_weight"]], axis=0),
        "cols": np.concatenate([column(v) for v in (
            a[0], a[1], f32["L1_gnn_bq"], f32["L1_gnn_bk"], f32["L1_gnn_bv"], f32["L2_gnn_w3_b"],
            f32["L2_gnn_u3_b"], f32["L2_gnn_w4_b"], f32["L2_gnn_w5_b"], f32["L2_gnn_u5_b"])], axis=1),
        "rows": np.stack([tile_rows(v) for v in (a[0], a[1], f32["L1_gnn_bo"], f32["L3_gnn_bias"])], axis=1),
        "adj": np.stack([f32["adj"], f32["adj"].T], axis=1),
        "identity": np.eye(P, dtype=np.float32),
        "beta": np.broadcast_to(f32["L0_gnn_beta"].reshape(1, 1), (P, 1)),
    }
    arrays = {name: np.ascontiguousarray(v) for name, v in arrays.items()}

    nc = bacc.Bacc("TRN2", target_bir_lowering=False, num_devices=1)
    dram = {name: nc.dram_tensor("in_" + name, v.shape, F32, kind="ExternalInput").ap() for name, v in arrays.items()}
    out = nc.dram_tensor("out_0", (GRAPHS, NODES, FEATURES), F32, kind="ExternalOutput").ap()
    build(nc, dram, out)
    result = run_bass_kernel_spmd(nc, [{"in_" + name: v for name, v in arrays.items()}], core_ids=[0])
    return result.results[0]["out_0"]
```

```python
from contextlib import ExitStack

import concourse.bass as bass
from concourse import mybir

F32 = mybir.dt.float32
F16 = mybir.dt.float16
ALU = mybir.AluOpType
ACT = mybir.ActivationFunctionType
AX = mybir.AxisListType.X

GRAPHS, NODES, FEATURES = 64, 128, 256
P = 128
CHUNKS = FEATURES // P
GROUP = 4
GROUPS = GRAPHS // GROUP
TOKENS = GROUP * NODES
HEADS = 8
HEAD = FEATURES // HEADS
LN_EPS = 1e-5
MASKED = -1e9
LEAK = 0.2
STEPS = 3

RAW = {"gat": 0, "q": 2, "k": 4, "v": 6, "o": 8, "w3": 10, "w4": 14, "w5": 18, "u3": 22, "u5": 24, "conv": 26}
RAW_SLOTS = 28
SPLIT = {"gat": 0, "q": 2, "k": 4, "v": 6, "o": 8, "conv": 10, "u3": 12, "u5": 14, "w4": 16, "w5": 18, "w3": 20}
SPLIT_SLOTS = 22
COLS = {"a1": 0, "a2": 2, "bq": 4, "bk": 6, "bv": 8, "w3b": 10, "u3b": 12, "w4b": 14, "w5b": 16, "u5b": 18}
COL_SLOTS = 20
ROWS = {"a1": 0, "a2": 1, "bo": 2, "conv_bias": 3}

HI, LO = 0, 1
PARTS = ((HI, HI), (HI, LO), (LO, HI))


def product(pe, out, stationary, moving, chunks=CHUNKS, start=True, stop=True, loose=False):
    last = None
    for c in range(chunks):
        for n, (a, b) in enumerate(PARTS):
            last = pe.matmul(out, stationary(a, c), moving(b, c),
                             start=start and c == 0 and n == 0,
                             stop=stop and c == chunks - 1 and n == len(PARTS) - 1,
                             skip_group_check=loose)
    return last


def graph(g, b):
    return bass.ds(g * GROUP + b, 1)


def group(g):
    return bass.ds(g * GROUP, GROUP)


def load_constants(nc, sem, dram, k):
    with ExitStack() as ctx:
        def sb(name, shape, dt=F32):
            return ctx.enter_context(nc.sbuf_tensor(name, shape, dt))

        raw = sb("raw_weights", [P, RAW_SLOTS, FEATURES])
        cols = sb("cols", [P, COL_SLOTS])
        rows = sb("rows", [P, 4, FEATURES])
        adj = sb("adj_raw", [P, 2, NODES])
        summed = sb("summed", [P, 3, CHUNKS, FEATURES])
        attn_vec = sb("attn_vec", [P, 2, CHUNKS])
        scratch = sb("scratch", [P, 2, CHUNKS, FEATURES])
        spread = sb("spread", [P, 3, CHUNKS, P])
        bv_split = sb("bv_split", [P, 2, CHUNKS, P], F16)
        crow = ctx.enter_context(nc.psum_tensor("crow", [P, FEATURES], F32))

        small_in = sem("small_in")
        gat_in = sem("gat_in")
        weights_in = sem("weights_in")
        done = sem("setup_done")
        split = sem("bv_split_ready")
        crow_ready = sem("crow_ready")
        block = ctx.enter_context(nc.Block())

        @block.sync
        def _(sp):
            view = dram["weights"].rearrange("(k p) f -> p k f", p=P)
            sp.dma_start(raw[:, 0:2, :], view[:, 0:2, :]).then_inc(gat_in, 16)
            sp.dma_start(cols[:], dram["cols"]).then_inc(small_in, 16)
            sp.dma_start(rows[:], dram["rows"]).then_inc(small_in, 16)
            sp.dma_start(adj[:], dram["adj"]).then_inc(small_in, 16)
            sp.dma_start(k.identity[:], dram["identity"]).then_inc(small_in, 16)
            sp.dma_start(k.beta[:], dram["beta"]).then_inc(small_in, 16)
            sp.dma_start(raw[:, 2:RAW_SLOTS, :], view[:, 2:RAW_SLOTS, :]).then_inc(weights_in, 16)

        @block.vector
        def _(dve):
            n = [0]

            def step(ins):
                n[0] += 1
                ins.then_inc(done, 1)
                dve.wait_ge(done, n[0])

            def split_of(hi, lo, full):
                step(dve.tensor_copy(hi, full))
                step(dve.tensor_tensor(lo, full, hi, ALU.subtract))

            step(dve.memset(k.eps[:], LN_EPS))
            step(dve.memset(k.minus_half[:], -0.5))
            step(dve.memset(k.minus_one[:], -1.0))
            dve.wait_ge(small_in, 16 * 5)
            step(dve.tensor_copy(k.mask[:, 0, :], adj[:, 0, :]))
            split_of(k.adjT[:, HI, :], k.adjT[:, LO, :], adj[:, 1, :])
            step(dve.tensor_scalar(k.mask_bias[:, 0, :], adj[:, 0, :], -1.0, 1.0, ALU.mult, ALU.add))
            step(dve.tensor_scalar(k.mask_bias[:, 0, :], k.mask_bias[:, 0, :], MASKED, None, ALU.mult))
            dve.wait_ge(gat_in, 16)
            for v in range(2):
                for c in range(CHUNKS):
                    step(dve.tensor_tensor(scratch[:, v, c, :], raw[:, c, :], rows[:, ROWS["a1"] + v, :], ALU.mult))
                    step(dve.reduce_sum(attn_vec[:, v, c:c + 1], scratch[:, v, c, :], AX))
                    step(dve.tensor_copy(spread[:, v, c, :], attn_vec[:, v, c:c + 1].broadcast_to([P, P])))
                    split_of(k.attn_vecs[:, HI, v, c, :], k.attn_vecs[:, LO, v, c, :], spread[:, v, c, :])
            split_of(k.w[:, HI, 0:2, :], k.w[:, LO, 0:2, :], raw[:, 0:2, :])
            dve.wait_ge(weights_in, 16)
            for name in ("q", "k", "v", "o", "u3", "u5", "conv"):
                a, b = RAW[name], SPLIT[name]
                split_of(k.w[:, HI, b:b + 2, :], k.w[:, LO, b:b + 2, :], raw[:, a:a + 2, :])
            for c in range(CHUNKS):
                step(dve.tensor_copy(spread[:, 2, c, :], cols[:, COLS["bv"] + c:COLS["bv"] + c + 1].broadcast_to([P, P])))
            step(dve.tensor_copy(bv_split[:, HI], spread[:, 2]))
            step(dve.tensor_tensor(bv_split[:, LO], spread[:, 2], bv_split[:, HI], ALU.subtract))
            dve.engine_nop().then_inc(split, 1)
            for j, name in enumerate(("w3", "w4", "w5")):
                a = RAW[name]
                step(dve.tensor_tensor(summed[:, j], raw[:, a:a + 2, :], raw[:, a + 2:a + 4, :], ALU.add))
            step(dve.tensor_tensor(summed[:, 0], summed[:, 0], summed[:, 1], ALU.subtract))
            for j, name in enumerate(("w3", "w4", "w5")):
                b = SPLIT[name]
                split_of(k.w[:, HI, b:b + 2, :], k.w[:, LO, b:b + 2, :], summed[:, j])
            step(dve.tensor_copy(k.bias_q[:], cols[:, COLS["bq"]:COLS["bq"] + 2]))
            step(dve.tensor_copy(k.bias_k[:], cols[:, COLS["bk"]:COLS["bk"] + 2]))
            for out, first, second in ((k.bias_z, "w3b", "u3b"), (k.bias_r, "w4b", "u3b"), (k.bias_h, "w5b", "u5b")):
                step(dve.tensor_tensor(out[:], cols[:, COLS[first]:COLS[first] + 2],
                                       cols[:, COLS[second]:COLS[second] + 2], ALU.add))
            step(dve.tensor_copy(k.conv_bias[:, 0, :], rows[:, ROWS["conv_bias"], :]))
            dve.wait_ge(crow_ready, 1)
            step(dve.tensor_tensor(k.attn_bias[:, 0, :], crow[:], rows[:, ROWS["bo"], :], ALU.add))

        @block.tensor
        def _(pe):
            pe.wait_ge(split, 1)
            product(pe, crow[:], lambda a, c: bv_split[:, a, c, :],
                    lambda b, c: k.w[:, b, SPLIT["o"] + c, :]).then_inc(crow_ready, 1)


def settle(eng, s):
    eng.sem_inc(s.settled, 1)


def layer_norm_stats(dve, k, g, ready, s):
    for b in range(GROUP):
        dve.bn_stats(s.stats[:, b, :], k.x[:, graph(g, b), :].rearrange("p a f -> p (a f)")).then_inc(ready, 1)
    dve.wait_ge(ready, (g * 2 + 1) * GROUP)
    settle(dve, s)
    for b in range(GROUP):
        dve.bn_aggr(s.moments[:, b, :], s.stats[:, b, :]).then_inc(ready, 1)


def layer_norm_rstd(pool, k, g, moments_ready, pool_step, s):
    pool.wait_ge(moments_ready, (g + 1) * 2 * GROUP)
    pool.tensor_tensor(s.var_eps[:], s.moments[:, :, 1], k.eps[:], ALU.add).then_inc(pool_step, 1)
    pool.wait_ge(pool_step, g * 2 + 1)
    pool.tensor_tensor(s.rstd[:], s.var_eps[:], k.minus_half[:], ALU.pow).then_inc(pool_step, 1)


def gat_layer(nc, sem, dram, k):
    with ExitStack() as ctx:
        def sb(name, shape, dt=F32):
            return ctx.enter_context(nc.sbuf_tensor("gat_" + name, shape, dt))

        def ps(name, shape):
            return ctx.enter_context(nc.psum_tensor("gat_" + name, shape, F32))

        class s:
            settled = sem("gat_settled")
            stats = sb("stats", [P, GROUP, 6])
            moments = sb("moments", [P, GROUP, 2])
            var_eps = sb("var_eps", [P, GROUP])
            rstd = sb("rstd", [P, GROUP])
        normed = sb("normed", [P, GROUP, FEATURES])
        hT = sb("hT", [P, 2, CHUNKS, TOKENS], F16)
        wh = sb("wh", [P, 2, GROUP, FEATURES], F16)
        beta_wh = sb("beta_wh", [P, GROUP, FEATURES])
        e_raw = sb("e_raw", [P, GROUP, NODES])
        e_leaky = sb("e_leaky", [P, GROUP, NODES])
        row_max = sb("row_max", [P, GROUP, 1])
        prob = sb("prob", [P, GROUP, NODES])
        row_sum = sb("row_sum", [P, GROUP])
        inv_sum = sb("inv_sum", [P, GROUP])
        probT = sb("probT", [P, 2, GROUP, NODES], F16)
        y = sb("y", [P, GROUP, FEATURES])
        y_neg = sb("y_neg", [P, GROUP, FEATURES])
        y_exp = sb("y_exp", [P, GROUP, FEATURES])

        hT_ps = ps("hT_ps", [P, CHUNKS, TOKENS])
        e_ps = ps("e_ps", [P, GROUP, NODES])
        wh_ps = ps("wh_ps", [P, GROUP, FEATURES])
        probT_ps = ps("probT_ps", [P, GROUP, NODES])
        att_ps = ps("att_ps", [P, GROUP, FEATURES])

        x_in = sem("x_in")
        moments_ready = sem("gat_moments_ready")
        rstd_step = sem("gat_rstd_step")
        normed_ready = sem("gat_normed_ready")
        hT_turned = sem("gat_hT_turned")
        hT_hi = sem("gat_hT_hi")
        hT_lo = sem("gat_hT_lo")
        e_ready = sem("gat_e_ready")
        e_copied = sem("gat_e_copied")
        leaky_ready = sem("gat_leaky_ready")
        masked_ready = sem("gat_masked_ready")
        max_ready = sem("gat_max_ready")
        shifted_ready = sem("gat_shifted_ready")
        prob_ready = sem("gat_prob_ready")
        sum_step = sem("gat_sum_step")
        wh_ready = sem("gat_wh_ready")
        wh_hi = sem("gat_wh_hi")
        beta_wh_ready = sem("gat_beta_wh_ready")
        wh_lo = sem("gat_wh_lo")
        probT_turned = sem("gat_probT_turned")
        probT_hi = sem("gat_probT_hi")
        probT_lo = sem("gat_probT_lo")
        att_ready = sem("gat_att_ready")
        y_ready = sem("gat_y_ready")
        y_neg_ready = sem("gat_y_neg_ready")
        y_exp_ready = sem("gat_y_exp_ready")
        y_pos_ready = sem("gat_y_pos_ready")
        x_step = sem("gat_x_step")
        block = ctx.enter_context(nc.Block())

        def pipeline(eng, body):
            body(0, None, None)
            body(1, 0, None)
            body(2, 1, 0)
            with eng.Fori(3, GROUPS) as i:
                body(i, i - 1, i - 2)
            body(None, GROUPS - 1, GROUPS - 2)
            body(None, None, GROUPS - 1)

        @block.sync
        def _(sp):
            x_view = dram["x"].rearrange("b n d -> n b d")
            sp.dma_start(k.x[:, group(0), :], x_view[:, group(0), :]).then_inc(x_in, 16)
            with sp.Fori(1, GROUPS) as g:
                sp.wait_ge(x_in, g * 16)
                sp.dma_start(k.x[:, group(g), :], x_view[:, group(g), :]).then_inc(x_in, 16)
            sp.wait_ge(x_in, GROUPS * 16)

        @block.vector
        def _(dve):
            def body(front, mid, back):
                if back is not None:
                    dve.wait_ge(probT_hi, back + 1)
                    if not isinstance(back, int) or back > 0:
                        dve.wait_ge(att_ready, back * 2)
                    dve.tensor_tensor(probT[:, LO], probT_ps[:], probT[:, HI], ALU.subtract).then_inc(probT_lo, 1)
                if mid is not None:
                    dve.wait_ge(e_copied, mid + 1)
                    dve.wait_ge(shifted_ready, mid)
                    dve.wait_ge(prob_ready, mid)
                    dve.scalar_tensor_tensor(e_leaky[:], e_raw[:], LEAK, e_raw[:], ALU.mult,
                                             ALU.max).then_inc(leaky_ready, 1)
                if back is not None:
                    dve.wait_ge(y_exp_ready, back)
                    dve.wait_ge(y_pos_ready, back)
                    dve.wait_ge(x_step, back * 2)
                    dve.wait_ge(beta_wh_ready, (back + 1) * 2)
                    dve.wait_ge(sum_step, (back + 1) * 2)
                    for b in range(GROUP):
                        if b % 2 == 0:
                            dve.wait_ge(att_ready, back * 2 + b // 2 + 1)
                        dve.scalar_tensor_tensor(y[:, b, :], att_ps[:, b, :], inv_sum[:, b:b + 1], beta_wh[:, b, :],
                                                 ALU.mult, ALU.add).then_inc(y_ready, 1)
                if mid is not None:
                    for j in range(2):
                        dve.wait_ge(wh_hi, mid * 2 + j + 1)
                        h = slice(2 * j, 2 * j + 2)
                        dve.tensor_tensor(wh[:, LO, h, :], wh_ps[:, h, :], wh[:, HI, h, :],
                                          ALU.subtract).then_inc(wh_lo, 1)
                if front is not None:
                    dve.wait_ge(x_in, (front + 1) * 16)
                    dve.wait_ge(rstd_step, front * 2)
                    layer_norm_stats(dve, k, front, moments_ready, s)
                if mid is not None:
                    dve.wait_ge(masked_ready, mid + 1)
                    dve.reduce_max(row_max[:, :, 0], e_leaky[:], AX).then_inc(max_ready, 1)
                if back is not None:
                    dve.wait_ge(y_neg_ready, back + 1)
                    dve.tensor_scalar(y[:], y[:], 0.0, -1.0, ALU.max, ALU.add).then_inc(y_pos_ready, 1)
                if front is not None:
                    dve.wait_ge(rstd_step, (front + 1) * 2)
                    dve.wait_ge(hT_turned, front * CHUNKS)
                    for b in range(GROUP):
                        dve.tensor_scalar(normed[:, b, :], k.x[:, graph(front, b), :].rearrange("p a f -> p (a f)"),
                                          s.moments[:, b, 0:1], s.rstd[:, b:b + 1], ALU.subtract,
                                          ALU.mult).then_inc(normed_ready, 1)
                if mid is not None:
                    dve.wait_ge(prob_ready, mid + 1)
                    dve.reduce_sum(row_sum[:], prob[:], AX).then_inc(sum_step, 1)
                    dve.wait_ge(sum_step, mid * 2 + 1)
                    if back is not None:
                        dve.wait_ge(y_ready, (back + 1) * GROUP)
                    dve.reciprocal(inv_sum[:], row_sum[:]).then_inc(sum_step, 1)
                if front is not None:
                    for c in range(CHUNKS):
                        dve.wait_ge(hT_hi, front * CHUNKS + c + 1)
                        dve.scalar_tensor_tensor(hT[:, LO, c, :], hT_ps[:, c, :], 0.0, hT[:, HI, c, :], ALU.max,
                                                 ALU.subtract).then_inc(hT_lo, 1)

            pipeline(dve, body)

        @block.gpsimd
        def _(pool):
            def body(front, mid, back):
                if mid is not None:
                    pool.wait_ge(leaky_ready, mid + 1)
                    pool.tensor_tensor(e_leaky[:], e_leaky[:], k.mask[:].broadcast_to([P, GROUP, NODES]),
                                       ALU.mult).then_inc(masked_ready, 1)
                if front is not None:
                    layer_norm_rstd(pool, k, front, moments_ready, rstd_step, s)
                if mid is not None:
                    pool.wait_ge(max_ready, mid + 1)
                    pool.tensor_tensor(e_leaky[:], e_leaky[:], row_max[:].broadcast_to([P, GROUP, NODES]),
                                       ALU.subtract).then_inc(shifted_ready, 1)
                if back is not None:
                    pool.wait_ge(y_pos_ready, back + 1)
                    settle(pool, s)
                    pool.tensor_tensor(k.x[:, group(back), :], k.x[:, group(back), :], y[:], ALU.add).then_inc(x_step, 1)
                    pool.wait_ge(x_step, back * 2 + 1)
                    pool.wait_ge(y_exp_ready, back + 1)
                    settle(pool, s)
                    pool.tensor_tensor(k.x[:, group(back), :], k.x[:, group(back), :], y_exp[:],
                                       ALU.add).then_inc(x_step, 1)

            pipeline(pool, body)

        @block.scalar
        def _(act):
            def body(front, mid, back):
                if back is not None:
                    act.wait_ge(probT_turned, back + 1)
                    act.wait_ge(att_ready, back * 2)
                    act.copy(probT[:, HI], probT_ps[:]).then_inc(probT_hi, 1)
                if mid is not None:
                    act.wait_ge(e_ready, mid + 1)
                    act.wait_ge(leaky_ready, mid)
                    act.copy(e_raw[:], e_ps[:]).then_inc(e_copied, 1)
                    for j in range(2):
                        h = slice(2 * j, 2 * j + 2)
                        act.wait_ge(wh_ready, mid * 2 + j + 1)
                        if back is not None:
                            act.wait_ge(y_ready, (back + 1) * GROUP)
                            act.wait_ge(att_ready, (back + 1) * 2)
                        act.activation(beta_wh[:, h, :], wh_ps[:, h, :], ACT.Identity,
                                       scale=k.beta[:, 0:1]).then_inc(beta_wh_ready, 1)
                        act.copy(wh[:, HI, h, :], wh_ps[:, h, :]).then_inc(wh_hi, 1)
                if back is not None:
                    act.wait_ge(y_ready, (back + 1) * GROUP)
                    act.wait_ge(y_exp_ready, back)
                    act.activation(y_neg[:], y[:], ACT.Relu, scale=-1.0).then_inc(y_neg_ready, 1)
                    act.wait_ge(y_neg_ready, back + 1)
                    act.wait_ge(x_step, back * 2)
                    act.activation(y_exp[:], y_neg[:], ACT.Exp, scale=-1.0).then_inc(y_exp_ready, 1)
                if mid is not None:
                    act.wait_ge(shifted_ready, mid + 1)
                    act.wait_ge(probT_turned, mid)
                    act.wait_ge(sum_step, mid * 2)
                    act.activation(prob[:], e_leaky[:], ACT.Exp).then_inc(prob_ready, 1)
                if front is not None:
                    for c in range(CHUNKS):
                        act.wait_ge(hT_turned, front * CHUNKS + c + 1)
                        act.wait_ge(wh_ready, front * 2)
                        act.activation(hT[:, HI, c, :], hT_ps[:, c, :], ACT.Relu).then_inc(hT_hi, 1)

            pipeline(act, body)

        @block.tensor
        def _(pe):
            def nodes(b):
                return slice(b * NODES, (b + 1) * NODES)

            def body(front, mid, back):
                if back is not None:
                    pe.wait_ge(prob_ready, back + 1)
                    pe.wait_ge(probT_lo, back)
                    for b in range(GROUP):
                        last = pe.transpose(probT_ps[:, b, :], prob[:, b, :], k.identity[:])
                    last.then_inc(probT_turned, 1)
                if mid is not None:
                    pe.wait_ge(hT_lo, (mid + 1) * CHUNKS)
                    pe.wait_ge(e_copied, mid)
                    product(pe, e_ps[:].rearrange("p b n -> p (b n)"), lambda a, c: k.attn_vecs[:, a, 1, c, :],
                            lambda b, c: hT[:, b, c, :], stop=False, loose=True)
                    for b in range(GROUP):
                        last = product(pe, e_ps[:, b, :], lambda a, c: hT[:, a, c, nodes(b)],
                                       lambda m, c: k.attn_vecs[:, m, 0, c, :], start=False, loose=True)
                    last.then_inc(e_ready, 1)
                if back is not None:
                    pe.wait_ge(probT_lo, back + 1)
                    pe.wait_ge(wh_lo, (back + 1) * 2)
                    pe.wait_ge(y_ready, back * GROUP)
                    for b in range(GROUP):
                        last = product(pe, att_ps[:, b, :], lambda a, c: probT[:, a, b, :],
                                       lambda m, c: wh[:, m, b, :], chunks=1)
                        if b % 2:
                            last.then_inc(att_ready, 1)
                if mid is not None:
                    pe.wait_ge(wh_lo, mid * 2)
                    for b in range(GROUP):
                        last = product(pe, wh_ps[:, b, :], lambda a, c: hT[:, a, c, nodes(b)],
                                       lambda m, c: k.w[:, m, SPLIT["gat"] + c, :])
                        if b % 2:
                            last.then_inc(wh_ready, 1)
                if front is not None:
                    pe.wait_ge(normed_ready, (front + 1) * GROUP)
                    pe.wait_ge(hT_lo, front * CHUNKS)
                    for c in range(CHUNKS):
                        for b in range(GROUP):
                            last = pe.transpose(hT_ps[:, c, nodes(b)], normed[:, b, c * P:(c + 1) * P], k.identity[:])
                        last.then_inc(hT_turned, 1)

            pipeline(pe, body)


class Group:
    def __init__(self, pairs, j):
        self.pairs, self.j = pairs, j
        self.index, self.parity = pairs * 2 + j, j % 2
        self.same = pairs + (j // 2 + 1)

    def before(self):
        return Group(self.pairs, self.j - 1)

    def exists(self, back):
        return not isinstance(self.index, int) or self.index >= back


def attention_layer(nc, sem, dram, k):
    with ExitStack() as ctx:
        def sb(name, shape, dt=F32):
            return ctx.enter_context(nc.sbuf_tensor("att_" + name, shape, dt))

        def ps(name, shape):
            return ctx.enter_context(nc.psum_tensor("att_" + name, shape, F32))

        class s:
            settled = sem("att_settled")
            stats = sb("stats", [P, GROUP, 6])
            moments = sb("moments", [P, GROUP, 2])
            var_eps = sb("var_eps", [P, GROUP])
            rstd = sb("rstd", [P, GROUP])
        normed = sb("normed", [P, GROUP, FEATURES])
        hT = sb("hT", [P, 2, CHUNKS, TOKENS], F16)
        neg_mean = sb("neg_mean", [P, GROUP])
        q_full = sb("q_full", [P, CHUNKS, TOKENS])
        k_full = sb("k_full", [P, CHUNKS, TOKENS])
        qT = sb("qT", [P, 2, CHUNKS, TOKENS], F16)
        kT = sb("kT", [P, 2, CHUNKS, TOKENS], F16)
        stack_q = [sb(f"stack_q{j}", [3 * HEAD, HEADS, TOKENS], F16) for j in range(2)]
        stack_k = [sb(f"stack_k{j}", [3 * HEAD, HEADS, TOKENS], F16) for j in range(2)]
        v = [sb(f"v{j}", [P, 2, GROUP, HEADS, HEAD + 1], F16) for j in range(2)]
        score = [sb(f"score{j}", [P, HEADS, NODES]) for j in range(2)]
        prob = [sb(f"prob{j}", [P, HEADS, NODES]) for j in range(2)]
        row_max = sb("row_max", [P, 2, HEADS, 1])
        probT = sb("probT", [P, 2, HEADS, NODES], F16)
        inv_sum = sb("inv_sum", [P, HEADS, 1])
        mixed = [sb(f"mixed{j}", [P, HEADS, HEAD]) for j in range(2)]
        mixedT = sb("mixedT", [P, 2, CHUNKS, NODES], F16)
        out_copy = [sb(f"out_copy{j}", [P, FEATURES]) for j in range(2)]

        score_ps = ps("score_ps", [P, HEADS, NODES])
        probT_ps = ps("probT_ps", [P, HEADS, NODES])
        mix_ps = ps("mix_ps", [P, HEADS, HEAD + 1])
        out_ps = ps("out_ps", [P, FEATURES])
        front_ps = ps("front_ps", [P, CHUNKS, TOKENS])

        moments_ready = sem("att_moments_ready")
        rstd_step = sem("att_rstd_step")
        normed_ready = sem("att_normed_ready")
        turned = sem("att_turned")
        hT_hi = sem("att_hT_hi")
        hT_lo = sem("att_hT_lo")
        shift_step = sem("att_shift_step")
        q_full_ready = sem("att_q_full_ready")
        k_full_ready = sem("att_k_full_ready")
        q_ready = sem("att_q_ready")
        q_lo = sem("att_q_lo")
        k_ready = sem("att_k_ready")
        k_lo = sem("att_k_lo")
        v_ready = sem("att_v_ready")
        v_full_ready = sem("att_v_full_ready")
        v_lo = sem("att_v_lo")
        ones_ready = sem("att_ones_ready")
        q_stacked = [sem(f"att_q_stacked{j}") for j in range(2)]
        k_stacked = [sem(f"att_k_stacked{j}") for j in range(2)]
        scores_ready = sem("att_scores_ready")
        masked = sem("att_masked")
        max_ready = sem("att_max_ready")
        shifted = sem("att_shifted")
        prob_ready = sem("att_prob_ready")
        prob_turned = sem("att_prob_turned")
        probT_hi = sem("att_probT_hi")
        probT_lo = sem("att_probT_lo")
        mix_ready = sem("att_mix_ready")
        inv_ready = sem("att_inv_ready")
        mixed_ready = sem("att_mixed_ready")
        mixed_turned = sem("att_mixed_turned")
        mixedT_hi = sem("att_mixedT_hi")
        mixedT_lo = sem("att_mixedT_lo")
        out_ready = sem("att_out_ready")
        out_copied = sem("att_out_copied")
        x_ready = sem("att_x_ready")
        x_biased = sem("att_x_biased")
        block = ctx.enter_context(nc.Block())
        scale = 1.0 / float(HEAD) ** 0.5
        STACK_DMAS = 3 * (P // HEAD) * 16

        def half(j):
            return slice(4 * j, 4 * j + 4)

        def nodes(b):
            return slice(b * NODES, (b + 1) * NODES)

        def pipeline(eng, body):
            def pair(pairs, last=False):
                for j in range(2):
                    for b in range(GROUP):
                        ahead = 1 if b < 3 else 2
                        after = None if last else Group(pairs, j + 2)
                        body(None if last and j + ahead > 1 else (Group(pairs, j + ahead), b), Group(pairs, j), b,
                             (after, b) if after and b < 2 else None, after if b == 2 else None)
            first, second = Group(0, 0), Group(0, 1)
            body(None, None, None, (first, 0), None)
            body(None, None, None, (first, 1), None)
            body(None, None, None, None, first)
            body((first, 3), None, None, None, None)
            body((first, 0), None, None, (second, 0), None)
            body((first, 1), None, None, (second, 1), None)
            body((first, 2), None, None, None, second)
            body((second, 3), None, None, None, None)
            pair(0)
            with eng.Fori(1, GROUPS // 2 - 1) as pairs:
                pair(pairs)
            pair(GROUPS // 2 - 1, last=True)
            for b in range(GROUP):
                body(None, Group(GROUPS // 2, 0), b, None, None)

        def newest(now, b, back):
            if now is None:
                return None
            n = now.index * GROUP + (b - back)
            if isinstance(n, int) and not 0 <= n < GRAPHS:
                return None
            return n

        def there_is(n):
            return n is not None and (not isinstance(n, int) or n >= 0)

        @block.sync
        def _(sp):
            def stack(dst, src, part, places, ready):
                for i in places:
                    heads = dst[i * HEAD:(i + 1) * HEAD, :, :].rearrange("p (c q) t -> p q c t", c=CHUNKS)
                    for q in range(P // HEAD):
                        sp.dma_start(heads[:, q], src[q * HEAD:(q + 1) * HEAD, part, :, :]).then_inc(ready, 16)

            def body(front, now, b, stats, norm):
                if front is None:
                    return
                f, part = front
                if part == 0:
                    sp.wait_ge(q_full_ready, (f.index + 1) * CHUNKS)
                    if f.exists(2):
                        sp.wait_ge(scores_ready, (f.index - 1) * GROUP * 2)
                    stack(stack_q[f.parity], qT, HI, (0, 1), q_stacked[f.parity])
                    sp.wait_ge(q_lo, (f.index + 1) * CHUNKS)
                    stack(stack_q[f.parity], qT, LO, (2,), q_stacked[f.parity])
                if part == 1:
                    sp.wait_ge(k_full_ready, (f.index + 1) * CHUNKS)
                    stack(stack_k[f.parity], kT, HI, (0, 2), k_stacked[f.parity])
                    sp.wait_ge(k_lo, (f.index + 1) * CHUNKS)
                    stack(stack_k[f.parity], kT, LO, (1,), k_stacked[f.parity])

            pipeline(sp, body)

        @block.vector
        def _(dve):
            for j in range(2):
                dve.memset(v[j][:, HI, :, :, HEAD:], 1.0).then_inc(ones_ready, 1)
                dve.memset(v[j][:, LO, :, :, HEAD:], 0.0).then_inc(ones_ready, 1)

            def layer_norm_half(dve, f, h):
                g = f.index
                for b in (2 * h, 2 * h + 1):
                    dve.bn_stats(s.stats[:, b, :], k.x[:, graph(g, b), :].rearrange("p a f -> p (a f)")).then_inc(moments_ready, 1)
                if h == 1:
                    dve.wait_ge(shift_step, g * 2)
                    dve.wait_ge(moments_ready, (g * 2 + 1) * GROUP)
                    settle(dve, s)
                    for b in range(GROUP):
                        dve.bn_aggr(s.moments[:, b, :], s.stats[:, b, :]).then_inc(moments_ready, 1)

            def body(front, now, b, stats, norm):
                n, turning = newest(now, b, 0), newest(now, b, 2)

                def masked_scores(h):
                    if h == 0 and there_is(newest(now, b, 2)):
                        dve.wait_ge(prob_ready, (n - 1) * 2)
                    dve.wait_ge(scores_ready, n * 2 + (h + 1))
                    dve.scalar_tensor_tensor(score[b % 2][:, half(h), :], score_ps[:, half(h), :], scale,
                                             k.mask_bias[:].broadcast_to([P, 4, NODES]), ALU.mult,
                                             ALU.add).then_inc(masked, 1)
                    dve.wait_ge(masked, n * 2 + (h + 1))
                    dve.reduce_max(row_max[:, b % 2, half(h), 0], score[b % 2][:, half(h), :],
                                   AX).then_inc(max_ready, 1)

                if turning is not None:
                    for h in range(2):
                        dve.wait_ge(probT_hi, turning * 2 + (h + 1))
                        dve.tensor_tensor(probT[:, LO, half(h), :], probT_ps[:, half(h), :], probT[:, HI, half(h), :],
                                          ALU.subtract).then_inc(probT_lo, 1)
                out = newest(now, b, 3)
                if out is not None:
                    dve.wait_ge(mixedT_hi, out + 1)
                    dve.tensor_tensor(mixedT[:, LO], out_ps[:].rearrange("p (c t) -> p c t", c=CHUNKS), mixedT[:, HI],
                                      ALU.subtract).then_inc(mixedT_lo, 1)
                if n is not None:
                    masked_scores(0)
                if front is not None and front[1] == 3:
                    for c in range(CHUNKS):
                        dve.wait_ge(hT_hi, front[0].index * CHUNKS + (c + 1))
                        dve.scalar_tensor_tensor(hT[:, LO, c, :], front_ps[:, c, :], 0.0, hT[:, HI, c, :], ALU.max,
                                                 ALU.subtract).then_inc(hT_lo, 1)
                if n is not None:
                    masked_scores(1)
                if stats is not None:
                    layer_norm_half(dve, *stats)
                n = newest(now, b, 2)
                if n is not None:
                    dve.wait_ge(mix_ready, n + 1)
                    dve.wait_ge(mixed_ready, n)
                    dve.reciprocal(inv_sum[:], mix_ps[:, :, HEAD:]).then_inc(inv_ready, 1)
                    dve.wait_ge(inv_ready, n + 1)
                    if there_is(newest(now, b, 4)):
                        dve.wait_ge(mixed_turned, n - 1)
                    dve.tensor_tensor(mixed[b % 2][:], mix_ps[:, :, 0:HEAD],
                                      inv_sum[:].broadcast_to([P, HEADS, HEAD]), ALU.mult).then_inc(mixed_ready, 1)

            pipeline(dve, body)

        @block.gpsimd
        def _(pool):
            def body(front, now, b, stats, norm):
                n = newest(now, b, 4)
                if n is not None:
                    pool.wait_ge(x_biased, now.index * 2)
                    pool.wait_ge(out_copied, n + 1)
                    xn = k.x[:, bass.ds(n, 1), :].rearrange("p a f -> p (a f)")
                    pool.tensor_tensor(xn, xn, out_copy[b % 2][:], ALU.add).then_inc(x_ready, 1)
                for h in range(2):
                    n = newest(now, b, 0)
                    if n is not None:
                        pool.wait_ge(max_ready, n * 2 + (h + 1))
                        pool.tensor_tensor(score[b % 2][:, half(h), :], score[b % 2][:, half(h), :],
                                           row_max[:, b % 2, half(h), :].broadcast_to([P, 4, NODES]),
                                           ALU.subtract).then_inc(shifted, 1)
                    if front is None:
                        continue
                    f, part = front
                    g = f.index
                    if part in (0, 1):
                        full_ready, full, lo, dst = ((q_full_ready, q_full, q_lo, qT), (k_full_ready, k_full, k_lo, kT))[part]
                        pool.wait_ge(full_ready, g * CHUNKS + (h + 1))
                        pool.tensor_tensor(dst[:, LO, h, :], full[:, h, :], dst[:, HI, h, :],
                                           ALU.subtract).then_inc(lo, 1)
                    if part == 2:
                        pool.wait_ge(v_full_ready, g * 2 + (h + 1))
                        dst = v[f.parity][:, :, 2 * h:2 * h + 2, :, 0:HEAD]
                        src = q_full[:, h, :].rearrange("p (b h e) -> p b h e", b=2, h=HEADS)
                        for i in range(2):
                            pool.tensor_tensor(dst[:, LO, i], src[:, i], dst[:, HI, i], ALU.subtract).then_inc(v_lo, 1)
                    if part == 3:
                        if h == 0:
                            pool.wait_ge(normed_ready, (g + 1) * GROUP)
                            settle(pool, s)
                        xs = k.x[:, bass.ds(g * GROUP + 2 * h, 2), :]
                        pool.tensor_tensor(xs, xs, k.attn_bias[:].broadcast_to([P, 2, FEATURES]), ALU.add).then_inc(x_biased, 1)
                if stats is not None and stats[1] == 1:
                    g = stats[0].index
                    pool.wait_ge(normed_ready, g * GROUP)
                    layer_norm_rstd(pool, k, g, moments_ready, rstd_step, s)
                    pool.tensor_tensor(neg_mean[:], s.moments[:, :, 0], k.minus_one[:], ALU.mult).then_inc(shift_step, 1)
                    pool.wait_ge(rstd_step, (g + 1) * 2)
                    pool.wait_ge(shift_step, g * 2 + 1)
                    pool.tensor_tensor(neg_mean[:], neg_mean[:], s.rstd[:], ALU.mult).then_inc(shift_step, 1)

            pipeline(pool, body)

        @block.scalar
        def _(act):
            def normalise(g, graphs):
                for b in graphs:
                    act.activation(normed[:, b, :], k.x[:, graph(g, b), :].rearrange("p a f -> p (a f)"), ACT.Identity,
                                   scale=s.rstd[:, b:b + 1], bias=neg_mean[:, b:b + 1]).then_inc(normed_ready, 1)

            def body(front, now, b, stats, norm):
                n = newest(now, b, 4)
                if n is not None:
                    act.wait_ge(out_ready, n + 1)
                    if there_is(newest(now, b, 6)):
                        act.wait_ge(x_ready, n - 1)
                    act.copy(out_copy[b % 2][:], out_ps[:]).then_inc(out_copied, 1)
                n = newest(now, b, 2)
                if n is not None:
                    act.wait_ge(mix_ready, n)
                    for h in range(2):
                        act.wait_ge(prob_turned, n * 2 + (h + 1))
                        act.copy(probT[:, HI, half(h), :], probT_ps[:, half(h), :]).then_inc(probT_hi, 1)
                if front is not None:
                    f, part = front
                    g = f.index
                    if part == 0:
                        act.wait_ge(v_lo, g * 4)
                    if part == 2:
                        act.wait_ge(q_lo, (g + 1) * CHUNKS)
                        act.wait_ge(ones_ready, 4)
                        if f.exists(2):
                            act.wait_ge(mix_ready, (g - 1) * GROUP)
                    if part in (0, 1) and f.exists(1):
                        stacked = (q_stacked, k_stacked)[part]
                        act.wait_ge(stacked[f.before().parity], f.before().same * STACK_DMAS)
                    if part == 3:
                        act.wait_ge(v_ready, g * 2)
                for h in range(2):
                    n = newest(now, b, 1)
                    if n is not None:
                        act.wait_ge(shifted, n * 2 + (h + 1))
                        if there_is(newest(now, b, 3)):
                            act.wait_ge(prob_turned, (n - 1) * 2)
                        act.activation(prob[(b - 1) % 2][:, half(h), :], score[(b - 1) % 2][:, half(h), :],
                                       ACT.Exp).then_inc(prob_ready, 1)
                    n = newest(now, b, 3)
                    if n is not None and h == 0:
                        act.wait_ge(mixed_turned, n + 1)
                        act.wait_ge(out_ready, n)
                        act.copy(mixedT[:, HI], out_ps[:].rearrange("p (c t) -> p c t", c=CHUNKS)).then_inc(mixedT_hi, 1)
                    if front is None:
                        continue
                    if part in (0, 1):
                        ready, full_ready, full, dst, bias = ((q_ready, q_full_ready, q_full, qT, k.bias_q),
                                                              (k_ready, k_full_ready, k_full, kT, k.bias_k))[part]
                        act.wait_ge(ready, g * CHUNKS + (h + 1))
                        act.activation(dst[:, HI, h, :], front_ps[:, h, :], ACT.Identity, bias=bias[:, h:h + 1])
                        act.activation(full[:, h, :], front_ps[:, h, :], ACT.Identity,
                                       bias=bias[:, h:h + 1]).then_inc(full_ready, 1)
                    if part == 2:
                        act.wait_ge(v_ready, g * 2 + (h + 1))
                        dst = v[f.parity][:, HI, 2 * h:2 * h + 2, :, 0:HEAD]
                        act.copy(dst, front_ps[:, h, :].rearrange("p (b h e) -> p b h e", b=2, h=HEADS))
                        act.copy(q_full[:, h, :], front_ps[:, h, :]).then_inc(v_full_ready, 1)
                    if part == 3:
                        act.wait_ge(turned, g * CHUNKS + (h + 1))
                        act.activation(hT[:, HI, h, :], front_ps[:, h, :], ACT.Relu).then_inc(hT_hi, 1)
                if norm is not None:
                    act.wait_ge(turned, norm.index * CHUNKS)
                    act.wait_ge(shift_step, (norm.index + 1) * 2)
                    normalise(norm.index, range(GROUP))

            pipeline(act, body)

        @block.tensor
        def _(pe):
            def front_half(f, part, h):
                g = f.index
                if part in (0, 1):
                    before, ready, slot = ((hT_lo, q_ready, SPLIT["q"]), (q_full_ready, k_ready, SPLIT["k"]))[part]
                    pe.wait_ge(before, (g + 1) * CHUNKS)
                    product(pe, front_ps[:, h, :], lambda a, i: k.w[:, a, slot + i, h * P:(h + 1) * P],
                            lambda m, i: hT[:, m, i, :]).then_inc(ready, 1)
                if part == 2:
                    pe.wait_ge(k_full_ready, (g + 1) * CHUNKS)
                    for b in (2 * h, 2 * h + 1):
                        last = product(pe, front_ps[:, h, (b % 2) * FEATURES:(b % 2 + 1) * FEATURES],
                                       lambda a, c: hT[:, a, c, nodes(b)], lambda m, c: k.w[:, m, SPLIT["v"] + c, :])
                    last.then_inc(v_ready, 1)
                if part == 3:
                    pe.wait_ge(normed_ready, (g + 1) * GROUP)
                    pe.wait_ge(v_full_ready, g * 2)
                    for b in range(GROUP):
                        last = pe.transpose(front_ps[:, h, nodes(b)], normed[:, b, h * P:(h + 1) * P], k.identity[:])
                    last.then_inc(turned, 1)

            def body(front, now, b, stats, norm):
                n = newest(now, b, 2)
                if n is not None:
                    for h in range(HEADS):
                        if h % 4 == 0:
                            pe.wait_ge(prob_ready, n * 2 + (h // 4 + 1))
                            if there_is(newest(now, b, 3)):
                                pe.wait_ge(probT_lo, (n - 1) * 2 + (h // 4 + 1))
                        last = pe.transpose(probT_ps[:, h, :], prob[b % 2][:, h, :], k.identity[:])
                        if h % 4 == 3:
                            last.then_inc(prob_turned, 1)
                if front is not None and front[1] < 3:
                    front_half(*front, 0)
                n = newest(now, b, 0)
                if n is not None:
                    if b == 0:
                        pe.wait_ge(q_stacked[now.parity], now.same * STACK_DMAS)
                        pe.wait_ge(k_stacked[now.parity], now.same * STACK_DMAS)
                    for h in range(HEADS):
                        if h % 4 == 0 and there_is(newest(now, b, 1)):
                            pe.wait_ge(masked, (n - 1) * 2 + (h // 4 + 1))
                        last = pe.matmul(score_ps[:, h, :], stack_q[now.parity][:, h, nodes(b)],
                                         stack_k[now.parity][:, h, nodes(b)], start=True, stop=True)
                        if h % 4 == 3:
                            last.then_inc(scores_ready, 1)
                n = newest(now, b, 3)
                if n is not None:
                    pe.wait_ge(mixed_ready, n + 1)
                    if there_is(newest(now, b, 4)):
                        pe.wait_ge(out_copied, n)
                    for c in range(CHUNKS):
                        last = pe.transpose(out_ps[:, c * P:(c + 1) * P],
                                            mixed[(b - 3) % 2][:, 4 * c:4 * c + 4, :].rearrange("p h e -> p (h e)"), k.identity[:])
                    last.then_inc(mixed_turned, 1)
                if front is not None:
                    if front[1] == 3:
                        front_half(*front, 0)
                    front_half(*front, 1)
                n = newest(now, b, 2)
                if n is not None:
                    if there_is(newest(now, b, 3)):
                        pe.wait_ge(mixed_ready, n)
                    pe.wait_ge(probT_lo, (n + 1) * 2)
                    source = now if b >= 2 else now.before()
                    pe.wait_ge(v_lo, (source.index + 1) * 4)
                    for h in range(HEADS):
                        last = product(pe, mix_ps[:, h, :], lambda a, c: probT[:, a, h, :],
                                       lambda m, c: v[source.parity][:, m, (b - 2) % GROUP, h, :], chunks=1)
                    last.then_inc(mix_ready, 1)
                n = newest(now, b, 3)
                if n is not None:
                    pe.wait_ge(mixedT_lo, n + 1)
                    product(pe, out_ps[:], lambda a, c: mixedT[:, a, c, :],
                            lambda m, c: k.w[:, m, SPLIT["o"] + c, :]).then_inc(out_ready, 1)

            pipeline(pe, body)


def gated_layer(nc, sem, dram, k):
    with ExitStack() as ctx:
        def sb(name, shape, dt=F32):
            return ctx.enter_context(nc.sbuf_tensor("gru_" + name, shape, dt))

        class Stream:
            def __init__(self, j):
                def sb_(name, shape, dt=F32):
                    return sb(f"{name}{j}", shape, dt)

                def sem_(name):
                    return sem(f"gru_{name}{j}")

                self.settled = sem_("settled")
                self.stats = sb_("stats", [P, GROUP, 6])
                self.moments = sb_("moments", [P, GROUP, 2])
                self.var_eps = sb_("var_eps", [P, GROUP])
                self.rstd = sb_("rstd", [P, GROUP])
                self.normed = sb_("normed", [P, GROUP, FEATURES])
                self.h = [sb_(f"h_{n}_", [P, CHUNKS, TOKENS]) for n in range(2)]
                self.hT = sb_("hT", [P, 2, CHUNKS, TOKENS], F16)
                self.h_rows = sb_("h_rows", [P, 2, GROUP, FEATURES], F16)
                self.aT = sb_("aT", [P, 2, CHUNKS, TOKENS], F16)
                self.r = sb_("r", [P, CHUNKS, TOKENS])
                self.rh = sb_("rh", [P, 2, CHUNKS, TOKENS], F16)
                self.z = sb_("z", [P, CHUNKS, TOKENS])
                self.kept = sb_("kept", [P, CHUNKS, TOKENS])
                self.new = sb_("new", [P, CHUNKS, TOKENS])
                self.mix_ps = ctx.enter_context(nc.psum_tensor(f"gru_mix_ps{j}", [P, CHUNKS, TOKENS], F32))
                self.gate_ps = ctx.enter_context(nc.psum_tensor(f"gru_gate_ps{j}", [P, CHUNKS, TOKENS], F32))
                self.moments_ready = sem_("moments_ready")
                self.rstd_step = sem_("rstd_step")
                self.normed_ready = sem_("normed_ready")
                self.normed_turned = sem_("normed_turned")
                self.first_copied = sem_("first_copied")
                self.h_hi = sem_("h_hi")
                self.h_lo = sem_("h_lo")
                self.h_turned = sem_("h_turned")
                self.rows_hi = sem_("rows_hi")
                self.rows_lo = sem_("rows_lo")
                self.a_ready = sem_("a_ready")
                self.a_hi = sem_("a_hi")
                self.a_lo = sem_("a_lo")
                self.r_sum = sem_("r_sum")
                self.r_ready = sem_("r_ready")
                self.rh_full = sem_("rh_full")
                self.rh_hi = sem_("rh_hi")
                self.rh_lo = sem_("rh_lo")
                self.z_sum = sem_("z_sum")
                self.z_ready = sem_("z_ready")
                self.kept_step = sem_("kept_step")
                self.new_sum = sem_("new_sum")
                self.new_ready = sem_("new_ready")
                self.scaled = sem_("scaled")
                self.h_ready = sem_("h_ready")
                self.x_ready = sem_("x_ready")

        streams = [Stream(j) for j in range(2)]
        block = ctx.enter_context(nc.Block())

        def nodes(b):
            return slice(b * NODES, (b + 1) * NODES)

        def half(c):
            return slice(c * P, (c + 1) * P)

        def bank(st, c):
            return st.mix_ps[:, c, :].rearrange("p (b f) -> p b f", b=GROUP)

        def pipeline(eng, body):
            body(0, True, False)
            with eng.Fori(1, GROUPS // 2 - 1) as pairs:
                body(pairs, False, False)
            body(GROUPS // 2 - 1, False, True)

        @block.vector
        def _(dve):
            def norm(st, j, pairs):
                g = pairs * 2 + j
                dve.wait_ge(st.rstd_step, pairs * 2)
                for b in range(GROUP):
                    dve.bn_stats(st.stats[:, b, :], k.x[:, graph(g, b), :].rearrange("p a f -> p (a f)")).then_inc(st.moments_ready, 1)
                dve.wait_ge(st.moments_ready, (pairs * 2 + 1) * GROUP)
                settle(dve, st)
                for b in range(GROUP):
                    dve.bn_aggr(st.moments[:, b, :], st.stats[:, b, :]).then_inc(st.moments_ready, 1)

            def norm_apply(st, j, pairs):
                g = pairs * 2 + j
                dve.wait_ge(st.rstd_step, (pairs + 1) * 2)
                dve.wait_ge(st.normed_turned, pairs * CHUNKS)
                for b in range(GROUP):
                    dve.tensor_scalar(st.normed[:, b, :], k.x[:, graph(g, b), :].rearrange("p a f -> p (a f)"),
                                      st.moments[:, b, 0:1], st.rstd[:, b:b + 1], ALU.subtract,
                                      ALU.mult).then_inc(st.normed_ready, 1)

            def start(st, pairs):
                q = pairs * STEPS
                for c in range(CHUNKS):
                    dve.wait_ge(st.h_hi, q * 2 + c + 1)
                    dve.scalar_tensor_tensor(st.hT[:, LO, c, :], st.gate_ps[:, c, :], 0.0, st.hT[:, HI, c, :],
                                             ALU.max, ALU.subtract).then_inc(st.h_lo, 1)
                for c in range(CHUNKS):
                    two = slice(2 * c, 2 * c + 2)
                    dve.wait_ge(st.rows_hi, q * 2 + c + 1)
                    dve.scalar_tensor_tensor(st.h_rows[:, LO, two], st.normed[:, two], 0.0, st.h_rows[:, HI, two],
                                             ALU.max, ALU.subtract).then_inc(st.rows_lo, 1)

            def finish(st, j, pairs):
                g = pairs * 2 + j
                for c in range(CHUNKS):
                    dve.wait_ge(st.h_turned, ((pairs + 1) * STEPS - 1) * 2 + c + 1)
                    xg = k.x[:, group(g), half(c)]
                    dve.tensor_tensor(xg, xg, bank(st, c), ALU.add).then_inc(st.x_ready, 1)

            def rows(st, q):
                for c in range(CHUNKS):
                    dve.wait_ge(st.rows_hi, q * 2 + c + 1)
                    dve.tensor_tensor(st.h_rows[:, LO, :, half(c)], bank(st, c), st.h_rows[:, HI, :, half(c)],
                                      ALU.subtract).then_inc(st.rows_lo, 1)

            def a_low(st, q):
                for c in range(CHUNKS):
                    dve.wait_ge(st.a_hi, q * 2 + c + 1)
                    dve.tensor_tensor(st.aT[:, LO, c, :], st.mix_ps[:, c, :], st.aT[:, HI, c, :],
                                      ALU.subtract).then_inc(st.a_lo, 1)

            def reset(st, q, h):
                for c in range(CHUNKS):
                    dve.wait_ge(st.r_ready, q * 2 + c + 1)
                    dve.tensor_tensor(st.r[:, c, :], st.r[:, c, :], h[:, c, :], ALU.mult).then_inc(st.rh_full, 1)
                for c in range(CHUNKS):
                    dve.wait_ge(st.rh_hi, q * 2 + c + 1)
                    dve.tensor_tensor(st.rh[:, LO, c, :], st.r[:, c, :], st.rh[:, HI, c, :],
                                      ALU.subtract).then_inc(st.rh_lo, 1)

            def update(st, q, after):
                for c in range(CHUNKS):
                    dve.wait_ge(st.new_ready, q * 2 + c + 1)
                    dve.wait_ge(st.z_ready, q * 2 + c + 1)
                    dve.tensor_tensor(st.new[:, c, :], st.new[:, c, :], st.z[:, c, :], ALU.mult).then_inc(st.scaled, 1)
                for c in range(CHUNKS):
                    dve.wait_ge(st.scaled, q * 2 + c + 1)
                    dve.wait_ge(st.kept_step, q * 4 + 2 * c + 2)
                    dve.tensor_tensor(after[:, c, :], st.kept[:, c, :], st.new[:, c, :], ALU.add).then_inc(st.h_ready, 1)

            def h_low(st, q, h):
                for c in range(CHUNKS):
                    dve.wait_ge(st.h_hi, q * 2 + c + 1)
                    dve.tensor_tensor(st.hT[:, LO, c, :], h[:, c, :], st.hT[:, HI, c, :], ALU.subtract).then_inc(st.h_lo, 1)

            for j, st in enumerate(streams):
                norm(st, j, 0)
                norm_apply(st, j, 0)
            for st in streams:
                start(st, 0)

            def body(pairs, first, last):
                for t in range(STEPS):
                    q = pairs * STEPS + t
                    before, after = t % 2, (t + 1) % 2
                    for j, st in enumerate(streams):
                        if t > 0 and j == 1:
                            rows(st, q)
                        elif t == 0 and not first:
                            finish(st, j, pairs - 1)
                            if j == 0:
                                start(streams[1], pairs)
                        a_low(st, q)
                    for j, st in enumerate(streams):
                        reset(st, q, st.h[before])
                        if t == STEPS - 1 and j == 1 and not last:
                            start(streams[0], pairs + 1)
                        if t == 0 and not last:
                            norm(st, j, pairs + 1)
                        update(st, q, st.h[after])
                        if t < STEPS - 1 and j == 1:
                            rows(streams[0], q + 1)
                        if t < STEPS - 1:
                            h_low(st, q + 1, st.h[after])
                        if t == 1 and not last:
                            norm_apply(st, j, pairs + 1)

            pipeline(dve, body)
            for j, st in enumerate(streams):
                finish(st, j, GROUPS // 2 - 1)

        @block.gpsimd
        def _(pool):
            for st in streams:
                layer_norm_rstd(pool, k, 0, st.moments_ready, st.rstd_step, st)

            def keep(st, q, h):
                for c in range(CHUNKS):
                    pool.wait_ge(st.z_ready, q * 2 + c + 1)
                    pool.wait_ge(st.h_ready, q * 2)
                    pool.tensor_tensor(st.kept[:, c, :], st.z[:, c, :], h[:, c, :], ALU.mult).then_inc(st.kept_step, 1)
                    pool.wait_ge(st.kept_step, q * 4 + 2 * c + 1)
                    pool.tensor_tensor(st.kept[:, c, :], h[:, c, :], st.kept[:, c, :], ALU.subtract).then_inc(st.kept_step, 1)

            def body(pairs, first, last):
                for t in range(STEPS):
                    for st in streams:
                        keep(st, pairs * STEPS + t, st.h[t % 2])
                        if t == 0 and not last:
                            layer_norm_rstd(pool, k, pairs + 1, st.moments_ready, st.rstd_step, st)

            pipeline(pool, body)

        @block.scalar
        def _(act):
            def start(st, pairs):
                q = pairs * STEPS
                act.wait_ge(st.kept_step, q * 4)
                for c in range(CHUNKS):
                    act.wait_ge(st.normed_turned, pairs * CHUNKS + c + 1)
                    act.activation(st.h[0][:, c, :], st.gate_ps[:, c, :], ACT.Relu).then_inc(st.first_copied, 1)
                    act.activation(st.hT[:, HI, c, :], st.gate_ps[:, c, :], ACT.Relu).then_inc(st.h_hi, 1)
                for c in range(CHUNKS):
                    act.activation(st.h_rows[:, HI, 2 * c:2 * c + 2], st.normed[:, 2 * c:2 * c + 2],
                                   ACT.Relu).then_inc(st.rows_hi, 1)

            def rows(st, q):
                for c in range(CHUNKS):
                    act.wait_ge(st.h_turned, q * 2 - 2 + c + 1)
                    act.copy(st.h_rows[:, HI, :, half(c)], bank(st, c)).then_inc(st.rows_hi, 1)

            def a_high(st, q):
                for c in range(CHUNKS):
                    act.wait_ge(st.a_ready, q * 2 + c + 1)
                    act.copy(st.aT[:, HI, c, :], st.mix_ps[:, c, :]).then_inc(st.a_hi, 1)

            def gates(st, q):
                def reset(c):
                    act.wait_ge(st.r_sum, q * 2 + c + 1)
                    act.activation(st.r[:, c, :], st.gate_ps[:, c, :], ACT.Sigmoid,
                                   bias=k.bias_r[:, c:c + 1]).then_inc(st.r_ready, 1)

                def reset_high(c):
                    act.wait_ge(st.rh_full, q * 2 + c + 1)
                    act.copy(st.rh[:, HI, c, :], st.r[:, c, :]).then_inc(st.rh_hi, 1)

                def update(c):
                    act.wait_ge(st.z_sum, q * 2 + c + 1)
                    act.activation(st.z[:, c, :], st.gate_ps[:, c, :], ACT.Sigmoid,
                                   bias=k.bias_z[:, c:c + 1]).then_inc(st.z_ready, 1)

                reset(0)
                reset(1)
                reset_high(0)
                update(0)
                reset_high(1)
                update(1)

            def candidate(st, q):
                for c in range(CHUNKS):
                    act.wait_ge(st.new_sum, q * 2 + c + 1)
                    act.activation(st.new[:, c, :], st.mix_ps[:, c, :], ACT.Tanh,
                                   bias=k.bias_h[:, c:c + 1]).then_inc(st.new_ready, 1)

            def h_high(st, q, h):
                for c in range(CHUNKS):
                    act.wait_ge(st.h_ready, q * 2 + c + 1)
                    act.copy(st.hT[:, HI, c, :], h[:, c, :]).then_inc(st.h_hi, 1)

            for st in streams:
                start(st, 0)

            def body(pairs, first, last):
                for t in range(STEPS):
                    q = pairs * STEPS + t
                    for j, st in enumerate(streams):
                        if t > 0 and j == 1:
                            rows(st, q)
                        a_high(st, q)
                    for j, st in enumerate(streams):
                        gates(st, q)
                        if t == STEPS - 1 and j == 1 and not last:
                            start(streams[0], pairs + 1)
                        candidate(st, q)
                        if t < STEPS - 1:
                            if j == 1:
                                rows(streams[0], q + 1)
                            h_high(st, q, st.h[(t + 1) % 2])
                        elif j == 1 and not last:
                            start(st, pairs + 1)

            pipeline(act, body)

        @block.tensor
        def _(pe):
            def weight(name, a, i, c):
                return k.w[:, a, SPLIT[name] + i, half(c)]

            def start(st, pairs):
                pe.wait_ge(st.normed_ready, (pairs + 1) * GROUP)
                pe.wait_ge(st.z_ready, pairs * STEPS * 2)
                for c in range(CHUNKS):
                    for b in range(GROUP):
                        last = pe.transpose(st.gate_ps[:, c, nodes(b)], st.normed[:, b, half(c)], k.identity[:])
                    last.then_inc(st.normed_turned, 1)

            def turn(st, q, h):
                for c in range(CHUNKS):
                    pe.wait_ge(st.h_ready, q * 2 - 2 + c + 1)
                    for b in range(GROUP):
                        last = pe.transpose(st.mix_ps[:, c, nodes(b)], h[:, c, nodes(b)], k.identity[:])
                    last.then_inc(st.h_turned, 1)

            def gate_from_h(st, pairs, q):
                pe.wait_ge(st.h_lo, q * 2 + 2)
                pe.wait_ge(st.first_copied, (pairs + 1) * CHUNKS)
                pe.wait_ge(st.z_ready, q * 2)
                for c in range(CHUNKS):
                    product(pe, st.gate_ps[:, c, :], lambda a, i: weight("u3", a, i, c),
                            lambda m, i: st.hT[:, m, i, :], stop=False, loose=True)

            def neighbours(st, pairs, t):
                pe.wait_ge(st.rows_lo, (pairs * STEPS + t) * 2 + 2)
                if t == 0:
                    pe.wait_ge(st.x_ready, pairs * CHUNKS)
                for c in range(CHUNKS):
                    for b in range(GROUP):
                        last = product(pe, st.mix_ps[:, c, nodes(b)], lambda a, i: st.h_rows[:, a, b, half(c)],
                                       lambda m, i: k.adjT[:, m, :], chunks=1)
                    last.then_inc(st.a_ready, 1)

            def gates_from_a(st, q):
                pe.wait_ge(st.a_lo, q * 2 + 2)
                for c in range(CHUNKS):
                    product(pe, st.gate_ps[:, c, :], lambda a, i: weight("w4", a, i, c),
                            lambda m, i: st.aT[:, m, i, :], start=False, loose=True).then_inc(st.r_sum, 1)
                for c in range(CHUNKS):
                    pe.wait_ge(st.r_ready, q * 2 + c + 1)
                    product(pe, st.gate_ps[:, c, :], lambda a, i: weight("w3", a, i, c),
                            lambda m, i: st.aT[:, m, i, :], start=False, loose=True).then_inc(st.z_sum, 1)
                for c in range(CHUNKS):
                    product(pe, st.mix_ps[:, c, :], lambda a, i: weight("w5", a, i, c),
                            lambda m, i: st.aT[:, m, i, :], stop=False, loose=True)

            def candidate(st, q):
                pe.wait_ge(st.rh_lo, q * 2 + 2)
                for c in range(CHUNKS):
                    product(pe, st.mix_ps[:, c, :], lambda a, i: weight("u5", a, i, c),
                            lambda m, i: st.rh[:, m, i, :], start=False, loose=True).then_inc(st.new_sum, 1)

            for st in streams:
                start(st, 0)

            def body(pairs, first, last):
                for t in range(STEPS):
                    q = pairs * STEPS + t
                    for st in streams:
                        if t > 0 or not first:
                            turn(st, q, st.h[t % 2 if t else STEPS % 2])
                        gate_from_h(st, pairs, q)
                        neighbours(st, pairs, t)
                    for st in streams:
                        gates_from_a(st, q)
                        candidate(st, q)
                        if t == STEPS - 1 and not last:
                            start(st, pairs + 1)

            pipeline(pe, body)
            for st in streams:
                turn(st, GROUPS // 2 * STEPS, st.h[STEPS % 2])


def conv_layer(nc, sem, dram, k):
    with ExitStack() as ctx:
        def sb(name, shape, dt=F32):
            return ctx.enter_context(nc.sbuf_tensor("conv_" + name, shape, dt))

        def ps(name, shape):
            return ctx.enter_context(nc.psum_tensor("conv_" + name, shape, F32))

        class s:
            settled = sem("conv_settled")
            stats = sb("stats", [P, GROUP, 6])
            moments = sb("moments", [P, GROUP, 2])
            var_eps = sb("var_eps", [P, GROUP])
            rstd = sb("rstd", [P, GROUP])
        normed = sb("normed", [P, GROUP, FEATURES])
        h_rows = sb("h_rows", [P, 2, GROUP, FEATURES], F16)
        aT = sb("aT", [P, 2, CHUNKS, TOKENS], F16)
        a_ps = ps("a_ps", [P, CHUNKS, TOKENS])
        y_ps = ps("y_ps", [P, GROUP, FEATURES])

        moments_ready = sem("conv_moments_ready")
        rstd_step = sem("conv_rstd_step")
        normed_ready = sem("conv_normed_ready")
        rows_hi = sem("conv_rows_hi")
        rows_lo = sem("conv_rows_lo")
        x_biased = sem("conv_x_biased")
        a_ready = sem("conv_a_ready")
        a_hi = sem("conv_a_hi")
        a_lo = sem("conv_a_lo")
        y_ready = sem("conv_y_ready")
        x_ready = sem("conv_x_ready")
        stored = sem("conv_stored")
        block = ctx.enter_context(nc.Block())

        def pipeline(eng, body):
            body(0, None, None)
            body(1, 0, None)
            body(2, 1, 0)
            with eng.Fori(3, GROUPS) as i:
                body(i, i - 1, i - 2)
            body(None, GROUPS - 1, GROUPS - 2)
            body(None, None, GROUPS - 1)

        def nodes(b):
            return slice(b * NODES, (b + 1) * NODES)

        @block.sync
        def _(sp):
            view = dram["out"].rearrange("b n d -> n b d")

            def body(front, mid, back):
                if back is not None:
                    sp.wait_ge(x_ready, (back + 1) * 2)
                    if not isinstance(back, int) or back > 0:
                        sp.wait_ge(stored, back * 16)
                    sp.dma_start(view[:, group(back), :], k.x[:, group(back), :]).then_inc(stored, 16)

            pipeline(sp, body)
            sp.wait_ge(stored, GROUPS * 16)

        @block.vector
        def _(dve):
            def body(front, mid, back):
                if front is not None:
                    dve.wait_ge(rstd_step, front * 2)
                    layer_norm_stats(dve, k, front, moments_ready, s)
                if mid is not None:
                    for c in range(CHUNKS):
                        dve.wait_ge(a_hi, mid * CHUNKS + c + 1)
                        dve.tensor_tensor(aT[:, LO, c, :], a_ps[:, c, :], aT[:, HI, c, :], ALU.subtract).then_inc(a_lo, 1)
                if front is not None:
                    dve.wait_ge(rstd_step, (front + 1) * 2)
                    dve.wait_ge(rows_lo, front)
                    for b in range(GROUP):
                        dve.tensor_scalar(normed[:, b, :], k.x[:, graph(front, b), :].rearrange("p a f -> p (a f)"),
                                          s.moments[:, b, 0:1], s.rstd[:, b:b + 1], ALU.subtract,
                                          ALU.mult).then_inc(normed_ready, 1)
                if back is not None:
                    dve.wait_ge(x_biased, back + 1)
                    for j in range(2):
                        dve.wait_ge(y_ready, back * 2 + j + 1)
                        xh = k.x[:, bass.ds(back * GROUP + 2 * j, 2), :]
                        dve.tensor_tensor(xh, xh, y_ps[:, 2 * j:2 * j + 2, :], ALU.add).then_inc(x_ready, 1)
                if front is not None:
                    dve.wait_ge(rows_hi, front + 1)
                    dve.scalar_tensor_tensor(h_rows[:, LO], normed[:], 0.0, h_rows[:, HI], ALU.max,
                                             ALU.subtract).then_inc(rows_lo, 1)

            pipeline(dve, body)

        @block.gpsimd
        def _(pool):
            def body(front, mid, back):
                if front is not None:
                    layer_norm_rstd(pool, k, front, moments_ready, rstd_step, s)
                    pool.wait_ge(normed_ready, (front + 1) * GROUP)
                    settle(pool, s)
                    pool.tensor_tensor(k.x[:, group(front), :], k.x[:, group(front), :],
                                       k.conv_bias[:].broadcast_to([P, GROUP, FEATURES]), ALU.add).then_inc(x_biased, 1)

            pipeline(pool, body)

        @block.scalar
        def _(act):
            def body(front, mid, back):
                if mid is not None:
                    act.wait_ge(y_ready, mid * 2)
                    for c in range(CHUNKS):
                        act.wait_ge(a_ready, mid * CHUNKS + c + 1)
                        act.copy(aT[:, HI, c, :], a_ps[:, c, :]).then_inc(a_hi, 1)
                if front is not None:
                    act.wait_ge(normed_ready, (front + 1) * GROUP)
                    act.wait_ge(a_ready, front * CHUNKS)
                    act.activation(h_rows[:, HI], normed[:], ACT.Relu).then_inc(rows_hi, 1)

            pipeline(act, body)

        @block.tensor
        def _(pe):
            def body(front, mid, back):
                if back is not None:
                    pe.wait_ge(a_lo, (back + 1) * CHUNKS)
                    pe.wait_ge(x_ready, back * 2)
                    for b in range(GROUP):
                        last = product(pe, y_ps[:, b, :], lambda a, c: aT[:, a, c, nodes(b)],
                                       lambda m, c: k.w[:, m, SPLIT["conv"] + c, :])
                        if b % 2:
                            last.then_inc(y_ready, 1)
                if mid is not None:
                    pe.wait_ge(rows_lo, mid + 1)
                    pe.wait_ge(a_lo, mid * CHUNKS)
                    for c in range(CHUNKS):
                        for b in range(GROUP):
                            last = product(pe, a_ps[:, c, nodes(b)], lambda a, i: h_rows[:, a, b, c * P:(c + 1) * P],
                                           lambda m, i: k.adjT[:, m, :], chunks=1)
                        last.then_inc(a_ready, 1)

            pipeline(pe, body)


def build(nc, dram, out):
    dram = dict(dram, out=out)
    with ExitStack() as ctx:
        def sb(name, shape, dt=F32):
            return ctx.enter_context(nc.sbuf_tensor(name, shape, dt))

        def sem(name):
            return ctx.enter_context(nc.semaphore(name))

        class k:
            x = sb("x_res", [P, GRAPHS, FEATURES])
            w = sb("w_split", [P, 2, SPLIT_SLOTS, FEATURES], F16)
            identity = sb("identity", [P, P])
            adjT = sb("adjT", [P, 2, NODES], F16)
            mask = sb("mask", [P, 1, NODES])
            mask_bias = sb("mask_bias", [P, 1, NODES])
            attn_vecs = sb("attn_vecs", [P, 2, 2, CHUNKS, P], F16)
            bias_q = sb("bias_q", [P, CHUNKS])
            bias_k = sb("bias_k", [P, CHUNKS])
            bias_z = sb("bias_z", [P, CHUNKS])
            bias_r = sb("bias_r", [P, CHUNKS])
            bias_h = sb("bias_h", [P, CHUNKS])
            attn_bias = sb("attn_bias", [P, 1, FEATURES])
            conv_bias = sb("conv_bias", [P, 1, FEATURES])
            beta = sb("beta", [P, 1])
            eps = sb("eps", [P, GROUP])
            minus_half = sb("minus_half", [P, GROUP])
            minus_one = sb("minus_one", [P, GROUP])

        load_constants(nc, sem, dram, k)
        for layer in (gat_layer, attention_layer, gated_layer, conv_layer):
            layer(nc, sem, dram, k)


def kernel(**inputs):
    import numpy as np
    import concourse.bacc as bacc
    from concourse.bass_utils import run_bass_kernel_spmd

    f32 = {name: np.asarray(a, dtype=np.float32) for name, a in inputs.items()}

    def tile_rows(v):
        return np.broadcast_to(v.reshape(1, -1), (P, v.size))

    def column(v):
        return v.reshape(CHUNKS, P).T

    a = f32["L0_gnn_a"].reshape(2, FEATURES)
    arrays = {
        "x": f32["x"],
        "weights": np.concatenate([
            f32["L0_gnn_W"], f32["L1_gnn_Wq"], f32["L1_gnn_Wk"], f32["L1_gnn_Wv"], f32["L1_gnn_Wo"],
            f32["L2_gnn_w3_w"].T, f32["L2_gnn_w4_w"].T, f32["L2_gnn_w5_w"].T, f32["L2_gnn_u3_w"].T,
            f32["L2_gnn_u5_w"].T, f32["L3_gnn_weight"]], axis=0),
        "cols": np.concatenate([column(v) for v in (
            a[0], a[1], f32["L1_gnn_bq"], f32["L1_gnn_bk"], f32["L1_gnn_bv"], f32["L2_gnn_w3_b"],
            f32["L2_gnn_u3_b"], f32["L2_gnn_w4_b"], f32["L2_gnn_w5_b"], f32["L2_gnn_u5_b"])], axis=1),
        "rows": np.stack([tile_rows(v) for v in (a[0], a[1], f32["L1_gnn_bo"], f32["L3_gnn_bias"])], axis=1),
        "adj": np.stack([f32["adj"], f32["adj"].T], axis=1),
        "identity": np.eye(P, dtype=np.float32),
        "beta": np.broadcast_to(f32["L0_gnn_beta"].reshape(1, 1), (P, 1)),
    }
    arrays = {name: np.ascontiguousarray(v) for name, v in arrays.items()}

    nc = bacc.Bacc("TRN2", target_bir_lowering=False, num_devices=1)
    dram = {name: nc.dram_tensor("in_" + name, v.shape, F32, kind="ExternalInput").ap() for name, v in arrays.items()}
    out = nc.dram_tensor("out_0", (GRAPHS, NODES, FEATURES), F32, kind="ExternalOutput").ap()
    build(nc, dram, out)
    result = run_bass_kernel_spmd(nc, [{"in_" + name: v for name, v in arrays.items()}], core_ids=[0])
    return result.results[0]["out_0"]
```

```python
from contextlib import ExitStack

import concourse.bass as bass
from concourse import mybir

F32 = mybir.dt.float32
F16 = mybir.dt.float16
ALU = mybir.AluOpType
ACT = mybir.ActivationFunctionType
AX = mybir.AxisListType.X

GRAPHS, NODES, FEATURES = 64, 128, 256
P = 128
CHUNKS = FEATURES // P
GROUP = 4
GROUPS = GRAPHS // GROUP
TOKENS = GROUP * NODES
HEADS = 8
HEAD = FEATURES // HEADS
LN_EPS = 1e-5
MASKED = -1e9
LEAK = 0.2
STEPS = 3

RAW = {"gat": 0, "q": 2, "k": 4, "v": 6, "o": 8, "w3": 10, "w4": 14, "w5": 18, "u3": 22, "u5": 24, "conv": 26}
RAW_SLOTS = 28
SPLIT = {"gat": 0, "q": 2, "k": 4, "v": 6, "o": 8, "conv": 10, "u3": 12, "u5": 14, "w4": 16, "w5": 18, "w3": 20}
SPLIT_SLOTS = 22
COLS = {"bq": 0, "bk": 2, "bv": 4, "w3b": 6, "u3b": 8, "w4b": 10, "w5b": 12, "u5b": 14}
COL_SLOTS = 16
ROWS = {"a1": 0, "a2": 1, "bo": 2, "conv_bias": 3}

HI, LO = 0, 1
PARTS = ((HI, HI), (HI, LO), (LO, HI))


def product(pe, out, stationary, moving, chunks=CHUNKS, start=True, stop=True, loose=False):
    last = None
    for c in range(chunks):
        for n, (a, b) in enumerate(PARTS):
            last = pe.matmul(out, stationary(a, c), moving(b, c),
                             start=start and c == 0 and n == 0,
                             stop=stop and c == chunks - 1 and n == len(PARTS) - 1,
                             skip_group_check=loose)
    return last


def graph(g, b):
    return bass.ds(g * GROUP + b, 1)


def group(g):
    return bass.ds(g * GROUP, GROUP)


def load_constants(nc, sem, dram, k):
    with ExitStack() as ctx:
        def sb(name, shape, dt=F32):
            return ctx.enter_context(nc.sbuf_tensor(name, shape, dt))

        raw = sb("raw_weights", [P, RAW_SLOTS, FEATURES])
        cols = sb("cols", [P, COL_SLOTS])
        rows = sb("rows", [P, 4, FEATURES])
        adj = sb("adj_raw", [P, 2, NODES])
        summed = sb("summed", [P, 3, CHUNKS, FEATURES])
        attn_vec = sb("attn_vec", [P, 2, CHUNKS])
        scratch = sb("scratch", [P, 2, CHUNKS, FEATURES])
        spread = sb("spread", [P, 3, CHUNKS, P])
        bv_split = sb("bv_split", [P, 2, CHUNKS, P], F16)
        crow = ctx.enter_context(nc.psum_tensor("crow", [P, FEATURES], F32))

        small_in = sem("small_in")
        gat_in = sem("gat_in")
        weights_in = sem("weights_in")
        done = sem("setup_done")
        plain_hi = sem("plain_hi")
        plain_lo = sem("plain_lo")
        summed_ready = sem("summed_ready")
        summed_hi = sem("summed_hi")
        summed_lo = sem("summed_lo")
        split = sem("bv_split_ready")
        crow_ready = sem("crow_ready")
        block = ctx.enter_context(nc.Block())
        PLAIN = ("o", "q", "k", "v", "u3", "u5", "conv")
        SUMMED = ("w4", "w5", "w3")

        @block.sync
        def _(sp):
            view = dram["weights"].rearrange("(k p) f -> p k f", p=P)
            sp.dma_start(raw[:, 0:2, :], view[:, 0:2, :]).then_inc(gat_in, 16)
            sp.dma_start(cols[:], dram["cols"]).then_inc(small_in, 16)
            sp.dma_start(rows[:], dram["rows"]).then_inc(small_in, 16)
            sp.dma_start(adj[:], dram["adj"]).then_inc(small_in, 16)
            sp.dma_start(k.identity[:], dram["identity"]).then_inc(small_in, 16)
            sp.dma_start(k.beta[:], dram["beta"]).then_inc(small_in, 16)
            sp.dma_start(raw[:, 2:RAW_SLOTS, :], view[:, 2:RAW_SLOTS, :]).then_inc(weights_in, 16)
            sp.dma_start(k.x[:, group(0), :], dram["x"].rearrange("b n d -> n b d")[:, group(0), :]).then_inc(k.x_in, 16)

        @block.vector
        def _(dve):
            n = [0]

            def step(ins):
                n[0] += 1
                ins.then_inc(done, 1)
                dve.wait_ge(done, n[0])

            def split_of(hi, lo, full):
                step(dve.tensor_copy(hi, full))
                step(dve.tensor_tensor(lo, full, hi, ALU.subtract))

            step(dve.memset(k.eps[:], LN_EPS))
            step(dve.memset(k.minus_half[:], -0.5))
            step(dve.memset(k.minus_one[:], -1.0))
            dve.wait_ge(small_in, 16 * 5)
            step(dve.tensor_copy(k.mask[:, 0, :], adj[:, 0, :]))
            split_of(k.adjT[:, HI, :], k.adjT[:, LO, :], adj[:, 1, :])
            step(dve.tensor_scalar(k.mask_bias[:, 0, :], adj[:, 0, :], -1.0, 1.0, ALU.mult, ALU.add))
            step(dve.tensor_scalar(k.mask_bias[:, 0, :], k.mask_bias[:, 0, :], MASKED, None, ALU.mult))
            dve.wait_ge(gat_in, 16)
            for v in range(2):
                for c in range(CHUNKS):
                    step(dve.tensor_tensor(scratch[:, v, c, :], raw[:, c, :], rows[:, ROWS["a1"] + v, :], ALU.mult))
                    step(dve.reduce_sum(attn_vec[:, v, c:c + 1], scratch[:, v, c, :], AX))
                    step(dve.tensor_copy(spread[:, v, c, :], attn_vec[:, v, c:c + 1].broadcast_to([P, P])))
                    split_of(k.attn_vecs[:, HI, v, c, :], k.attn_vecs[:, LO, v, c, :], spread[:, v, c, :])
            split_of(k.w[:, HI, 0:2, :], k.w[:, LO, 0:2, :], raw[:, 0:2, :])
            for n_plain, name in enumerate(PLAIN):
                dve.wait_ge(plain_hi, n_plain + 1)
                dve.tensor_tensor(k.w[:, LO, SPLIT[name]:SPLIT[name] + 2, :], raw[:, RAW[name]:RAW[name] + 2, :],
                                  k.w[:, HI, SPLIT[name]:SPLIT[name] + 2, :], ALU.subtract).then_inc(plain_lo, 1)
            dve.wait_ge(plain_lo, len(PLAIN))
            for c in range(CHUNKS):
                step(dve.tensor_copy(spread[:, 2, c, :], cols[:, COLS["bv"] + c:COLS["bv"] + c + 1].broadcast_to([P, P])))
            step(dve.tensor_copy(bv_split[:, HI], spread[:, 2]))
            step(dve.tensor_tensor(bv_split[:, LO], spread[:, 2], bv_split[:, HI], ALU.subtract))
            dve.engine_nop().then_inc(split, 1)
            step(dve.tensor_copy(k.bias_q[:], cols[:, COLS["bq"]:COLS["bq"] + 2]))
            step(dve.tensor_copy(k.bias_k[:], cols[:, COLS["bk"]:COLS["bk"] + 2]))
            for out, first, second in ((k.bias_z, "w3b", "u3b"), (k.bias_r, "w4b", "u3b"), (k.bias_h, "w5b", "u5b")):
                step(dve.tensor_tensor(out[:], cols[:, COLS[first]:COLS[first] + 2],
                                       cols[:, COLS[second]:COLS[second] + 2], ALU.add))
            step(dve.tensor_copy(k.conv_bias[:, 0, :], rows[:, ROWS["conv_bias"], :]))
            dve.wait_ge(crow_ready, 1)
            step(dve.tensor_tensor(k.attn_bias[:, 0, :], crow[:], rows[:, ROWS["bo"], :], ALU.add))

        @block.gpsimd
        def _(pool):
            pool.wait_ge(weights_in, 16)
            for j, name in enumerate(SUMMED):
                a = RAW[name]
                pool.tensor_tensor(summed[:, j], raw[:, a:a + 2, :], raw[:, a + 2:a + 4, :], ALU.add).then_inc(summed_ready, 1)
            pool.wait_ge(summed_ready, 3)
            pool.tensor_tensor(summed[:, 2], summed[:, 2], summed[:, 0], ALU.subtract).then_inc(summed_ready, 1)
            for j, name in enumerate(SUMMED):
                b = SPLIT[name]
                pool.wait_ge(summed_hi, j + 1)
                pool.tensor_tensor(k.w[:, LO, b:b + 2, :], summed[:, j], k.w[:, HI, b:b + 2, :],
                                   ALU.subtract).then_inc(summed_lo, 1)

        @block.scalar
        def _(act):
            act.wait_ge(weights_in, 16)
            for name in PLAIN:
                a, b = RAW[name], SPLIT[name]
                act.copy(k.w[:, HI, b:b + 2, :], raw[:, a:a + 2, :]).then_inc(plain_hi, 1)
            for j, name in enumerate(SUMMED):
                act.wait_ge(summed_ready, (1, 2, 4)[j])
                act.copy(k.w[:, HI, SPLIT[name]:SPLIT[name] + 2, :], summed[:, j]).then_inc(summed_hi, 1)

        @block.tensor
        def _(pe):
            pe.wait_ge(split, 1)
            product(pe, crow[:], lambda a, c: bv_split[:, a, c, :],
                    lambda b, c: k.w[:, b, SPLIT["o"] + c, :]).then_inc(crow_ready, 1)


def settle(eng, s):
    eng.sem_inc(s.settled, 1)


def layer_norm_stats(dve, k, g, ready, s):
    for b in range(GROUP):
        dve.bn_stats(s.stats[:, b, :], k.x[:, graph(g, b), :].rearrange("p a f -> p (a f)")).then_inc(ready, 1)
    dve.wait_ge(ready, (g * 2 + 1) * GROUP)
    settle(dve, s)
    for b in range(GROUP):
        dve.bn_aggr(s.moments[:, b, :], s.stats[:, b, :]).then_inc(ready, 1)


def layer_norm_rstd(pool, k, g, moments_ready, pool_step, s):
    pool.wait_ge(moments_ready, (g + 1) * 2 * GROUP)
    pool.tensor_tensor(s.var_eps[:], s.moments[:, :, 1], k.eps[:], ALU.add).then_inc(pool_step, 1)
    pool.wait_ge(pool_step, g * 2 + 1)
    pool.tensor_tensor(s.rstd[:], s.var_eps[:], k.minus_half[:], ALU.pow).then_inc(pool_step, 1)


def layer_norm_shift(pool, k, g, rstd_step, shift_step, neg_mean, s):
    pool.tensor_tensor(neg_mean[:], s.moments[:, :, 0], k.minus_one[:], ALU.mult).then_inc(shift_step, 1)
    pool.wait_ge(rstd_step, (g + 1) * 2)
    pool.wait_ge(shift_step, g * 2 + 1)
    pool.tensor_tensor(neg_mean[:], neg_mean[:], s.rstd[:], ALU.mult).then_inc(shift_step, 1)


def gat_layer(nc, sem, dram, k):
    with ExitStack() as ctx:
        def sb(name, shape, dt=F32):
            return ctx.enter_context(nc.sbuf_tensor("gat_" + name, shape, dt))

        def ps(name, shape):
            return ctx.enter_context(nc.psum_tensor("gat_" + name, shape, F32))

        class s:
            settled = sem("gat_settled")
            stats = sb("stats", [P, GROUP, 6])
            moments = sb("moments", [P, GROUP, 2])
            var_eps = sb("var_eps", [P, GROUP])
            rstd = sb("rstd", [P, GROUP])
        normed = sb("normed", [P, GROUP, FEATURES])
        neg_mean = sb("neg_mean", [P, GROUP])
        hT = [sb(f"hT{j}", [P, 2, CHUNKS, TOKENS], F16) for j in range(2)]
        wh = sb("wh", [P, 2, GROUP, FEATURES], F16)
        beta_wh = sb("beta_wh", [P, GROUP, FEATURES])
        e_raw = sb("e_raw", [P, GROUP, NODES])
        e_leaky = sb("e_leaky", [P, GROUP, NODES])
        row_max = sb("row_max", [P, GROUP, 1])
        prob = sb("prob", [P, GROUP, NODES])
        row_sum = sb("row_sum", [P, GROUP])
        inv_sum = sb("inv_sum", [P, GROUP])
        probT = sb("probT", [P, 2, GROUP, NODES], F16)
        y = sb("y", [P, GROUP, FEATURES])
        y_neg = sb("y_neg", [P, GROUP, FEATURES])
        y_exp = sb("y_exp", [P, GROUP, FEATURES])

        hT_ps = ps("hT_ps", [P, CHUNKS, TOKENS])
        e_ps = ps("e_ps", [P, GROUP, NODES])
        wh_ps = ps("wh_ps", [P, GROUP, FEATURES])
        probT_ps = ps("probT_ps", [P, GROUP, NODES])
        att_ps = ps("att_ps", [P, GROUP, FEATURES])

        x_in = k.x_in
        moments_ready = sem("gat_moments_ready")
        rstd_step = sem("gat_rstd_step")
        shift_step = sem("gat_shift_step")
        normed_ready = sem("gat_normed_ready")
        hT_turned = sem("gat_hT_turned")
        hT_hi = sem("gat_hT_hi")
        hT_lo = sem("gat_hT_lo")
        e_ready = sem("gat_e_ready")
        e_copied = sem("gat_e_copied")
        leaky_ready = sem("gat_leaky_ready")
        masked_ready = sem("gat_masked_ready")
        max_ready = sem("gat_max_ready")
        shifted_ready = sem("gat_shifted_ready")
        prob_ready = sem("gat_prob_ready")
        sum_step = sem("gat_sum_step")
        wh_ready = sem("gat_wh_ready")
        wh_hi = sem("gat_wh_hi")
        beta_wh_ready = sem("gat_beta_wh_ready")
        wh_lo = sem("gat_wh_lo")
        probT_turned = sem("gat_probT_turned")
        probT_hi = sem("gat_probT_hi")
        probT_lo = sem("gat_probT_lo")
        att_ready = sem("gat_att_ready")
        y_ready = sem("gat_y_ready")
        y_neg_ready = sem("gat_y_neg_ready")
        y_exp_ready = sem("gat_y_exp_ready")
        y_pos_ready = sem("gat_y_pos_ready")
        x_step = sem("gat_x_step")
        block = ctx.enter_context(nc.Block())

        def pipeline(eng, body):
            def step(i, j):
                body(i, i - 1, i - 2, i - 3, i - 4, j)
            body(0, None, None, None, None, 1)
            body(1, 0, None, None, None, 0)
            body(2, 1, 0, None, None, 1)
            body(3, 2, 1, 0, None, 0)
            step(4, 1)
            step(5, 0)
            with eng.Fori(3, GROUPS // 2) as pairs:
                step(pairs * 2, 1)
                step(pairs * 2 + 1, 0)
            n = GROUPS
            body(None, n - 1, n - 2, n - 3, n - 4, 1)
            body(None, None, n - 1, n - 2, n - 3, 0)
            body(None, None, None, n - 1, n - 2, 1)
            body(None, None, None, None, n - 1, 0)

        def later(g):
            return not isinstance(g, int) or g > 0

        @block.sync
        def _(sp):
            x_view = dram["x"].rearrange("b n d -> n b d")
            with sp.Fori(1, GROUPS) as g:
                sp.wait_ge(x_in, g * 16)
                sp.dma_start(k.x[:, group(g), :], x_view[:, group(g), :]).then_inc(x_in, 16)
            sp.wait_ge(x_in, GROUPS * 16)

        @block.vector
        def _(dve):
            def wh_low(mid, i):
                dve.wait_ge(wh_hi, mid * 2 + (i + 1))
                h = slice(2 * i, 2 * i + 2)
                dve.tensor_tensor(wh[:, LO, h, :], wh_ps[:, h, :], wh[:, HI, h, :], ALU.subtract).then_inc(wh_lo, 1)

            def body(ahead, norm, front, mid, back, j):
                if mid is not None:
                    dve.wait_ge(e_copied, mid + 1)
                    dve.wait_ge(prob_ready, mid)
                    dve.scalar_tensor_tensor(e_leaky[:], e_raw[:], LEAK, e_raw[:], ALU.mult,
                                             ALU.max).then_inc(leaky_ready, 1)
                if back is not None:
                    dve.wait_ge(probT_hi, back + 1)
                    if later(back):
                        dve.wait_ge(att_ready, back * 2)
                    dve.tensor_tensor(probT[:, LO], probT_ps[:], probT[:, HI], ALU.subtract).then_inc(probT_lo, 1)
                if mid is not None:
                    dve.wait_ge(leaky_ready, mid + 1)
                    dve.tensor_tensor(e_leaky[:], e_leaky[:], k.mask[:].broadcast_to([P, GROUP, NODES]),
                                      ALU.mult).then_inc(masked_ready, 1)
                    dve.wait_ge(masked_ready, mid + 1)
                    dve.wait_ge(shifted_ready, mid)
                    dve.reduce_max(row_max[:, :, 0], e_leaky[:], AX).then_inc(max_ready, 1)
                if back is not None:
                    dve.wait_ge(prob_ready, back + 1)
                    dve.reduce_sum(row_sum[:], prob[:], AX).then_inc(sum_step, 1)
                    dve.wait_ge(sum_step, back * 2 + 1)
                    dve.wait_ge(y_ready, back * GROUP)
                    dve.reciprocal(inv_sum[:], row_sum[:]).then_inc(sum_step, 1)
                if back is not None:
                    dve.wait_ge(y_neg_ready, back)
                    dve.wait_ge(y_pos_ready, back)
                    if later(back):
                        dve.wait_ge(x_step, back * 2 - 1)
                    dve.wait_ge(beta_wh_ready, (back + 1) * 2)
                    dve.wait_ge(sum_step, (back + 1) * 2)
                    for b in range(GROUP):
                        if b % 2 == 0:
                            dve.wait_ge(att_ready, back * 2 + (b // 2 + 1))
                        dve.scalar_tensor_tensor(y[:, b, :], att_ps[:, b, :], inv_sum[:, b:b + 1], beta_wh[:, b, :],
                                                 ALU.mult, ALU.add).then_inc(y_ready, 1)
                if front is not None:
                    for c in range(CHUNKS):
                        dve.wait_ge(hT_hi, front * CHUNKS + (c + 1))
                        dve.scalar_tensor_tensor(hT[1 - j][:, LO, c, :], hT_ps[:, c, :], 0.0, hT[1 - j][:, HI, c, :],
                                                 ALU.max, ALU.subtract).then_inc(hT_lo, 1)
                if mid is not None:
                    wh_low(mid, 0)
                if ahead is not None:
                    dve.wait_ge(x_in, (ahead + 1) * 16)
                    dve.wait_ge(shift_step, ahead * 2)
                    layer_norm_stats(dve, k, ahead, moments_ready, s)
                if back is not None:
                    dve.wait_ge(y_neg_ready, back + 1)
                    dve.tensor_scalar(y[:], y[:], 0.0, -1.0, ALU.max, ALU.add).then_inc(y_pos_ready, 1)
                if mid is not None:
                    wh_low(mid, 1)

            pipeline(dve, body)

        @block.gpsimd
        def _(pool):
            def add_exp(g):
                pool.wait_ge(x_step, g * 2 + 1)
                pool.wait_ge(y_exp_ready, g + 1)
                settle(pool, s)
                pool.tensor_tensor(k.x[:, group(g), :], k.x[:, group(g), :], y_exp[:], ALU.add).then_inc(x_step, 1)

            def body(ahead, norm, front, mid, back, j):
                if mid is not None:
                    pool.wait_ge(max_ready, mid + 1)
                    pool.tensor_tensor(e_leaky[:], e_leaky[:], row_max[:].broadcast_to([P, GROUP, NODES]),
                                       ALU.subtract).then_inc(shifted_ready, 1)
                if back is not None and later(back):
                    add_exp(back - 1)
                if ahead is not None:
                    pool.wait_ge(normed_ready, ahead * GROUP)
                    layer_norm_rstd(pool, k, ahead, moments_ready, rstd_step, s)
                    layer_norm_shift(pool, k, ahead, rstd_step, shift_step, neg_mean, s)
                if back is not None:
                    pool.wait_ge(y_pos_ready, back + 1)
                    settle(pool, s)
                    pool.tensor_tensor(k.x[:, group(back), :], k.x[:, group(back), :], y[:], ALU.add).then_inc(x_step, 1)

            pipeline(pool, body)
            add_exp(GROUPS - 1)

        @block.scalar
        def _(act):
            def wh_parts(mid, back, i):
                h = slice(2 * i, 2 * i + 2)
                act.wait_ge(wh_ready, mid * 2 + (i + 1))
                if back is not None:
                    act.wait_ge(y_ready, (back + 1) * GROUP)
                    act.wait_ge(att_ready, (back + 1) * 2)
                act.activation(beta_wh[:, h, :], wh_ps[:, h, :], ACT.Identity,
                               scale=k.beta[:, 0:1]).then_inc(beta_wh_ready, 1)
                act.copy(wh[:, HI, h, :], wh_ps[:, h, :]).then_inc(wh_hi, 1)

            def body(ahead, norm, front, mid, back, j):
                if mid is not None:
                    act.wait_ge(e_ready, mid + 1)
                    act.wait_ge(leaky_ready, mid)
                    act.copy(e_raw[:], e_ps[:]).then_inc(e_copied, 1)
                if back is not None:
                    act.wait_ge(probT_turned, back + 1)
                    act.wait_ge(att_ready, back * 2)
                    act.copy(probT[:, HI], probT_ps[:]).then_inc(probT_hi, 1)
                if front is not None:
                    if not isinstance(front, int) or front >= 2:
                        act.wait_ge(wh_ready, (front - 1) * 2)
                    for c in range(CHUNKS):
                        act.wait_ge(hT_turned, front * CHUNKS + (c + 1))
                        act.activation(hT[1 - j][:, HI, c, :], hT_ps[:, c, :], ACT.Relu).then_inc(hT_hi, 1)
                if norm is not None:
                    act.wait_ge(shift_step, (norm + 1) * 2)
                    act.wait_ge(x_in, (norm + 1) * 16)
                    act.wait_ge(hT_turned, norm * CHUNKS)
                    for b in range(GROUP):
                        act.activation(normed[:, b, :], k.x[:, graph(norm, b), :].rearrange("p a f -> p (a f)"),
                                       ACT.Identity, scale=s.rstd[:, b:b + 1],
                                       bias=neg_mean[:, b:b + 1]).then_inc(normed_ready, 1)
                if mid is not None:
                    act.wait_ge(shifted_ready, mid + 1)
                    act.wait_ge(probT_turned, mid)
                    act.wait_ge(sum_step, mid * 2)
                    act.activation(prob[:], e_leaky[:], ACT.Exp).then_inc(prob_ready, 1)
                    wh_parts(mid, back, 0)
                if back is not None:
                    act.wait_ge(y_ready, (back + 1) * GROUP)
                    act.wait_ge(y_exp_ready, back)
                    act.activation(y_neg[:], y[:], ACT.Relu, scale=-1.0).then_inc(y_neg_ready, 1)
                if mid is not None:
                    wh_parts(mid, back, 1)
                if back is not None:
                    act.wait_ge(y_neg_ready, back + 1)
                    act.wait_ge(x_step, back * 2)
                    act.activation(y_exp[:], y_neg[:], ACT.Exp, scale=-1.0).then_inc(y_exp_ready, 1)

            pipeline(act, body)

        @block.tensor
        def _(pe):
            def nodes(b):
                return slice(b * NODES, (b + 1) * NODES)

            def body(ahead, norm, front, mid, back, j):
                if mid is not None:
                    pe.wait_ge(hT_lo, (mid + 1) * CHUNKS)
                    pe.wait_ge(e_copied, mid)
                    product(pe, e_ps[:].rearrange("p b n -> p (b n)"), lambda a, c: k.attn_vecs[:, a, 1, c, :],
                            lambda b, c: hT[j][:, b, c, :], stop=False, loose=True)
                    for b in range(GROUP):
                        last = product(pe, e_ps[:, b, :], lambda a, c: hT[j][:, a, c, nodes(b)],
                                       lambda m, c: k.attn_vecs[:, m, 0, c, :], start=False, loose=True)
                    last.then_inc(e_ready, 1)
                if back is not None:
                    pe.wait_ge(prob_ready, back + 1)
                    pe.wait_ge(probT_lo, back)
                    for b in range(GROUP):
                        last = pe.transpose(probT_ps[:, b, :], prob[:, b, :], k.identity[:])
                    last.then_inc(probT_turned, 1)
                if front is not None:
                    pe.wait_ge(normed_ready, (front + 1) * GROUP)
                    pe.wait_ge(hT_lo, front * CHUNKS)
                    for c in range(CHUNKS):
                        for b in range(GROUP):
                            last = pe.transpose(hT_ps[:, c, nodes(b)], normed[:, b, c * P:(c + 1) * P], k.identity[:])
                        last.then_inc(hT_turned, 1)
                if back is not None:
                    pe.wait_ge(probT_lo, back + 1)
                    pe.wait_ge(wh_lo, (back + 1) * 2)
                    pe.wait_ge(y_ready, back * GROUP)
                    for b in range(GROUP):
                        last = product(pe, att_ps[:, b, :], lambda a, c: probT[:, a, b, :],
                                       lambda m, c: wh[:, m, b, :], chunks=1)
                        if b % 2:
                            last.then_inc(att_ready, 1)
                if mid is not None:
                    pe.wait_ge(wh_lo, mid * 2)
                    for b in range(GROUP):
                        last = product(pe, wh_ps[:, b, :], lambda a, c: hT[j][:, a, c, nodes(b)],
                                       lambda m, c: k.w[:, m, SPLIT["gat"] + c, :])
                        if b % 2:
                            last.then_inc(wh_ready, 1)

            pipeline(pe, body)


class Group:
    def __init__(self, pairs, j):
        self.pairs, self.j = pairs, j
        self.index, self.parity = pairs * 2 + j, j % 2
        self.same = pairs + (j // 2 + 1)

    def before(self):
        return Group(self.pairs, self.j - 1)

    def exists(self, back):
        return not isinstance(self.index, int) or self.index >= back


def attention_layer(nc, sem, dram, k):
    with ExitStack() as ctx:
        def sb(name, shape, dt=F32):
            return ctx.enter_context(nc.sbuf_tensor("att_" + name, shape, dt))

        def ps(name, shape):
            return ctx.enter_context(nc.psum_tensor("att_" + name, shape, F32))

        class s:
            settled = sem("att_settled")
            stats = sb("stats", [P, GROUP, 6])
            moments = sb("moments", [P, GROUP, 2])
            var_eps = sb("var_eps", [P, GROUP])
            rstd = sb("rstd", [P, GROUP])
        normed = sb("normed", [P, GROUP, FEATURES])
        hT = sb("hT", [P, 2, CHUNKS, TOKENS], F16)
        neg_mean = sb("neg_mean", [P, GROUP])
        q_full = sb("q_full", [P, CHUNKS, TOKENS])
        k_full = sb("k_full", [P, CHUNKS, TOKENS])
        qT = sb("qT", [P, 2, CHUNKS, TOKENS], F16)
        kT = sb("kT", [P, 2, CHUNKS, TOKENS], F16)
        stack_q = [sb(f"stack_q{j}", [3 * HEAD, HEADS, TOKENS], F16) for j in range(2)]
        stack_k = [sb(f"stack_k{j}", [3 * HEAD, HEADS, TOKENS], F16) for j in range(2)]
        v = [sb(f"v{j}", [P, 2, GROUP, HEADS, HEAD + 1], F16) for j in range(2)]
        score = [sb(f"score{j}", [P, HEADS, NODES]) for j in range(2)]
        prob = [sb(f"prob{j}", [P, HEADS, NODES]) for j in range(2)]
        row_max = sb("row_max", [P, 2, HEADS, 1])
        probT = sb("probT", [P, 2, HEADS, NODES], F16)
        inv_sum = sb("inv_sum", [P, HEADS, 1])
        mixed = [sb(f"mixed{j}", [P, HEADS, HEAD]) for j in range(2)]
        mixedT = sb("mixedT", [P, 2, CHUNKS, NODES], F16)
        out_copy = [sb(f"out_copy{j}", [P, FEATURES]) for j in range(2)]

        score_ps = ps("score_ps", [P, HEADS, NODES])
        probT_ps = ps("probT_ps", [P, HEADS, NODES])
        mix_ps = ps("mix_ps", [P, HEADS, HEAD + 1])
        out_ps = ps("out_ps", [P, FEATURES])
        front_ps = ps("front_ps", [P, CHUNKS, TOKENS])

        moments_ready = sem("att_moments_ready")
        rstd_step = sem("att_rstd_step")
        normed_ready = sem("att_normed_ready")
        turned = sem("att_turned")
        hT_hi = sem("att_hT_hi")
        hT_lo = sem("att_hT_lo")
        shift_step = sem("att_shift_step")
        q_full_ready = sem("att_q_full_ready")
        k_full_ready = sem("att_k_full_ready")
        q_ready = sem("att_q_ready")
        q_lo = sem("att_q_lo")
        k_ready = sem("att_k_ready")
        k_lo = sem("att_k_lo")
        v_ready = sem("att_v_ready")
        v_full_ready = sem("att_v_full_ready")
        v_lo = sem("att_v_lo")
        ones_ready = sem("att_ones_ready")
        q_stacked = [sem(f"att_q_stacked{j}") for j in range(2)]
        k_stacked = [sem(f"att_k_stacked{j}") for j in range(2)]
        scores_ready = sem("att_scores_ready")
        masked = sem("att_masked")
        max_ready = sem("att_max_ready")
        shifted = sem("att_shifted")
        prob_ready = sem("att_prob_ready")
        prob_turned = sem("att_prob_turned")
        probT_hi = sem("att_probT_hi")
        probT_lo = sem("att_probT_lo")
        mix_ready = sem("att_mix_ready")
        inv_ready = sem("att_inv_ready")
        mixed_ready = sem("att_mixed_ready")
        mixed_turned = sem("att_mixed_turned")
        mixedT_hi = sem("att_mixedT_hi")
        mixedT_lo = sem("att_mixedT_lo")
        out_ready = sem("att_out_ready")
        out_copied = sem("att_out_copied")
        x_ready = sem("att_x_ready")
        x_biased = sem("att_x_biased")
        block = ctx.enter_context(nc.Block())
        scale = 1.0 / float(HEAD) ** 0.5
        STACK_DMAS = 3 * (P // HEAD) * 16

        def half(j):
            return slice(4 * j, 4 * j + 4)

        def nodes(b):
            return slice(b * NODES, (b + 1) * NODES)

        def pipeline(eng, body):
            def pair(pairs, last=False):
                for j in range(2):
                    for b in range(GROUP):
                        ahead = 1 if b < 3 else 2
                        after = None if last else Group(pairs, j + 2)
                        body(None if last and j + ahead > 1 else (Group(pairs, j + ahead), b), Group(pairs, j), b,
                             after if b == 0 else None, (after, b - 1) if after and b in (1, 2) else None)
            first, second = Group(0, 0), Group(0, 1)
            body(None, None, None, first, None)
            body(None, None, None, None, (first, 0))
            body(None, None, None, None, (first, 1))
            body((first, 3), None, None, None, None)
            body((first, 0), None, None, second, None)
            body((first, 1), None, None, None, (second, 0))
            body((first, 2), None, None, None, (second, 1))
            body((second, 3), None, None, None, None)
            pair(0)
            with eng.Fori(1, GROUPS // 2 - 1) as pairs:
                pair(pairs)
            pair(GROUPS // 2 - 1, last=True)
            for b in range(GROUP):
                body(None, Group(GROUPS // 2, 0), b, None, None)

        def newest(now, b, back):
            if now is None:
                return None
            n = now.index * GROUP + (b - back)
            if isinstance(n, int) and not 0 <= n < GRAPHS:
                return None
            return n

        def there_is(n):
            return n is not None and (not isinstance(n, int) or n >= 0)

        @block.sync
        def _(sp):
            def stack(dst, src, part, places, ready):
                for i in places:
                    heads = dst[i * HEAD:(i + 1) * HEAD, :, :].rearrange("p (c q) t -> p q c t", c=CHUNKS)
                    for q in range(P // HEAD):
                        sp.dma_start(heads[:, q], src[q * HEAD:(q + 1) * HEAD, part, :, :]).then_inc(ready, 16)

            def body(front, now, b, stats, norm):
                if front is None:
                    return
                f, part = front
                if part == 0:
                    sp.wait_ge(q_full_ready, (f.index + 1) * CHUNKS)
                    if f.exists(2):
                        sp.wait_ge(scores_ready, (f.index - 1) * GROUP * 2)
                    stack(stack_q[f.parity], qT, HI, (0, 1), q_stacked[f.parity])
                    sp.wait_ge(q_lo, (f.index + 1) * CHUNKS)
                    stack(stack_q[f.parity], qT, LO, (2,), q_stacked[f.parity])
                if part == 1:
                    sp.wait_ge(k_full_ready, (f.index + 1) * CHUNKS)
                    stack(stack_k[f.parity], kT, HI, (0, 2), k_stacked[f.parity])
                    sp.wait_ge(k_lo, (f.index + 1) * CHUNKS)
                    stack(stack_k[f.parity], kT, LO, (1,), k_stacked[f.parity])

            pipeline(sp, body)

        @block.vector
        def _(dve):
            for j in range(2):
                dve.memset(v[j][:, HI, :, :, HEAD:], 1.0).then_inc(ones_ready, 1)
                dve.memset(v[j][:, LO, :, :, HEAD:], 0.0).then_inc(ones_ready, 1)

            def body(front, now, b, stats, norm):
                n, turning = newest(now, b, 0), newest(now, b, 2)

                def masked_scores(h):
                    if h == 0 and there_is(newest(now, b, 2)):
                        dve.wait_ge(prob_ready, (n - 1) * 2)
                    dve.wait_ge(scores_ready, n * 2 + (h + 1))
                    dve.scalar_tensor_tensor(score[b % 2][:, half(h), :], score_ps[:, half(h), :], scale,
                                             k.mask_bias[:].broadcast_to([P, 4, NODES]), ALU.mult,
                                             ALU.add).then_inc(masked, 1)

                def maximum(h):
                    dve.wait_ge(masked, n * 2 + (h + 1))
                    dve.reduce_max(row_max[:, b % 2, half(h), 0], score[b % 2][:, half(h), :],
                                   AX).then_inc(max_ready, 1)

                if turning is not None:
                    for h in range(2):
                        dve.wait_ge(probT_hi, turning * 2 + (h + 1))
                        dve.tensor_tensor(probT[:, LO, half(h), :], probT_ps[:, half(h), :], probT[:, HI, half(h), :],
                                          ALU.subtract).then_inc(probT_lo, 1)
                out = newest(now, b, 3)
                if out is not None:
                    dve.wait_ge(mixedT_hi, out + 1)
                    dve.tensor_tensor(mixedT[:, LO], out_ps[:].rearrange("p (c t) -> p c t", c=CHUNKS), mixedT[:, HI],
                                      ALU.subtract).then_inc(mixedT_lo, 1)
                if n is not None:
                    masked_scores(0)
                if front is not None and front[1] == 3:
                    for c in range(CHUNKS):
                        dve.wait_ge(hT_hi, front[0].index * CHUNKS + (c + 1))
                        dve.scalar_tensor_tensor(hT[:, LO, c, :], front_ps[:, c, :], 0.0, hT[:, HI, c, :], ALU.max,
                                                 ALU.subtract).then_inc(hT_lo, 1)
                if n is not None:
                    masked_scores(1)
                    maximum(0)
                    maximum(1)
                n = newest(now, b, 2)
                if n is not None:
                    dve.wait_ge(mix_ready, n + 1)
                    dve.wait_ge(mixed_ready, n)
                    dve.reciprocal(inv_sum[:], mix_ps[:, :, HEAD:]).then_inc(inv_ready, 1)
                    dve.wait_ge(inv_ready, n + 1)
                    if there_is(newest(now, b, 4)):
                        dve.wait_ge(mixed_turned, n - 1)
                    dve.tensor_tensor(mixed[b % 2][:], mix_ps[:, :, 0:HEAD],
                                      inv_sum[:].broadcast_to([P, HEADS, HEAD]), ALU.mult).then_inc(mixed_ready, 1)
                if stats is not None:
                    dve.wait_ge(shift_step, stats.index * 2)
                    layer_norm_stats(dve, k, stats.index, moments_ready, s)

            pipeline(dve, body)

        @block.gpsimd
        def _(pool):
            def body(front, now, b, stats, norm):
                n = newest(now, b, 4)
                if n is not None:
                    pool.wait_ge(x_biased, now.index * 2)
                    pool.wait_ge(out_copied, n + 1)
                    xn = k.x[:, bass.ds(n, 1), :].rearrange("p a f -> p (a f)")
                    pool.tensor_tensor(xn, xn, out_copy[b % 2][:], ALU.add).then_inc(x_ready, 1)
                for h in range(2):
                    n = newest(now, b, 0)
                    if n is not None:
                        pool.wait_ge(max_ready, n * 2 + (h + 1))
                        pool.tensor_tensor(score[b % 2][:, half(h), :], score[b % 2][:, half(h), :],
                                           row_max[:, b % 2, half(h), :].broadcast_to([P, 4, NODES]),
                                           ALU.subtract).then_inc(shifted, 1)
                    if front is None:
                        continue
                    f, part = front
                    g = f.index
                    if part in (0, 1):
                        full_ready, full, lo, dst = ((q_full_ready, q_full, q_lo, qT), (k_full_ready, k_full, k_lo, kT))[part]
                        pool.wait_ge(full_ready, g * CHUNKS + (h + 1))
                        pool.tensor_tensor(dst[:, LO, h, :], full[:, h, :], dst[:, HI, h, :],
                                           ALU.subtract).then_inc(lo, 1)
                    if part == 2:
                        pool.wait_ge(v_full_ready, g * 2 + (h + 1))
                        dst = v[f.parity][:, :, 2 * h:2 * h + 2, :, 0:HEAD]
                        src = q_full[:, h, :].rearrange("p (b h e) -> p b h e", b=2, h=HEADS)
                        for i in range(2):
                            pool.tensor_tensor(dst[:, LO, i], src[:, i], dst[:, HI, i], ALU.subtract).then_inc(v_lo, 1)
                    if part == 3:
                        if h == 0:
                            pool.wait_ge(normed_ready, (g + 1) * GROUP)
                            settle(pool, s)
                        xs = k.x[:, bass.ds(g * GROUP + 2 * h, 2), :]
                        pool.tensor_tensor(xs, xs, k.attn_bias[:].broadcast_to([P, 2, FEATURES]), ALU.add).then_inc(x_biased, 1)
                if stats is not None:
                    g = stats.index
                    pool.wait_ge(normed_ready, g * GROUP)
                    layer_norm_rstd(pool, k, g, moments_ready, rstd_step, s)
                    layer_norm_shift(pool, k, g, rstd_step, shift_step, neg_mean, s)

            pipeline(pool, body)

        @block.scalar
        def _(act):
            def normalise(g, graphs):
                for b in graphs:
                    act.activation(normed[:, b, :], k.x[:, graph(g, b), :].rearrange("p a f -> p (a f)"), ACT.Identity,
                                   scale=s.rstd[:, b:b + 1], bias=neg_mean[:, b:b + 1]).then_inc(normed_ready, 1)

            def body(front, now, b, stats, norm):
                n = newest(now, b, 4)
                if n is not None:
                    act.wait_ge(out_ready, n + 1)
                    if there_is(newest(now, b, 6)):
                        act.wait_ge(x_ready, n - 1)
                    act.copy(out_copy[b % 2][:], out_ps[:]).then_inc(out_copied, 1)
                n = newest(now, b, 2)
                if n is not None:
                    act.wait_ge(mix_ready, n)
                    for h in range(2):
                        act.wait_ge(prob_turned, n * 2 + (h + 1))
                        act.copy(probT[:, HI, half(h), :], probT_ps[:, half(h), :]).then_inc(probT_hi, 1)
                if front is not None:
                    f, part = front
                    g = f.index
                    if part == 0:
                        act.wait_ge(v_lo, g * 4)
                    if part == 2:
                        act.wait_ge(q_lo, (g + 1) * CHUNKS)
                        act.wait_ge(ones_ready, 4)
                        if f.exists(2):
                            act.wait_ge(mix_ready, (g - 1) * GROUP)
                    if part in (0, 1) and f.exists(1):
                        stacked = (q_stacked, k_stacked)[part]
                        act.wait_ge(stacked[f.before().parity], f.before().same * STACK_DMAS)
                    if part == 3:
                        act.wait_ge(v_ready, g * 2)
                for h in range(2):
                    n = newest(now, b, 1)
                    if n is not None:
                        act.wait_ge(shifted, n * 2 + (h + 1))
                        if there_is(newest(now, b, 3)):
                            act.wait_ge(prob_turned, (n - 1) * 2)
                        act.activation(prob[(b - 1) % 2][:, half(h), :], score[(b - 1) % 2][:, half(h), :],
                                       ACT.Exp).then_inc(prob_ready, 1)
                    n = newest(now, b, 3)
                    if n is not None and h == 0:
                        act.wait_ge(mixed_turned, n + 1)
                        act.wait_ge(out_ready, n)
                        act.copy(mixedT[:, HI], out_ps[:].rearrange("p (c t) -> p c t", c=CHUNKS)).then_inc(mixedT_hi, 1)
                    if front is None:
                        continue
                    if part in (0, 1):
                        ready, full_ready, full, dst, bias = ((q_ready, q_full_ready, q_full, qT, k.bias_q),
                                                              (k_ready, k_full_ready, k_full, kT, k.bias_k))[part]
                        act.wait_ge(ready, g * CHUNKS + (h + 1))
                        act.activation(dst[:, HI, h, :], front_ps[:, h, :], ACT.Identity, bias=bias[:, h:h + 1])
                        act.activation(full[:, h, :], front_ps[:, h, :], ACT.Identity,
                                       bias=bias[:, h:h + 1]).then_inc(full_ready, 1)
                    if part == 2:
                        act.wait_ge(v_ready, g * 2 + (h + 1))
                        dst = v[f.parity][:, HI, 2 * h:2 * h + 2, :, 0:HEAD]
                        act.copy(dst, front_ps[:, h, :].rearrange("p (b h e) -> p b h e", b=2, h=HEADS))
                        act.copy(q_full[:, h, :], front_ps[:, h, :]).then_inc(v_full_ready, 1)
                    if part == 3 and h == 0:
                        for c in range(CHUNKS):
                            act.wait_ge(turned, g * CHUNKS + (c + 1))
                            act.activation(hT[:, HI, c, :], front_ps[:, c, :], ACT.Relu).then_inc(hT_hi, 1)
                if norm is not None:
                    f, h = norm
                    act.wait_ge(turned, f.index * CHUNKS)
                    act.wait_ge(shift_step, (f.index + 1) * 2)
                    normalise(f.index, (2 * h, 2 * h + 1))

            pipeline(act, body)

        @block.tensor
        def _(pe):
            def front_half(f, part, h):
                g = f.index
                if part in (0, 1):
                    before, ready, slot = ((hT_lo, q_ready, SPLIT["q"]), (q_full_ready, k_ready, SPLIT["k"]))[part]
                    pe.wait_ge(before, (g + 1) * CHUNKS)
                    product(pe, front_ps[:, h, :], lambda a, i: k.w[:, a, slot + i, h * P:(h + 1) * P],
                            lambda m, i: hT[:, m, i, :]).then_inc(ready, 1)
                if part == 2:
                    pe.wait_ge(k_full_ready, (g + 1) * CHUNKS)
                    for b in (2 * h, 2 * h + 1):
                        last = product(pe, front_ps[:, h, (b % 2) * FEATURES:(b % 2 + 1) * FEATURES],
                                       lambda a, c: hT[:, a, c, nodes(b)], lambda m, c: k.w[:, m, SPLIT["v"] + c, :])
                    last.then_inc(v_ready, 1)
                if part == 3:
                    pe.wait_ge(normed_ready, (g + 1) * GROUP)
                    pe.wait_ge(v_full_ready, g * 2)
                    for b in range(GROUP):
                        last = pe.transpose(front_ps[:, h, nodes(b)], normed[:, b, h * P:(h + 1) * P], k.identity[:])
                    last.then_inc(turned, 1)

            def body(front, now, b, stats, norm):
                n = newest(now, b, 2)
                if n is not None:
                    for h in range(HEADS):
                        if h % 4 == 0:
                            pe.wait_ge(prob_ready, n * 2 + (h // 4 + 1))
                            if there_is(newest(now, b, 3)):
                                pe.wait_ge(probT_lo, (n - 1) * 2 + (h // 4 + 1))
                        last = pe.transpose(probT_ps[:, h, :], prob[b % 2][:, h, :], k.identity[:])
                        if h % 4 == 3:
                            last.then_inc(prob_turned, 1)
                if front is not None and front[1] < 3:
                    front_half(*front, 0)
                n = newest(now, b, 0)
                if n is not None:
                    if b == 0:
                        pe.wait_ge(q_stacked[now.parity], now.same * STACK_DMAS)
                        pe.wait_ge(k_stacked[now.parity], now.same * STACK_DMAS)
                    for h in range(HEADS):
                        if h % 4 == 0 and there_is(newest(now, b, 1)):
                            pe.wait_ge(masked, (n - 1) * 2 + (h // 4 + 1))
                        last = pe.matmul(score_ps[:, h, :], stack_q[now.parity][:, h, nodes(b)],
                                         stack_k[now.parity][:, h, nodes(b)], start=True, stop=True)
                        if h % 4 == 3:
                            last.then_inc(scores_ready, 1)
                n = newest(now, b, 3)
                if n is not None:
                    pe.wait_ge(mixed_ready, n + 1)
                    if there_is(newest(now, b, 4)):
                        pe.wait_ge(out_copied, n)
                    for c in range(CHUNKS):
                        last = pe.transpose(out_ps[:, c * P:(c + 1) * P],
                                            mixed[(b - 3) % 2][:, 4 * c:4 * c + 4, :].rearrange("p h e -> p (h e)"), k.identity[:])
                    last.then_inc(mixed_turned, 1)
                if front is not None:
                    if front[1] == 3:
                        front_half(*front, 0)
                    front_half(*front, 1)
                n = newest(now, b, 2)
                if n is not None:
                    if there_is(newest(now, b, 3)):
                        pe.wait_ge(mixed_ready, n)
                    pe.wait_ge(probT_lo, (n + 1) * 2)
                    source = now if b >= 2 else now.before()
                    pe.wait_ge(v_lo, (source.index + 1) * 4)
                    for h in range(HEADS):
                        last = product(pe, mix_ps[:, h, :], lambda a, c: probT[:, a, h, :],
                                       lambda m, c: v[source.parity][:, m, (b - 2) % GROUP, h, :], chunks=1)
                    last.then_inc(mix_ready, 1)
                n = newest(now, b, 3)
                if n is not None:
                    pe.wait_ge(mixedT_lo, n + 1)
                    product(pe, out_ps[:], lambda a, c: mixedT[:, a, c, :],
                            lambda m, c: k.w[:, m, SPLIT["o"] + c, :]).then_inc(out_ready, 1)

            pipeline(pe, body)


def gated_layer(nc, sem, dram, k):
    with ExitStack() as ctx:
        def sb(name, shape, dt=F32):
            return ctx.enter_context(nc.sbuf_tensor("gru_" + name, shape, dt))

        class Stream:
            def __init__(self, j):
                def sb_(name, shape, dt=F32):
                    return sb(f"{name}{j}", shape, dt)

                def sem_(name):
                    return sem(f"gru_{name}{j}")

                self.settled = sem_("settled")
                self.stats = sb_("stats", [P, GROUP, 6])
                self.moments = sb_("moments", [P, GROUP, 2])
                self.var_eps = sb_("var_eps", [P, GROUP])
                self.rstd = sb_("rstd", [P, GROUP])
                self.normed = sb_("normed", [P, GROUP, FEATURES])
                self.h = [sb_(f"h_{n}_", [P, CHUNKS, TOKENS]) for n in range(2)]
                self.hT = sb_("hT", [P, 2, CHUNKS, TOKENS], F16)
                self.h_rows = sb_("h_rows", [P, 2, GROUP, FEATURES], F16)
                self.aT = sb_("aT", [P, 2, CHUNKS, TOKENS], F16)
                self.r = sb_("r", [P, CHUNKS, TOKENS])
                self.rh = sb_("rh", [P, 2, CHUNKS, TOKENS], F16)
                self.z = sb_("z", [P, CHUNKS, TOKENS])
                self.kept = sb_("kept", [P, CHUNKS, TOKENS])
                self.new = sb_("new", [P, CHUNKS, TOKENS])
                self.mix_ps = ctx.enter_context(nc.psum_tensor(f"gru_mix_ps{j}", [P, CHUNKS, TOKENS], F32))
                self.gate_ps = ctx.enter_context(nc.psum_tensor(f"gru_gate_ps{j}", [P, CHUNKS, TOKENS], F32))
                self.moments_ready = sem_("moments_ready")
                self.rstd_step = sem_("rstd_step")
                self.normed_ready = sem_("normed_ready")
                self.normed_turned = sem_("normed_turned")
                self.first_copied = sem_("first_copied")
                self.h_hi = sem_("h_hi")
                self.h_lo = sem_("h_lo")
                self.h_turned = sem_("h_turned")
                self.rows_hi = sem_("rows_hi")
                self.rows_lo = sem_("rows_lo")
                self.a_ready = sem_("a_ready")
                self.a_hi = sem_("a_hi")
                self.a_lo = sem_("a_lo")
                self.r_sum = sem_("r_sum")
                self.r_ready = sem_("r_ready")
                self.rh_full = sem_("rh_full")
                self.rh_hi = sem_("rh_hi")
                self.rh_lo = sem_("rh_lo")
                self.z_sum = sem_("z_sum")
                self.z_ready = sem_("z_ready")
                self.kept_step = sem_("kept_step")
                self.new_sum = sem_("new_sum")
                self.new_ready = sem_("new_ready")
                self.scaled = sem_("scaled")
                self.h_ready = sem_("h_ready")
                self.x_ready = sem_("x_ready")

        streams = [Stream(j) for j in range(2)]
        block = ctx.enter_context(nc.Block())

        def nodes(b):
            return slice(b * NODES, (b + 1) * NODES)

        def half(c):
            return slice(c * P, (c + 1) * P)

        def bank(st, c):
            return st.mix_ps[:, c, :].rearrange("p (b f) -> p b f", b=GROUP)

        def pipeline(eng, body):
            body(0, True, False)
            with eng.Fori(1, GROUPS // 2 - 1) as pairs:
                body(pairs, False, False)
            body(GROUPS // 2 - 1, False, True)

        @block.vector
        def _(dve):
            def norm(st, j, pairs):
                g = pairs * 2 + j
                dve.wait_ge(st.rstd_step, pairs * 2)
                for b in range(GROUP):
                    dve.bn_stats(st.stats[:, b, :], k.x[:, graph(g, b), :].rearrange("p a f -> p (a f)")).then_inc(st.moments_ready, 1)
                dve.wait_ge(st.moments_ready, (pairs * 2 + 1) * GROUP)
                settle(dve, st)
                for b in range(GROUP):
                    dve.bn_aggr(st.moments[:, b, :], st.stats[:, b, :]).then_inc(st.moments_ready, 1)

            def norm_apply(st, j, pairs):
                g = pairs * 2 + j
                dve.wait_ge(st.rstd_step, (pairs + 1) * 2)
                dve.wait_ge(st.normed_turned, pairs * CHUNKS)
                for b in range(GROUP):
                    dve.tensor_scalar(st.normed[:, b, :], k.x[:, graph(g, b), :].rearrange("p a f -> p (a f)"),
                                      st.moments[:, b, 0:1], st.rstd[:, b:b + 1], ALU.subtract,
                                      ALU.mult).then_inc(st.normed_ready, 1)

            def start(st, pairs):
                q = pairs * STEPS
                for c in range(CHUNKS):
                    dve.wait_ge(st.h_hi, q * 2 + c + 1)
                    dve.scalar_tensor_tensor(st.hT[:, LO, c, :], st.gate_ps[:, c, :], 0.0, st.hT[:, HI, c, :],
                                             ALU.max, ALU.subtract).then_inc(st.h_lo, 1)
                for c in range(CHUNKS):
                    two = slice(2 * c, 2 * c + 2)
                    dve.wait_ge(st.rows_hi, q * 2 + c + 1)
                    dve.scalar_tensor_tensor(st.h_rows[:, LO, two], st.normed[:, two], 0.0, st.h_rows[:, HI, two],
                                             ALU.max, ALU.subtract).then_inc(st.rows_lo, 1)

            def finish(st, j, pairs):
                g = pairs * 2 + j
                for c in range(CHUNKS):
                    dve.wait_ge(st.h_turned, ((pairs + 1) * STEPS - 1) * 2 + c + 1)
                    xg = k.x[:, group(g), half(c)]
                    dve.tensor_tensor(xg, xg, bank(st, c), ALU.add).then_inc(st.x_ready, 1)

            def rows(st, q):
                for c in range(CHUNKS):
                    dve.wait_ge(st.rows_hi, q * 2 + c + 1)
                    dve.tensor_tensor(st.h_rows[:, LO, :, half(c)], bank(st, c), st.h_rows[:, HI, :, half(c)],
                                      ALU.subtract).then_inc(st.rows_lo, 1)

            def a_low(st, q):
                for c in range(CHUNKS):
                    dve.wait_ge(st.a_hi, q * 2 + c + 1)
                    dve.tensor_tensor(st.aT[:, LO, c, :], st.mix_ps[:, c, :], st.aT[:, HI, c, :],
                                      ALU.subtract).then_inc(st.a_lo, 1)

            def reset(st, q, h):
                for c in range(CHUNKS):
                    dve.wait_ge(st.r_ready, q * 2 + c + 1)
                    dve.tensor_tensor(st.r[:, c, :], st.r[:, c, :], h[:, c, :], ALU.mult).then_inc(st.rh_full, 1)
                for c in range(CHUNKS):
                    dve.wait_ge(st.rh_hi, q * 2 + c + 1)
                    dve.tensor_tensor(st.rh[:, LO, c, :], st.r[:, c, :], st.rh[:, HI, c, :],
                                      ALU.subtract).then_inc(st.rh_lo, 1)

            def update(st, q, after):
                for c in range(CHUNKS):
                    dve.wait_ge(st.new_ready, q * 2 + c + 1)
                    dve.wait_ge(st.z_ready, q * 2 + c + 1)
                    dve.tensor_tensor(st.new[:, c, :], st.new[:, c, :], st.z[:, c, :], ALU.mult).then_inc(st.scaled, 1)
                for c in range(CHUNKS):
                    dve.wait_ge(st.scaled, q * 2 + c + 1)
                    dve.wait_ge(st.kept_step, q * 4 + 2 * c + 2)
                    dve.tensor_tensor(after[:, c, :], st.kept[:, c, :], st.new[:, c, :], ALU.add).then_inc(st.h_ready, 1)

            def h_low(st, q, h):
                for c in range(CHUNKS):
                    dve.wait_ge(st.h_hi, q * 2 + c + 1)
                    dve.tensor_tensor(st.hT[:, LO, c, :], h[:, c, :], st.hT[:, HI, c, :], ALU.subtract).then_inc(st.h_lo, 1)

            for j, st in enumerate(streams):
                norm(st, j, 0)
                norm_apply(st, j, 0)
            for st in streams:
                start(st, 0)

            def body(pairs, first, last):
                for t in range(STEPS):
                    q = pairs * STEPS + t
                    before, after = t % 2, (t + 1) % 2
                    for j, st in enumerate(streams):
                        if t > 0 and j == 1:
                            rows(st, q)
                        elif t == 0 and not first:
                            finish(st, j, pairs - 1)
                            if j == 0:
                                start(streams[1], pairs)
                        a_low(st, q)
                    for j, st in enumerate(streams):
                        reset(st, q, st.h[before])
                        if t == STEPS - 1 and j == 1 and not last:
                            start(streams[0], pairs + 1)
                        if t == 0 and not last:
                            norm(st, j, pairs + 1)
                        update(st, q, st.h[after])
                        if t < STEPS - 1 and j == 1:
                            rows(streams[0], q + 1)
                        if t < STEPS - 1:
                            h_low(st, q + 1, st.h[after])
                        if t == 1 and not last:
                            norm_apply(st, j, pairs + 1)

            pipeline(dve, body)
            for j, st in enumerate(streams):
                finish(st, j, GROUPS // 2 - 1)

        @block.gpsimd
        def _(pool):
            for st in streams:
                layer_norm_rstd(pool, k, 0, st.moments_ready, st.rstd_step, st)

            def keep(st, q, h):
                for c in range(CHUNKS):
                    pool.wait_ge(st.z_ready, q * 2 + c + 1)
                    pool.wait_ge(st.h_ready, q * 2)
                    pool.tensor_tensor(st.kept[:, c, :], st.z[:, c, :], h[:, c, :], ALU.mult).then_inc(st.kept_step, 1)
                    pool.wait_ge(st.kept_step, q * 4 + 2 * c + 1)
                    pool.tensor_tensor(st.kept[:, c, :], h[:, c, :], st.kept[:, c, :], ALU.subtract).then_inc(st.kept_step, 1)

            def body(pairs, first, last):
                for t in range(STEPS):
                    for st in streams:
                        keep(st, pairs * STEPS + t, st.h[t % 2])
                        if t == 0 and not last:
                            layer_norm_rstd(pool, k, pairs + 1, st.moments_ready, st.rstd_step, st)

            pipeline(pool, body)

        @block.scalar
        def _(act):
            def start(st, pairs):
                q = pairs * STEPS
                act.wait_ge(st.kept_step, q * 4)
                for c in range(CHUNKS):
                    act.wait_ge(st.normed_turned, pairs * CHUNKS + c + 1)
                    act.activation(st.h[0][:, c, :], st.gate_ps[:, c, :], ACT.Relu).then_inc(st.first_copied, 1)
                    act.activation(st.hT[:, HI, c, :], st.gate_ps[:, c, :], ACT.Relu).then_inc(st.h_hi, 1)
                for c in range(CHUNKS):
                    act.activation(st.h_rows[:, HI, 2 * c:2 * c + 2], st.normed[:, 2 * c:2 * c + 2],
                                   ACT.Relu).then_inc(st.rows_hi, 1)

            def rows(st, q):
                for c in range(CHUNKS):
                    act.wait_ge(st.h_turned, q * 2 - 2 + c + 1)
                    act.copy(st.h_rows[:, HI, :, half(c)], bank(st, c)).then_inc(st.rows_hi, 1)

            def a_high(st, q):
                for c in range(CHUNKS):
                    act.wait_ge(st.a_ready, q * 2 + c + 1)
                    act.copy(st.aT[:, HI, c, :], st.mix_ps[:, c, :]).then_inc(st.a_hi, 1)

            def gates(st, q):
                def reset(c):
                    act.wait_ge(st.r_sum, q * 2 + c + 1)
                    act.activation(st.r[:, c, :], st.gate_ps[:, c, :], ACT.Sigmoid,
                                   bias=k.bias_r[:, c:c + 1]).then_inc(st.r_ready, 1)

                def reset_high(c):
                    act.wait_ge(st.rh_full, q * 2 + c + 1)
                    act.copy(st.rh[:, HI, c, :], st.r[:, c, :]).then_inc(st.rh_hi, 1)

                def update(c):
                    act.wait_ge(st.z_sum, q * 2 + c + 1)
                    act.activation(st.z[:, c, :], st.gate_ps[:, c, :], ACT.Sigmoid,
                                   bias=k.bias_z[:, c:c + 1]).then_inc(st.z_ready, 1)

                reset(0)
                reset(1)
                reset_high(0)
                update(0)
                reset_high(1)
                update(1)

            def candidate(st, q):
                for c in range(CHUNKS):
                    act.wait_ge(st.new_sum, q * 2 + c + 1)
                    act.activation(st.new[:, c, :], st.mix_ps[:, c, :], ACT.Tanh,
                                   bias=k.bias_h[:, c:c + 1]).then_inc(st.new_ready, 1)

            def h_high(st, q, h):
                for c in range(CHUNKS):
                    act.wait_ge(st.h_ready, q * 2 + c + 1)
                    act.copy(st.hT[:, HI, c, :], h[:, c, :]).then_inc(st.h_hi, 1)

            for st in streams:
                start(st, 0)

            def body(pairs, first, last):
                for t in range(STEPS):
                    q = pairs * STEPS + t
                    for j, st in enumerate(streams):
                        if t > 0 and j == 1:
                            rows(st, q)
                        a_high(st, q)
                    for j, st in enumerate(streams):
                        gates(st, q)
                        if t == STEPS - 1 and j == 1 and not last:
                            start(streams[0], pairs + 1)
                        candidate(st, q)
                        if t < STEPS - 1:
                            if j == 1:
                                rows(streams[0], q + 1)
                            h_high(st, q, st.h[(t + 1) % 2])
                        elif j == 1 and not last:
                            start(st, pairs + 1)

            pipeline(act, body)

        @block.tensor
        def _(pe):
            def weight(name, a, i, c):
                return k.w[:, a, SPLIT[name] + i, half(c)]

            def start(st, pairs):
                pe.wait_ge(st.normed_ready, (pairs + 1) * GROUP)
                pe.wait_ge(st.z_ready, pairs * STEPS * 2)
                for c in range(CHUNKS):
                    for b in range(GROUP):
                        last = pe.transpose(st.gate_ps[:, c, nodes(b)], st.normed[:, b, half(c)], k.identity[:])
                    last.then_inc(st.normed_turned, 1)

            def turn(st, q, h):
                for c in range(CHUNKS):
                    pe.wait_ge(st.h_ready, q * 2 - 2 + c + 1)
                    for b in range(GROUP):
                        last = pe.transpose(st.mix_ps[:, c, nodes(b)], h[:, c, nodes(b)], k.identity[:])
                    last.then_inc(st.h_turned, 1)

            def gate_from_h(st, pairs, q):
                pe.wait_ge(st.h_lo, q * 2 + 2)
                pe.wait_ge(st.first_copied, (pairs + 1) * CHUNKS)
                pe.wait_ge(st.z_ready, q * 2)
                for c in range(CHUNKS):
                    product(pe, st.gate_ps[:, c, :], lambda a, i: weight("u3", a, i, c),
                            lambda m, i: st.hT[:, m, i, :], stop=False, loose=True)

            def neighbours(st, pairs, t):
                pe.wait_ge(st.rows_lo, (pairs * STEPS + t) * 2 + 2)
                if t == 0:
                    pe.wait_ge(st.x_ready, pairs * CHUNKS)
                for c in range(CHUNKS):
                    for b in range(GROUP):
                        last = product(pe, st.mix_ps[:, c, nodes(b)], lambda a, i: st.h_rows[:, a, b, half(c)],
                                       lambda m, i: k.adjT[:, m, :], chunks=1)
                    last.then_inc(st.a_ready, 1)

            def gates_from_a(st, q):
                pe.wait_ge(st.a_lo, q * 2 + 2)
                for c in range(CHUNKS):
                    product(pe, st.gate_ps[:, c, :], lambda a, i: weight("w4", a, i, c),
                            lambda m, i: st.aT[:, m, i, :], start=False, loose=True).then_inc(st.r_sum, 1)
                for c in range(CHUNKS):
                    pe.wait_ge(st.r_ready, q * 2 + c + 1)
                    product(pe, st.gate_ps[:, c, :], lambda a, i: weight("w3", a, i, c),
                            lambda m, i: st.aT[:, m, i, :], start=False, loose=True).then_inc(st.z_sum, 1)
                for c in range(CHUNKS):
                    product(pe, st.mix_ps[:, c, :], lambda a, i: weight("w5", a, i, c),
                            lambda m, i: st.aT[:, m, i, :], stop=False, loose=True)

            def candidate(st, q):
                pe.wait_ge(st.rh_lo, q * 2 + 2)
                for c in range(CHUNKS):
                    product(pe, st.mix_ps[:, c, :], lambda a, i: weight("u5", a, i, c),
                            lambda m, i: st.rh[:, m, i, :], start=False, loose=True).then_inc(st.new_sum, 1)

            for st in streams:
                start(st, 0)

            def body(pairs, first, last):
                for t in range(STEPS):
                    q = pairs * STEPS + t
                    for st in streams:
                        if t > 0 or not first:
                            turn(st, q, st.h[t % 2 if t else STEPS % 2])
                        gate_from_h(st, pairs, q)
                        neighbours(st, pairs, t)
                    for st in streams:
                        gates_from_a(st, q)
                        candidate(st, q)
                        if t == STEPS - 1 and not last:
                            start(st, pairs + 1)

            pipeline(pe, body)
            for st in streams:
                turn(st, GROUPS // 2 * STEPS, st.h[STEPS % 2])


def conv_layer(nc, sem, dram, k):
    with ExitStack() as ctx:
        def sb(name, shape, dt=F32):
            return ctx.enter_context(nc.sbuf_tensor("conv_" + name, shape, dt))

        def ps(name, shape):
            return ctx.enter_context(nc.psum_tensor("conv_" + name, shape, F32))

        class s:
            settled = sem("conv_settled")
            stats = sb("stats", [P, GROUP, 6])
            moments = sb("moments", [P, GROUP, 2])
            var_eps = sb("var_eps", [P, GROUP])
            rstd = sb("rstd", [P, GROUP])
        neg_mean = sb("neg_mean", [P, GROUP])
        h_full = sb("h_full", [P, GROUP, FEATURES])
        h_rows = [sb(f"h_rows{j}", [P, 2, GROUP, FEATURES], F16) for j in range(2)]
        aT = [sb(f"aT{j}", [P, 2, CHUNKS, TOKENS], F16) for j in range(2)]
        a_ps = ps("a_ps", [P, CHUNKS, TOKENS])
        y_ps = ps("y_ps", [P, GROUP, FEATURES])

        moments_ready = sem("conv_moments_ready")
        rstd_step = sem("conv_rstd_step")
        shift_step = sem("conv_shift_step")
        full_ready = sem("conv_full_ready")
        rows_hi = sem("conv_rows_hi")
        rows_lo = sem("conv_rows_lo")
        x_biased = sem("conv_x_biased")
        a_ready = sem("conv_a_ready")
        a_hi = sem("conv_a_hi")
        a_lo = sem("conv_a_lo")
        y_ready = sem("conv_y_ready")
        x_ready = sem("conv_x_ready")
        stored = sem("conv_stored")
        block = ctx.enter_context(nc.Block())

        def pipeline(eng, body):
            def step(i, j):
                body(i, i - 1, i - 2, i - 3, j)
            body(0, None, None, None, 0)
            body(1, 0, None, None, 1)
            body(2, 1, 0, None, 0)
            step(3, 1)
            with eng.Fori(2, GROUPS // 2) as pairs:
                step(pairs * 2, 0)
                step(pairs * 2 + 1, 1)
            body(None, GROUPS - 1, GROUPS - 2, GROUPS - 3, 0)
            body(None, None, GROUPS - 1, GROUPS - 2, 1)
            body(None, None, None, GROUPS - 1, 0)

        def nodes(b):
            return slice(b * NODES, (b + 1) * NODES)

        @block.sync
        def _(sp):
            view = dram["out"].rearrange("b n d -> n b d")

            def body(ahead, front, mid, back, j):
                if back is not None:
                    sp.wait_ge(x_ready, (back + 1) * 2)
                    settle(sp, s)
                    if not isinstance(back, int) or back > 0:
                        sp.wait_ge(stored, back * 16)
                    settle(sp, s)
                    sp.dma_start(view[:, group(back), :], k.x[:, group(back), :]).then_inc(stored, 16)

            pipeline(sp, body)
            sp.wait_ge(stored, GROUPS * 16)

        @block.vector
        def _(dve):
            def body(ahead, front, mid, back, j):
                if ahead is not None:
                    dve.wait_ge(shift_step, ahead * 2)
                    layer_norm_stats(dve, k, ahead, moments_ready, s)
                if mid is not None:
                    for c in range(CHUNKS):
                        dve.wait_ge(a_hi, mid * CHUNKS + (c + 1))
                        dve.tensor_tensor(aT[j][:, LO, c, :], a_ps[:, c, :], aT[j][:, HI, c, :], ALU.subtract).then_inc(a_lo, 1)
                if front is not None:
                    dve.wait_ge(rows_hi, front + 1)
                    dve.tensor_tensor(h_rows[1 - j][:, LO], h_full[:], h_rows[1 - j][:, HI],
                                      ALU.subtract).then_inc(rows_lo, 1)
                if back is not None:
                    dve.wait_ge(x_biased, back + 1)
                    for i in range(2):
                        dve.wait_ge(y_ready, back * 2 + (i + 1))
                        xh = k.x[:, bass.ds(back * GROUP + 2 * i, 2), :]
                        dve.tensor_tensor(xh, xh, y_ps[:, 2 * i:2 * i + 2, :], ALU.add).then_inc(x_ready, 1)

            pipeline(dve, body)

        @block.gpsimd
        def _(pool):
            def body(ahead, front, mid, back, j):
                if ahead is not None:
                    pool.wait_ge(full_ready, ahead * GROUP)
                    layer_norm_rstd(pool, k, ahead, moments_ready, rstd_step, s)
                    layer_norm_shift(pool, k, ahead, rstd_step, shift_step, neg_mean, s)
                if front is not None:
                    pool.wait_ge(full_ready, (front + 1) * GROUP)
                    settle(pool, s)
                    pool.tensor_tensor(k.x[:, group(front), :], k.x[:, group(front), :],
                                       k.conv_bias[:].broadcast_to([P, GROUP, FEATURES]), ALU.add).then_inc(x_biased, 1)

            pipeline(pool, body)

        @block.scalar
        def _(act):
            def body(ahead, front, mid, back, j):
                if front is not None:
                    act.wait_ge(shift_step, (front + 1) * 2)
                    act.wait_ge(rows_lo, front)
                    for b in range(GROUP):
                        act.activation(h_full[:, b, :], k.x[:, graph(front, b), :].rearrange("p a f -> p (a f)"),
                                       ACT.Relu, scale=s.rstd[:, b:b + 1],
                                       bias=neg_mean[:, b:b + 1]).then_inc(full_ready, 1)
                if mid is not None:
                    if not isinstance(mid, int) or mid >= 2:
                        act.wait_ge(y_ready, (mid - 1) * 2)
                    for c in range(CHUNKS):
                        act.wait_ge(a_ready, mid * CHUNKS + (c + 1))
                        act.copy(aT[j][:, HI, c, :], a_ps[:, c, :]).then_inc(a_hi, 1)
                if front is not None:
                    act.wait_ge(full_ready, (front + 1) * GROUP)
                    if not isinstance(front, int) or front >= 2:
                        act.wait_ge(a_ready, (front - 1) * CHUNKS)
                    act.copy(h_rows[1 - j][:, HI], h_full[:]).then_inc(rows_hi, 1)

            pipeline(act, body)

        @block.tensor
        def _(pe):
            def body(ahead, front, mid, back, j):
                if mid is not None:
                    pe.wait_ge(rows_lo, mid + 1)
                    pe.wait_ge(a_lo, mid * CHUNKS)
                    for c in range(CHUNKS):
                        for b in range(GROUP):
                            last = product(pe, a_ps[:, c, nodes(b)], lambda a, i: h_rows[j][:, a, b, c * P:(c + 1) * P],
                                           lambda m, i: k.adjT[:, m, :], chunks=1)
                        last.then_inc(a_ready, 1)
                if back is not None:
                    pe.wait_ge(a_lo, (back + 1) * CHUNKS)
                    pe.wait_ge(x_ready, back * 2)
                    for b in range(GROUP):
                        last = product(pe, y_ps[:, b, :], lambda a, c: aT[1 - j][:, a, c, nodes(b)],
                                       lambda m, c: k.w[:, m, SPLIT["conv"] + c, :])
                        if b % 2:
                            last.then_inc(y_ready, 1)

            pipeline(pe, body)


def build(nc, dram, out):
    dram = dict(dram, out=out)
    with ExitStack() as ctx:
        def sb(name, shape, dt=F32):
            return ctx.enter_context(nc.sbuf_tensor(name, shape, dt))

        def sem(name):
            return ctx.enter_context(nc.semaphore(name))

        class k:
            x = sb("x_res", [P, GRAPHS, FEATURES])
            x_in = sem("x_in")
            w = sb("w_split", [P, 2, SPLIT_SLOTS, FEATURES], F16)
            identity = sb("identity", [P, P])
            adjT = sb("adjT", [P, 2, NODES], F16)
            mask = sb("mask", [P, 1, NODES])
            mask_bias = sb("mask_bias", [P, 1, NODES])
            attn_vecs = sb("attn_vecs", [P, 2, 2, CHUNKS, P], F16)
            bias_q = sb("bias_q", [P, CHUNKS])
            bias_k = sb("bias_k", [P, CHUNKS])
            bias_z = sb("bias_z", [P, CHUNKS])
            bias_r = sb("bias_r", [P, CHUNKS])
            bias_h = sb("bias_h", [P, CHUNKS])
            attn_bias = sb("attn_bias", [P, 1, FEATURES])
            conv_bias = sb("conv_bias", [P, 1, FEATURES])
            beta = sb("beta", [P, 1])
            eps = sb("eps", [P, GROUP])
            minus_half = sb("minus_half", [P, GROUP])
            minus_one = sb("minus_one", [P, GROUP])

        load_constants(nc, sem, dram, k)
        for layer in (gat_layer, attention_layer, gated_layer, conv_layer):
            layer(nc, sem, dram, k)


def kernel(**inputs):
    import numpy as np
    import concourse.bacc as bacc
    from concourse.bass_utils import run_bass_kernel_spmd

    f32 = {name: np.asarray(a, dtype=np.float32) for name, a in inputs.items()}

    def tile_rows(v):
        return np.broadcast_to(v.reshape(1, -1), (P, v.size))

    def column(v):
        return v.reshape(CHUNKS, P).T

    a = f32["L0_gnn_a"].reshape(2, FEATURES)
    arrays = {
        "x": f32["x"],
        "weights": np.concatenate([
            f32["L0_gnn_W"], f32["L1_gnn_Wq"], f32["L1_gnn_Wk"], f32["L1_gnn_Wv"], f32["L1_gnn_Wo"],
            f32["L2_gnn_w3_w"].T, f32["L2_gnn_w4_w"].T, f32["L2_gnn_w5_w"].T, f32["L2_gnn_u3_w"].T,
            f32["L2_gnn_u5_w"].T, f32["L3_gnn_weight"]], axis=0),
        "cols": np.concatenate([column(v) for v in (
            f32["L1_gnn_bq"], f32["L1_gnn_bk"], f32["L1_gnn_bv"], f32["L2_gnn_w3_b"],
            f32["L2_gnn_u3_b"], f32["L2_gnn_w4_b"], f32["L2_gnn_w5_b"], f32["L2_gnn_u5_b"])], axis=1),
        "rows": np.stack([tile_rows(v) for v in (a[0], a[1], f32["L1_gnn_bo"], f32["L3_gnn_bias"])], axis=1),
        "adj": np.stack([f32["adj"], f32["adj"].T], axis=1),
        "identity": np.eye(P, dtype=np.float32),
        "beta": np.broadcast_to(f32["L0_gnn_beta"].reshape(1, 1), (P, 1)),
    }
    arrays = {name: np.ascontiguousarray(v) for name, v in arrays.items()}

    nc = bacc.Bacc("TRN2", target_bir_lowering=False, num_devices=1)
    dram = {name: nc.dram_tensor("in_" + name, v.shape, F32, kind="ExternalInput").ap() for name, v in arrays.items()}
    out = nc.dram_tensor("out_0", (GRAPHS, NODES, FEATURES), F32, kind="ExternalOutput").ap()
    build(nc, dram, out)
    result = run_bass_kernel_spmd(nc, [{"in_" + name: v for name, v in arrays.items()}], core_ids=[0])
    return result.results[0]["out_0"]
```
